# Optimizing a Trainium2 kernel written in Bass

```python
import numpy as np
import jax
import jax.numpy as jnp

def _softmax(x, axis=-1):
    return jax.nn.softmax(x, axis=axis)

def _gelu(x):
    return jax.nn.gelu(x, approximate=True)

def _silu(x):
    return jax.nn.silu(x)

def _sigmoid(x):
    return jax.nn.sigmoid(x)

def _layernorm(x, axis=-1, eps=1e-05):
    m = jnp.mean(x, axis=axis, keepdims=True)
    v = jnp.var(x, axis=axis, keepdims=True)
    return (x - m) / jnp.sqrt(v + eps)

def _scatter_add(tgt, idx, src, axis=0):
    return tgt.at[idx].add(src)

def _segment_sum(src, seg, n):
    return jax.ops.segment_sum(src, seg, n)
kernel_name = 'mk_gnn_resnorm_d4_gnn_r8_c6932c'

def setup_inputs(seed: int=0):
    np.random.seed(seed)
    _w = jnp.asarray

    def _rec_inputs():
        import jax
        import jax.numpy as jnp
        _gk = jax.random.key(seed)
        x = -0.000202 + 1 * jax.random.normal(jax.random.fold_in(_gk, 1), (6250, 128), jnp.float32)
        _s = jax.random.randint(jax.random.fold_in(_gk, 2), (50000,), 0, 6250, jnp.int32)
        _d = jax.random.randint(jax.random.fold_in(_gk, 3), (50000,), 0, 6250, jnp.int32)
        _loop = jnp.arange(6250, dtype=jnp.int32)
        src = jnp.concatenate([_s, _d, _loop])
        dst = jnp.concatenate([_d, _s, _loop])
        _o = jnp.argsort(dst, stable=True)
        src = src[_o]
        dst = dst[_o]
        edge_attr_128 = -8.513e-05 + 0.999844 * jax.random.normal(jax.random.fold_in(_gk, 12), (106250, 128), jnp.float32)
        edge_weight = jax.random.uniform(jax.random.fold_in(_gk, 14), (106250,), jnp.float32, 0.0, 0.999999)
        return (x, src, dst, edge_attr_128, edge_weight)
    x, src, dst, edge_attr_128, edge_weight = _rec_inputs()

    def _L0_gnn_setup():
        import jax, jax.numpy as jnp
        import numpy as np
        N_NODES = 6250
        N_EDGES = 100000
        D_IN = 128
        D_OUT = 128
        key = jax.random.key(seed)
        ks = jax.random.split(key, 6)
        x = jax.random.normal(ks[0], (N_NODES, D_IN), dtype=jnp.float32)
        edge_src = jax.random.randint(ks[1], (N_EDGES,), 0, N_NODES)
        edge_dst = jax.random.randint(ks[2], (N_EDGES,), 0, N_NODES)
        edge_val = jax.random.uniform(ks[3], (N_EDGES,), dtype=jnp.float32)
        W = jax.random.normal(ks[4], (D_OUT, D_IN), dtype=jnp.float32) / np.sqrt(D_IN)
        b = jax.random.normal(ks[5], (D_OUT,), dtype=jnp.float32) * 0.01
        return {'x': x, 'edge_src': edge_src, 'edge_dst': edge_dst, 'edge_val': edge_val, 'W': W, 'b': b}
    _L0_gnn_all = _L0_gnn_setup()
    _L0_gnn_in = {k: v for k, v in _L0_gnn_all.items() if k in ('W', 'b')}
    del _L0_gnn_all

    def _L1_gnn_setup():
        import jax, jax.numpy as jnp
        import numpy as np
        N = 12500
        E = 200000
        D_IN = 128
        D_HID = 128

        def gcn_conv(x, src, dst, norm, W, b, n_nodes):
            h = x @ W
            msg = h[src] * norm[:, None]
            out = jax.ops.segment_sum(msg, dst, num_segments=n_nodes)
            return out + b

        def _prep_edges(edge_index, n_nodes):
            loops = jnp.arange(n_nodes, dtype=edge_index.dtype)
            src = jnp.concatenate([edge_index[0], loops])
            dst = jnp.concatenate([edge_index[1], loops])
            deg = jax.ops.segment_sum(jnp.ones_like(dst, dtype=jnp.float32), dst, num_segments=n_nodes)
            dinv = jnp.where(deg > 0, jax.lax.rsqrt(deg), 0.0)
            norm = dinv[src] * dinv[dst]
            return (src, dst, norm)
        key = jax.random.key(seed)
        k1, k2, k3, k4 = jax.random.split(key, 4)
        x = jax.random.normal(k1, (N, D_IN), dtype=jnp.float32)
        edge_index = jax.random.randint(k2, (2, E), 0, N, dtype=jnp.int64)
        s1 = 1.0 / np.sqrt(D_IN)
        s2 = 1.0 / np.sqrt(D_HID)
        W1 = jax.random.uniform(k3, (D_IN, D_HID), jnp.float32, -s1, s1)
        W2 = jax.random.uniform(k4, (D_HID, D_HID), jnp.float32, -s2, s2)
        b1 = jnp.zeros((D_HID,), jnp.float32)
        b2 = jnp.zeros((D_HID,), jnp.float32)
        return {'x': x, 'edge_index': edge_index, 'W1': W1, 'b1': b1, 'W2': W2, 'b2': b2}
    _L1_gnn_all = _L1_gnn_setup()
    _L1_gnn_in = {k: v for k, v in _L1_gnn_all.items() if k in ('W1', 'b1', 'W2', 'b2')}
    del _L1_gnn_all

    def _L2_gnn_setup():
        import jax, jax.numpy as jnp
        import numpy as np
        N_NODES = 2500
        N_EDGES = 80000
        D = 128
        EPS = 1e-05

        def _layernorm(x, g, b):
            mu = jnp.mean(x, axis=-1, keepdims=True)
            var = jnp.var(x, axis=-1, keepdims=True)
            return (x - mu) * jax.lax.rsqrt(var + EPS) * g + b
        key = jax.random.key(seed)
        ks = jax.random.split(key, 16)
        s = lambda fan_in: 1.0 / np.sqrt(fan_in)
        inp = {'h_V': jax.random.normal(ks[0], (N_NODES, D), jnp.float32), 'h_E': jax.random.normal(ks[1], (N_EDGES, D), jnp.float32), 'edge_idx': jax.random.randint(ks[2], (2, N_EDGES), 0, N_NODES, jnp.int64), 'W1': jax.random.uniform(ks[3], (3 * D, D), jnp.float32, -s(3 * D), s(3 * D)), 'b1': jnp.zeros((D,), jnp.float32), 'W2': jax.random.uniform(ks[4], (D, D), jnp.float32, -s(D), s(D)), 'b2': jnp.zeros((D,), jnp.float32), 'W3': jax.random.uniform(ks[5], (D, D), jnp.float32, -s(D), s(D)), 'b3': jnp.zeros((D,), jnp.float32), 'Wd1': jax.random.uniform(ks[6], (D, 4 * D), jnp.float32, -s(D), s(D)), 'bd1': jnp.zeros((4 * D,), jnp.float32), 'Wd2': jax.random.uniform(ks[7], (4 * D, D), jnp.float32, -s(4 * D), s(4 * D)), 'bd2': jnp.zeros((D,), jnp.float32), 'g1': jnp.ones((D,), jnp.float32), 'beta1': jnp.zeros((D,), jnp.float32), 'g2': jnp.ones((D,), jnp.float32), 'beta2': jnp.zeros((D,), jnp.float32)}
        return inp
    _L2_gnn_all = _L2_gnn_setup()
    _L2_gnn_in = {k: v for k, v in _L2_gnn_all.items() if k in ('W1', 'b1', 'W2', 'b2', 'W3', 'b3', 'Wd1', 'bd1', 'Wd2', 'bd2', 'g1', 'beta1', 'g2', 'beta2')}
    del _L2_gnn_all

    def _L3_gnn_setup():
        import jax, jax.numpy as jnp
        import numpy as np
        N = 6250
        D = 128
        E = 100000
        key = jax.random.key(seed)
        k1, k2, k3, k4 = jax.random.split(key, 4)
        x = jax.random.normal(k1, (N, D), dtype=jnp.float32)
        W = jax.random.normal(k2, (2 * D, D), dtype=jnp.float32) * (1.0 / np.sqrt(D))
        edge_src = jax.random.randint(k3, (E,), 0, N, dtype=jnp.int32)
        edge_dst = jax.random.randint(k4, (E,), 0, N, dtype=jnp.int32)
        edge_val = jnp.ones((E,), dtype=jnp.float32)
        return {'x': x, 'W': W, 'edge_src': edge_src, 'edge_dst': edge_dst, 'edge_val': edge_val}
    _L3_gnn_all = _L3_gnn_setup()
    _L3_gnn_in = {k: v for k, v in _L3_gnn_all.items() if k in ('W',)}
    del _L3_gnn_all
    return {'x': x, 'src': src, 'dst': dst, 'edge_attr_128': edge_attr_128, 'edge_weight': edge_weight, 'L0_gnn_W': _L0_gnn_in['W'], 'L0_gnn_b': _L0_gnn_in['b'], 'L1_gnn_W1': _L1_gnn_in['W1'], 'L1_gnn_b1': _L1_gnn_in['b1'], 'L1_gnn_W2': _L1_gnn_in['W2'], 'L1_gnn_b2': _L1_gnn_in['b2'], 'L2_gnn_W1': _L2_gnn_in['W1'], 'L2_gnn_b1': _L2_gnn_in['b1'], 'L2_gnn_W2': _L2_gnn_in['W2'], 'L2_gnn_b2': _L2_gnn_in['b2'], 'L2_gnn_W3': _L2_gnn_in['W3'], 'L2_gnn_b3': _L2_gnn_in['b3'], 'L2_gnn_Wd1': _L2_gnn_in['Wd1'], 'L2_gnn_bd1': _L2_gnn_in['bd1'], 'L2_gnn_Wd2': _L2_gnn_in['Wd2'], 'L2_gnn_bd2': _L2_gnn_in['bd2'], 'L2_gnn_g1': _L2_gnn_in['g1'], 'L2_gnn_beta1': _L2_gnn_in['beta1'], 'L2_gnn_g2': _L2_gnn_in['g2'], 'L2_gnn_beta2': _L2_gnn_in['beta2'], 'L3_gnn_W': _L3_gnn_in['W']}

def reference(x, src, dst, edge_attr_128, edge_weight, L0_gnn_W, L0_gnn_b, L1_gnn_W1, L1_gnn_b1, L1_gnn_W2, L1_gnn_b2, L2_gnn_W1, L2_gnn_b1, L2_gnn_W2, L2_gnn_b2, L2_gnn_W3, L2_gnn_b3, L2_gnn_Wd1, L2_gnn_bd1, L2_gnn_Wd2, L2_gnn_bd2, L2_gnn_g1, L2_gnn_beta1, L2_gnn_g2, L2_gnn_beta2, L3_gnn_W):
    import jax
    import jax.numpy as jnp

    def _L0_gnn_ref(x, edge_src, edge_dst, edge_val, W, b):
        import jax, jax.numpy as jnp
        import numpy as np
        N_NODES = 6250
        N_EDGES = 100000
        D_IN = 128
        D_OUT = 128
        msgs = edge_val[:, None] * x[edge_src]
        h = jax.ops.segment_sum(msgs, edge_dst, num_segments=N_NODES)
        out = jnp.einsum('nd,od->no', h, W) + b
        return jax.nn.relu(out)

    def _L1_gnn_ref(x, edge_index, W1, b1, W2, b2):
        import jax, jax.numpy as jnp
        import numpy as np
        N = 12500
        E = 200000
        D_IN = 128
        D_HID = 128

        def gcn_conv(x, src, dst, norm, W, b, n_nodes):
            h = x @ W
            msg = h[src] * norm[:, None]
            out = jax.ops.segment_sum(msg, dst, num_segments=n_nodes)
            return out + b

        def _prep_edges(edge_index, n_nodes):
            loops = jnp.arange(n_nodes, dtype=edge_index.dtype)
            src = jnp.concatenate([edge_index[0], loops])
            dst = jnp.concatenate([edge_index[1], loops])
            deg = jax.ops.segment_sum(jnp.ones_like(dst, dtype=jnp.float32), dst, num_segments=n_nodes)
            dinv = jnp.where(deg > 0, jax.lax.rsqrt(deg), 0.0)
            norm = dinv[src] * dinv[dst]
            return (src, dst, norm)
        n_nodes = x.shape[0]
        src, dst, norm = _prep_edges(edge_index, n_nodes)
        h = gcn_conv(x, src, dst, norm, W1, b1, n_nodes)
        h = jax.nn.relu(h)
        out = gcn_conv(h, src, dst, norm, W2, b2, n_nodes)
        return out

    def _L2_gnn_ref(h_V, h_E, edge_idx, W1, b1, W2, b2, W3, b3, Wd1, bd1, Wd2, bd2, g1, beta1, g2, beta2):
        import jax, jax.numpy as jnp
        import numpy as np
        N_NODES = 2500
        N_EDGES = 80000
        D = 128
        EPS = 1e-05

        def _layernorm(x, g, b):
            mu = jnp.mean(x, axis=-1, keepdims=True)
            var = jnp.var(x, axis=-1, keepdims=True)
            return (x - mu) * jax.lax.rsqrt(var + EPS) * g + b
        src_idx, tgt_idx = (edge_idx[0], edge_idx[1])
        n = h_V.shape[0]
        h_EV = jnp.concatenate([h_E, h_V[src_idx], h_V[tgt_idx]], axis=-1)
        h = jax.nn.relu(h_EV @ W1 + b1)
        h = jax.nn.relu(h @ W2 + b2)
        h_message = h @ W3 + b3
        msg_sum = jax.ops.segment_sum(h_message, tgt_idx, num_segments=n)
        cnt = jax.ops.segment_sum(jnp.ones((h_message.shape[0],), h_message.dtype), tgt_idx, num_segments=n)
        dh = msg_sum / cnt[:, None]
        h_V = _layernorm(h_V + dh, g1, beta1)
        dh = jax.nn.relu(h_V @ Wd1 + bd1) @ Wd2 + bd2
        h_V = _layernorm(h_V + dh, g2, beta2)
        return h_V

    def _L3_gnn_ref(x, W, edge_src, edge_dst, edge_val):
        import jax, jax.numpy as jnp
        import numpy as np
        N = 6250
        D = 128
        E = 100000
        n = x.shape[0]
        msgs = edge_val[:, None] * x[edge_dst]
        h1 = jax.ops.segment_sum(msgs, edge_src, num_segments=n)
        degree = jax.ops.segment_sum(edge_val, edge_src, num_segments=n)
        h1 = h1 / (degree[:, None] + 1e-06)
        h = jnp.concatenate([x, h1], axis=1)
        return h @ W
    edge_index = jnp.stack([src, dst])
    x = _layernorm(x + _L0_gnn_ref(x, src, dst, edge_weight, L0_gnn_W, L0_gnn_b), axis=-1)
    x = _layernorm(x + _L1_gnn_ref(x, edge_index, L1_gnn_W1, L1_gnn_b1, L1_gnn_W2, L1_gnn_b2), axis=-1)
    x = _layernorm(x + _L2_gnn_ref(x, edge_attr_128, edge_index, L2_gnn_W1, L2_gnn_b1, L2_gnn_W2, L2_gnn_b2, L2_gnn_W3, L2_gnn_b3, L2_gnn_Wd1, L2_gnn_bd1, L2_gnn_Wd2, L2_gnn_bd2, L2_gnn_g1, L2_gnn_beta1, L2_gnn_g2, L2_gnn_beta2), axis=-1)
    x = _layernorm(x + _L3_gnn_ref(x, L3_gnn_W, src, dst, edge_weight), axis=-1)
    return x

_drawn_inputs = setup_inputs


def setup_inputs(seed=0):
    import zlib

    import numpy as np

    out = dict(_drawn_inputs(seed))
    spreads = {'L1_gnn_b1': (0.0, 0.1),
     'L1_gnn_b2': (0.0, 0.1),
     'L2_gnn_b1': (0.0, 0.8),
     'L2_gnn_b2': (0.0, 0.487),
     'L2_gnn_b3': (0.0, 0.1),
     'L2_gnn_bd1': (0.0, 0.387),
     'L2_gnn_bd2': (0.0, 0.1),
     'L2_gnn_g1': (1.0, 0.2),
     'L2_gnn_beta1': (0.0, 0.1),
     'L2_gnn_g2': (1.0, 0.2),
     'L2_gnn_beta2': (0.0, 0.1)}
    factors = {'edge_attr_128': 8.0, 'L0_gnn_b': 8.0, 'L2_gnn_W1': 2.884}
    for name, (base, spread) in spreads.items():
        noise = np.random.default_rng([zlib.crc32(name.encode()), seed]).standard_normal(out[name].shape)
        drawn = base * np.exp(spread * noise) if base else spread * noise
        out[name] = jnp.asarray(drawn.astype(out[name].dtype))
    for name, factor in factors.items():
        out[name] = (out[name] * factor).astype(out[name].dtype)
    return out
```

```python
import concourse.bass as bass
from concourse import mybir
from contextlib import ExitStack

P = 128
N_NODES = 6250
N_EDGES = 106250
BLOCKS = -(-N_NODES // P)
NODES = BLOCKS * P
GROUP = 7
GROUPS = BLOCKS // GROUP
SPAN = GROUP * P
HALF = 8
BATCH = 4
ITERATIONS = -(-N_EDGES // (P * HALF * 2))
CHUNKS = ITERATIONS * HALF * 2
EDGES = CHUNKS * P
CHUNKS_AHEAD = CHUNKS + 2 * HALF
STEPS = CHUNKS // BATCH
WIDE = NODES + P
ROW = P + 1
EPS = 1e-5
TABLES = 2 * BATCH
ZERO_PARTS = 10
ZERO_COLS = WIDE * ROW // P // ZERO_PARTS


def gnn_program(nc, x, edge_attr, first_dst, dst_t, src_t, weight_t, w0_t, w1, w2, e_w1, e_w2, e_w3,
                e_wd1, e_wd2, w_last, row_vectors, e_b1, e_bd1, out):
    f32, bf16, i32, u32 = mybir.dt.float32, mybir.dt.bfloat16, mybir.dt.int32, mybir.dt.uint32
    ALU = mybir.AluOpType
    ACT = mybir.ActivationFunctionType
    AX = mybir.AxisListType
    ds = bass.ds

    with ExitStack() as ctx:
        def sb(name, shape, dt=f32):
            return ctx.enter_context(nc.sbuf_tensor(name, shape, dt))

        def sem(name):
            return ctx.enter_context(nc.semaphore(name))

        def dram(name, shape, dt=f32):
            return nc.dram_tensor(name, shape, dt, kind="Internal").ap()

        table1 = dram("table1", [NODES, P])
        table2 = dram("table2", [NODES, P])
        table_p = dram("table_p", [NODES, P])
        table_q = dram("table_q", [WIDE, P])
        table_x = dram("table_x", [WIDE, P])
        dloc_rows = dram("dloc_rows", [CHUNKS, P], bf16)
        src_rows = dram("src_rows", [CHUNKS, P])
        count_row_d = dram("count_row_d", [NODES])
        sums_d = [dram(f"sums{t}", [WIDE, ROW]) for t in range(TABLES)]

        X = sb("X", [P, BLOCKS, P])
        acc = sb("acc", [P, WIDE])
        srcI = sb("srcI", [P, CHUNKS], i32)
        srcF = sb("srcF", [P, CHUNKS])
        dloc = sb("dloc", [P, CHUNKS_AHEAD])
        wt = sb("wt", [P, CHUNKS])
        first = sb("first", [1, CHUNKS], i32)
        rowI = sb("rowI", [P, CHUNKS], i32)
        dstI = rowI
        W0 = sb("W0", [P, P])
        W1 = sb("W1", [P, P])
        W2 = sb("W2", [P, P])
        EW1 = sb("EW1", [P, 3, P])
        EW2 = sb("EW2", [P, P])
        EW3 = sb("EW3", [P, P])
        EWd1 = sb("EWd1", [P, 4 * P])
        EWd2 = sb("EWd2", [P, 4, P])
        WL = sb("WL", [P, 2, P])
        vec = sb("vec", [P, 9, P])
        eb2 = sb("eb2", [1, P])
        eb1 = sb("eb1", [P, 1])
        ebd1 = sb("ebd1", [P, 4])
        iota = sb("iota", [P, P])
        iopI = sb("iopI", [P, 1], i32)
        iop = sb("iop", [P, 1])
        trash = sb("trash", [P, 1])
        ident = sb("ident", [P, P])
        lower = sb("lower", [P, P])
        ones = sb("ones", [P, P])
        ones_bf = sb("ones_bf", [1, P], bf16)
        zeros = sb("zeros", [P, ZERO_COLS])
        count_row = sb("count_row", [1, WIDE])
        count = sb("count", [P, BLOCKS])
        dinv = sb("dinv", [P, BLOCKS])
        cinv = sb("cinv", [P, BLOCKS])
        space = sb("space", [P, 8 * HALF * P])

        def in_space(at, *shape):
            n = shape[0] * shape[1]
            return space[:, at:at + n].rearrange("p (a b) -> p a b", b=shape[1])

        G, Gw, O, Win = ([in_space((2 * n + b) * HALF * P, HALF, P) for b in range(2)] for n in range(4))
        sT = in_space(6 * HALF * P, GROUP, P)
        dT = space[:, 7 * HALF * P:7 * HALF * P + SPAN // 2].bitcast(bf16).rearrange(
            "p (a b) -> p a b", b=P)
        PQ = in_space(0, GROUP, 2 * P)
        HD = in_space(0, 4, SPAN)
        SG = in_space(0, TABLES, GROUP * ROW)
        S1 = space[:, TABLES * GROUP * ROW:(TABLES + 1) * GROUP * ROW]
        IX = [sb(f"IX{b}", [P, HALF], i32) for b in range(2)]
        drow = [sb(f"drow{b}", [1, HALF * P], bf16) for b in range(2)]
        srow = [sb(f"srow{b}", [1, HALF * P]) for b in range(2)]
        OT = [sb(f"OT{b}", [P, BATCH, P]) for b in range(2)]
        ET = [sb(f"ET{b}", [P, BATCH, P]) for b in range(2)]
        H1 = [sb(f"H1{b}", [P, BATCH, P]) for b in range(2)]
        H2 = [sb(f"H2{b}", [P, BATCH, P]) for b in range(2)]
        eq = H2[0]
        iotaI = H2[1][:, 0, :].bitcast(i32)
        Mw = [sb(f"Mw{b}", [P, BATCH, ROW]) for b in range(2)]
        R = [sb(f"R{b}", [P, BATCH, ROW]) for b in range(2)]
        RX = [sb(f"RX{b}", [P, BATCH], i32) for b in range(2)]
        stage = sb("stage", [P, SPAN])
        firstF = stage[0:1, 0:CHUNKS]
        A = sb("A", [P, GROUP, P])
        V = sb("V", [P, GROUP, P])
        T = sb("T", [P, GROUP, P])
        TX = sb("TX", [P, GROUP, P])
        XT = sb("XT", [P, SPAN])
        HT = V[:].rearrange("p a b -> p (a b)")
        repeats = HT[:, 0:CHUNKS]
        dstF = TX[:].rearrange("p a b -> p (a b)")[:, 0:CHUNKS]
        stats = sb("stats", [P, GROUP, 6])
        mv = sb("mv", [P, GROUP, 2])
        var = sb("var", [P, GROUP])
        sd = sb("sd", [P, GROUP])
        rstd = sb("rstd", [P, GROUP])
        ps = ctx.enter_context(nc.psum_tensor("ps", [P, 8, 512], f32))

        N_LOADS = 17 + 9

        loaded = sem("loaded")
        made_iota = sem("made_iota")
        dve_step = sem("dve_step")
        setup_bc = sem("setup_bc")
        setup_dloc = sem("setup_dloc")
        setup_tr = sem("setup_tr")
        setup_ev = sem("setup_ev")
        rows_out = sem("rows_out")
        zeroed = sem("zeroed")
        gate = {n: sem(f"gate_{n}") for n in ("pool", "act", "dve", "sp")}
        staged_idx = sem("staged_idx")
        gathered = [[sem(f"gathered{k}{b}") for b in range(2)] for k in range(4)]
        onehot = [[sem(f"onehot{k}{b}") for b in range(2)] for k in range(3)]
        summed = [[sem(f"summed{k}{b}") for b in range(2)] for k in range(3)]
        added = [[sem(f"added{k}{b}") for b in range(2)] for k in range(3)]
        scaled = [sem(f"scaled{b}") for b in range(2)]
        srow_in = [sem(f"srow_in{b}") for b in range(2)]
        src_bc = sem("src_bc")
        eq_made = sem("eq_made")
        row_index = sem("row_index")
        acc_clear = sem("acc_clear")
        counted = sem("counted")
        count_out = sem("count_out")
        count_in = sem("count_in")
        deg_made = sem("deg_made")
        root_made = sem("root_made")
        acc_staged = [sem(f"acc_staged{s}") for s in range(4)]
        product = [sem(f"product{s}") for s in range(5)]
        product_read = [sem(f"product_read{s}") for s in range(5)]
        var_ready = [sem(f"var_ready{s}") for s in range(6)]
        sd_ready = [sem(f"sd_ready{s}") for s in range(6)]
        t_ready = [sem(f"t_ready{s}") for s in range(5)]
        t_stored = [sem(f"t_stored{s}") for s in range(5)]
        turned = [sem(f"turned{s}") for s in range(5)]
        acc_set = [sem(f"acc_set{s}") for s in range(5)]
        pq_product = sem("pq_product")
        pq_ready = sem("pq_ready")
        pq_stored = sem("pq_stored")
        pad_stored = sem("pad_stored")
        e_loaded = [sem(f"e_loaded{b}") for b in range(2)]
        q_loaded = [sem(f"q_loaded{b}") for b in range(2)]
        e_used = [sem(f"e_used{b}") for b in range(2)]
        g_used = [sem(f"g_used{b}") for b in range(2)]
        e_turned = sem("e_turned")
        et_ready = sem("et_ready")
        ot_made = sem("ot_made")
        o_made = sem("o_made")
        h1_product = sem("h1_product")
        h1_ready = sem("h1_ready")
        h2_product = sem("h2_product")
        h2_ready = sem("h2_ready")
        e_summed = sem("e_summed")
        e_added = sem("e_added")
        hid_product = sem("hid_product")
        hid_ready = sem("hid_ready")
        ffn_product = sem("ffn_product")
        ffn_read = sem("ffn_read")
        l_rows = [sem(f"l_rows{b}") for b in range(2)]
        l_win = [sem(f"l_win{b}") for b in range(2)]
        rows_used = [sem(f"rows_used{b}") for b in range(2)]
        win_used = [sem(f"win_used{b}") for b in range(2)]
        l_bc = sem("l_bc")
        l_ot = sem("l_ot")
        l_eq = sem("l_eq")
        m_product = sem("m_product")
        m_ready = sem("m_ready")
        r_product = sem("r_product")
        r_ready = sem("r_ready")
        scattered = [sem(f"scattered{q}") for q in range(2)]
        sums_in = sem("sums_in")
        sums_used = sem("sums_used")
        out_stored = sem("out_stored")

        block = ctx.enter_context(nc.Block())

        def bank(n, k=1):
            return ps[:, n:n + k, :].rearrange("p a b -> p (a b)")

        def blocks_of(ap, width=P, n=GROUP):
            return ap[:, 0:n * width].rearrange("p (a b) -> p a b", b=width)

        def along(ap, n=P):
            return ap.unsqueeze(2).broadcast_to([ap.shape[0], ap.shape[1], n])

        def over(ap, n):
            return ap.unsqueeze(1).broadcast_to([ap.shape[0], n, ap.shape[1]])

        def acc_group(g):
            return acc[:, ds(g * SPAN, SPAN)]

        def x_group(g):
            return X[:, ds(g * GROUP, GROUP), :]

        def window_starts(eng, kind, c, n):
            return [nc.values_load(first[0:1, ds(c + j, 1)], engines=[kind], min_val=0, max_val=NODES - 1,
                                   skip_runtime_bounds_check_because="destinations are node numbers")
                    for j in range(n)]

        class Steps:

            def __init__(self, eng):
                self.eng, self.base, self.k, self.i, self.per = eng, 0, 0, None, 0

            def __call__(self, ins):
                ins.then_inc(dve_step, 1)
                self.k += 1
                at = self.base + self.k if self.i is None else self.i * self.per + (self.base + self.k)
                self.eng.wait_ge(dve_step, at)

            def enter(self, i, per, start=0):
                self.base += self.k - start * per
                self.i, self.per, self.k = i, per, 0
                self.start = start

            def leave(self, end):
                assert self.k == self.per, (self.k, self.per)
                self.base += end * self.per
                self.i, self.k = None, 0

        @block.sync
        def _(sp):
            SP = mybir.EngineType.SP
            for tile, source in [
                (dstI[:], dst_t), (first[:], first_dst), (srcI[:], src_t), (wt[:], weight_t),
                (W0[:], w0_t), (W1[:], w1), (W2[:], w2),
                (EW1[:], e_w1.rearrange("(a p) n -> p a n", p=P)), (EW2[:], e_w2), (EW3[:], e_w3),
                (EWd1[:], e_wd1), (EWd2[:], e_wd2.rearrange("(a p) n -> p a n", p=P)),
                (WL[:], w_last.rearrange("(a p) n -> p a n", p=P)),
                (eb1[:], e_b1), (ebd1[:], e_bd1),
                (eb2[:], row_vectors[9:10, :]),
                (X[:], x.rearrange("(b p) d -> p b d", p=P)),
            ]:
                sp.dma_start(tile, source).then_inc(loaded, 16)
            for v in range(9):
                sp.dma_start(vec[:, v, :], row_vectors[v:v + 1, :].broadcast_to([P, P])).then_inc(loaded, 16)
            sp.wait_ge(setup_ev, 4)
            full = CHUNKS // P
            rest = CHUNKS - full * P
            sp.dma_start(dloc_rows[0:full * P, :].rearrange("(a p) e -> p a e", p=P),
                         dT[:, 0:full, :]).then_inc(rows_out, 16)
            sp.dma_start(dloc_rows[full * P:CHUNKS, :], dT[0:rest, full, :]).then_inc(rows_out, 16)
            sp.dma_start(src_rows[0:full * P, :].rearrange("(a p) e -> p a e", p=P),
                         sT[:, 0:full, :]).then_inc(rows_out, 16)
            sp.dma_start(src_rows[full * P:CHUNKS, :], sT[0:rest, full, :]).then_inc(rows_out, 16)
            sp.wait_ge(made_iota, 5)
            sp.dma_start(table_q[NODES:WIDE, :], zeros[:, 0:P]).then_inc(pad_stored, 16)
            sp.dma_start(table_x[NODES:WIDE, :], zeros[:, 0:P]).then_inc(pad_stored, 16)

            sp.wait_ge(counted, 1)
            sp.dma_start(count_row_d.rearrange("(o n) -> o n", o=1), count_row[0:1, 0:NODES]).then_inc(count_out, 16)
            sp.wait_ge(count_out, 16)
            sp.dma_start(count[:], count_row_d.rearrange("(b p) -> p b", p=P), allow_slow_non_contiguous=True).then_inc(count_in, 16)

            def store_groups(s, table, ready):
                rows = table[0:NODES, :].rearrange("(b p) d -> p b d", p=P)
                with sp.Fori(0, GROUPS) as g:
                    sp.wait_ge(ready, g + 1)
                    sp.dma_start(rows[:, ds(g * GROUP, GROUP), :], T[:]).then_inc(t_stored[s], 16)

            store_groups(0, table1, t_ready[0])
            store_groups(1, table2, t_ready[1])

            sp.wait_ge(rows_out, 64)
            with sp.Fori(0, ITERATIONS) as i:
                for b in range(2):
                    sp.wait_ge(eq_made, i * 4 + 2 * b)
                    sp.dma_start(srow[b][:], src_rows[ds(i * 2 * HALF + b * HALF, HALF), :]
                                 .rearrange("(o c) e -> o (c e)", o=1)).then_inc(srow_in[b], 16)

            rows_p = table_p.rearrange("(b p) d -> p b d", p=P)
            rows_q = table_q[0:NODES, :].rearrange("(b p) d -> p b d", p=P)
            with sp.Fori(0, GROUPS) as g:
                sp.wait_ge(pq_ready, g + 1)
                sp.dma_start(rows_p[:, ds(g * GROUP, GROUP), :], PQ[:, :, 0:P]).then_inc(pq_stored, 16)
                sp.dma_start(rows_q[:, ds(g * GROUP, GROUP), :], PQ[:, :, P:2 * P]).then_inc(pq_stored, 16)

            sp.wait_ge(pq_stored, 32 * GROUPS)
            sp.wait_ge(pad_stored, 32)
            edge_rows = edge_attr.rearrange("(c e) d -> e c d", e=P)
            with sp.Fori(0, ITERATIONS) as i:
                for b in range(2):
                    c = i * 2 * HALF + b * HALF
                    sp.wait_ge(e_used[b], i)
                    sp.dma_start(Gw[b], edge_rows[:, ds(c, HALF), :]).then_inc(e_loaded[b], 16)
                    sp.dma_start(drow[b][:], dloc_rows[ds(c, HALF), :].rearrange("(o c) e -> o (c e)", o=1)
                                 ).then_inc(e_loaded[b], 16)
                    sp.wait_ge(g_used[b], i)
                    sp.sem_inc(gate["sp"], 1)
                    for j, n0 in enumerate(window_starts(sp, SP, c, HALF)):
                        sp.dma_start(Win[b][:, j, :], table_q[ds(n0, P), :]).then_inc(q_loaded[b], 16)

            store_groups(3, table_x, t_ready[3])
            sp.wait_ge(t_stored[3], 16 * GROUPS)
            with sp.Fori(0, ITERATIONS) as i:
                for b in range(2):
                    c = i * 2 * HALF + b * HALF
                    sp.wait_ge(rows_used[b], i)
                    sp.dma_start(drow[b][:], dloc_rows[ds(c, HALF), :].rearrange("(o c) e -> o (c e)", o=1)
                                 ).then_inc(l_rows[b], 16)
                    sp.dma_start(srow[b][:], src_rows[ds(c, HALF), :].rearrange("(o c) e -> o (c e)", o=1)
                                 ).then_inc(l_rows[b], 16)
                    sp.wait_ge(win_used[b], i)
                    sp.sem_inc(gate["sp"], 1)
                    for j, n0 in enumerate(window_starts(sp, SP, c, HALF)):
                        sp.dma_start(Win[b][:, j, :], table_x[ds(n0, P), :]).then_inc(l_win[b], 16)

            for q in range(2):
                sp.wait_ge(scattered[q], 16 * BATCH * (STEPS // 2))
            with sp.Fori(0, GROUPS) as g:
                sp.wait_ge(sums_used, g)
                for t in range(TABLES):
                    rows = sums_d[t][0:NODES, :].rearrange("(b p) d -> p b d", p=P)
                    sp.dma_start(SG[:, t, :].rearrange("p (a b) -> p a b", b=ROW),
                                 rows[:, ds(g * GROUP, GROUP), :]).then_inc(sums_in, 16)
            sp.wait_ge(out_stored, 16 * GROUPS)

        @block.gpsimd
        def _(pool):
            nc.gpsimd.iota(iotaI, pattern=[[1, P]], base=0, channel_multiplier=0).then_inc(made_iota, 1)
            nc.gpsimd.iota(iopI[:], pattern=[[0, 1]], base=0, channel_multiplier=1).then_inc(made_iota, 1)
            nc.gpsimd.memset(zeros[:], 0.0).then_inc(made_iota, 1)
            nc.gpsimd.memset(acc[:], 0.0).then_inc(made_iota, 1)
            nc.gpsimd.memset(count_row[:], 0.0).then_inc(made_iota, 1)
            pool.wait_ge(loaded, 16 * N_LOADS)

            def gathers(k, table, used):
                with pool.Fori(0, ITERATIONS) as i:
                    for b in range(2):
                        pool.wait_ge(gathered[k][b], i * (16 * HALF))
                        pool.wait_ge(used[b], i)
                        pool.sem_inc(gate["pool"], 1)
                        nc.gpsimd.tensor_copy(IX[b][:], srcI[:, ds(i * 2 * HALF + b * HALF, HALF)]
                                              ).then_inc(staged_idx, 1)
                        pool.wait_ge(staged_idx, i * 2 + (k * 2 * ITERATIONS + b + 1))
                        pool.sem_inc(gate["pool"], 1)
                        for j in range(HALF):
                            pool.indirect_dma_start(
                                G[b][:, j, :], None, table,
                                bass.IndirectOffsetOnAxis(ap=IX[b][:, j:j + 1].bitcast(u32), axis=0),
                            ).then_inc(gathered[k][b], 16)

            def stage_groups(s):
                with pool.Fori(0, GROUPS) as g:
                    pool.wait_ge(product[s], g)
                    pool.sem_inc(gate["pool"], 1)
                    nc.gpsimd.tensor_copy(stage[:], acc_group(g)).then_inc(acc_staged[s], 1)

            gathers(0, x, scaled)
            for b in range(2):
                pool.wait_ge(added[0][b], ITERATIONS)
            stage_groups(0)
            pool.wait_ge(t_stored[0], 16 * GROUPS)
            gathers(1, table1, summed[1])
            for b in range(2):
                pool.wait_ge(added[1][b], ITERATIONS)
            stage_groups(1)
            pool.wait_ge(t_stored[1], 16 * GROUPS)
            gathers(2, table2, summed[2])
            for b in range(2):
                pool.wait_ge(added[2][b], ITERATIONS)
            stage_groups(2)
            pool.wait_ge(acc_staged[2], GROUPS)
            nc.gpsimd.memset(acc[:], 0.0).then_inc(acc_clear, 1)
            pool.wait_ge(pq_stored, 32 * GROUPS)
            gathers(3, table_p, g_used)
            pool.wait_ge(e_added, STEPS)
            stage_groups(3)

            pool.wait_ge(zeroed, 16 * TABLES * ZERO_PARTS)
            pool.wait_ge(row_index, 1)
            with pool.Fori(0, ITERATIONS * 2) as i:
                for q in range(2):
                    pool.wait_ge(scattered[q], i * (16 * BATCH))
                    pool.sem_inc(gate["pool"], 1)
                    nc.gpsimd.tensor_copy(RX[q][:], rowI[:, ds(i * HALF + q * BATCH, BATCH)]).then_inc(staged_idx, 1)
                    pool.wait_ge(staged_idx, i * 2 + (8 * ITERATIONS + q + 1))
                    pool.wait_ge(r_ready, i * 2 + (q + 1))
                    pool.sem_inc(gate["pool"], 1)
                    for j in range(BATCH):
                        pool.indirect_dma_start(
                            sums_d[q * BATCH + j],
                            bass.IndirectOffsetOnAxis(ap=RX[q][:, j:j + 1].bitcast(u32), axis=0),
                            R[q][:, j, :], None, compute_op=ALU.add,
                        ).then_inc(scattered[q], 16)

        @block.scalar
        def _(act):
            act.wait_ge(made_iota, 3)
            act.wait_ge(loaded, 16 * N_LOADS)

            with act.Fori(0, ITERATIONS) as i:
                for b in range(2):
                    act.wait_ge(gathered[0][b], i * (16 * HALF) + 16 * HALF)
                    act.wait_ge(summed[0][b], i)
                    act.sem_inc(gate["act"], 1)
                    for j in range(HALF):
                        last = nc.scalar.activation(Gw[b][:, j, :], G[b][:, j, :], ACT.Copy,
                                                    scale=wt[:, ds(i * 2 * HALF + b * HALF + j, 1)])
                    last.then_inc(scaled[b], 1)

            act.wait_ge(deg_made, 1)
            nc.scalar.activation(dinv[:], dinv[:], ACT.Sqrt).then_inc(root_made, 1)

            def roots(s, g):
                act.wait_ge(var_ready[s], g + 1)
                nc.scalar.activation(sd[:], var[:], ACT.Sqrt).then_inc(sd_ready[s], 1)

            def set_acc(s, g):
                act.wait_ge(turned[s], g + 1)
                act.sem_inc(gate["act"], 1)
                nc.scalar.copy(acc_group(g), bank(2, 2)[:, 0:SPAN]).then_inc(acc_set[s], 1)

            with act.Fori(0, GROUPS) as g:
                roots(0, g)
                set_acc(0, g)

            for t in range(TABLES):
                parts = sums_d[t].rearrange("n d -> (n d)").rearrange("(a p f) -> a p f", p=P, f=ZERO_COLS)
                for a in range(ZERO_PARTS):
                    act.dma_start(parts[a], zeros[:]).then_inc(zeroed, 16)

            with act.Fori(0, GROUPS) as g:
                set_acc(1, g)

            with act.Fori(0, GROUPS) as g:
                roots(2, g)
                act.wait_ge(turned[2], g + 1)
                act.wait_ge(pq_product, g)
                nc.scalar.copy(XT[:], bank(2, 2)[:, 0:SPAN]).then_inc(acc_set[2], 1)
                act.wait_ge(pq_product, g + 1)
                act.wait_ge(pq_stored, g * 32)
                nc.scalar.copy(PQ, bank(4, 4)[:, 0:GROUP * 2 * P].rearrange("p (a b) -> p a b", b=2 * P)
                               ).then_inc(pq_ready, 1)

            def evacuate_e(t, par):
                act.wait_ge(e_turned, t + 1)
                if not (type(t) is int and t < 2):
                    act.wait_ge(h1_product, t - 1)
                nc.scalar.copy(ET[par][:].rearrange("p a b -> p (a b)"), bank(1 if par == 0 else 7)
                               ).then_inc(et_ready, 1)

            def relu_h1(t, par):
                act.wait_ge(h1_product, t + 1)
                if not (type(t) is int and t < 2):
                    act.wait_ge(h2_product, t - 1)
                nc.scalar.activation(H1[par][:].rearrange("p a b -> p (a b)"), bank(2 + par), ACT.Relu,
                                     bias=eb1[:, 0:1]).then_inc(h1_ready, 1)

            def relu_h2(t, par):
                act.wait_ge(h2_product, t + 1)
                if not (type(t) is int and t < 2):
                    act.wait_ge(e_summed, t - 1)
                nc.scalar.activation(H2[par][:].rearrange("p a b -> p (a b)"), bank(4), ACT.Relu
                                     ).then_inc(h2_ready, 1)

            def edge_iteration(i, start, end):
                for s in range(4):
                    t = i * 4 + s
                    if not (end and s == 3):
                        evacuate_e(t + 1, (s + 1) % 2)
                    relu_h1(t, s % 2)
                    if not (start and s == 0):
                        relu_h2(t - 1, (s + 1) % 2)

            evacuate_e(0, 0)
            edge_iteration(0, True, False)
            with act.Fori(1, ITERATIONS - 1) as i:
                edge_iteration(i, False, False)
            edge_iteration(ITERATIONS - 1, False, True)
            relu_h2(STEPS - 1, 1)

            with act.Fori(0, GROUPS) as g:
                roots(3, g)
                act.wait_ge(turned[3], g + 1)
                act.wait_ge(hid_product, g * 8)
                nc.scalar.copy(XT[:], bank(2, 2)[:, 0:SPAN]).then_inc(acc_set[3], 1)
                for h in range(4):
                    for z in range(2):
                        act.wait_ge(hid_product, g * 8 + (2 * h + z + 1))
                        if h == 0 and z == 0:
                            act.wait_ge(ffn_product, g)
                        nc.scalar.activation(HD[:, h, z * (SPAN // 2):(z + 1) * (SPAN // 2)],
                                             bank(4 + z)[:, 0:SPAN // 2], ACT.Relu,
                                             bias=ebd1[:, h:h + 1]).then_inc(hid_ready, 1)
                for z in range(2):
                    act.wait_ge(var_ready[4], g * 2 + (z + 1))
                    nc.scalar.activation(sd[:], var[:], ACT.Sqrt).then_inc(sd_ready[4], 1)

            def weigh(i, q, b, t, par):
                act.wait_ge(m_product, t + 1)
                if not (type(t) is int and t < 2):
                    act.wait_ge(r_product, t - 1)
                act.sem_inc(gate["act"], 1)
                c = i * 2 * HALF + (b * HALF + q * BATCH)
                for j in range(BATCH):
                    nc.scalar.activation(Mw[par][:, j, 0:P], bank(2 + par)[:, j * P:(j + 1) * P], ACT.Copy,
                                         scale=wt[:, ds(c + j, 1)])
                nc.scalar.copy(Mw[par][:, :, P:ROW], wt[:, ds(c, BATCH)].unsqueeze(2)).then_inc(m_ready, 1)

            def evacuate_r(i, q, b, t, par):
                act.wait_ge(r_product, t + 1)
                if i is not None:
                    act.wait_ge(scattered[q], i * (32 * BATCH) + b * (16 * BATCH))
                nc.scalar.copy(R[par][:], bank(4 + 2 * par, 2).rearrange("p (a b) -> p a b", b=256)[:, :, 0:ROW]
                               ).then_inc(r_ready, 1)

            def last_iteration(i, start):
                for s in range(4):
                    t = i * 4 + s
                    weigh(i, s % 2, s // 2, t, s % 2)
                    if s == 0:
                        if not start:
                            evacuate_r(i - 1, 1, 1, t - 1, 1)
                    else:
                        evacuate_r(i, (s - 1) % 2, (s - 1) // 2, t - 1, (s - 1) % 2)

            last_iteration(0, True)
            with act.Fori(1, ITERATIONS) as i:
                last_iteration(i, False)
            evacuate_r(ITERATIONS - 1, 1, 1, STEPS - 1, 1)

            with act.Fori(0, GROUPS) as g:
                act.wait_ge(turned[4], g + 1)
                act.wait_ge(product[4], g)
                nc.scalar.copy(XT[:], bank(2, 2)[:, 0:SPAN])
                nc.scalar.copy(HT[:], bank(4, 2)[:, 0:SPAN]).then_inc(acc_set[4], 1)
                roots(5, g)
                act.wait_ge(t_ready[4], g + 1)
                act.dma_start(out.rearrange("(b p) d -> p b d", p=P)[:, ds(g * GROUP, GROUP), :], A[:]
                              ).then_inc(out_stored, 16)

        @block.vector
        def _(dve):
            DVE = mybir.EngineType.DVE
            step = Steps(dve)
            VB0, VB1, VB2, VB3, VBD2, VG1, VBE1, VG2, VBE2 = range(9)

            dve.wait_ge(made_iota, 2)
            nc.vector.memset(ones[:], 1.0)
            nc.vector.memset(ones_bf[:], 1.0)
            nc.vector.memset(dloc[:, CHUNKS:CHUNKS_AHEAD], 0.0)
            nc.vector.tensor_copy(iota[:], iotaI)
            step(nc.vector.tensor_copy(iop[:], iopI[:]))
            nc.vector.tensor_scalar(trash[:], iop[:], float(NODES), None, ALU.add)
            nc.vector.tensor_scalar(ident[:], iota[:], iop[:, 0:1], None, ALU.is_equal)
            nc.vector.tensor_scalar(lower[:], iota[:], iop[:, 0:1], None, ALU.is_lt)
            dve.wait_ge(loaded, 16 * N_LOADS)
            nc.vector.tensor_copy(srcF[:], srcI[:])
            nc.vector.tensor_copy(dloc[:, 0:CHUNKS], dstI[:])
            nc.vector.tensor_copy(firstF, first[:]).then_inc(setup_dloc, 1)
            dve.wait_ge(setup_dloc, 1)
            dve.wait_ge(setup_bc, 1)
            half_c = CHUNKS // 2
            for z in range(2):
                last = nc.vector.tensor_tensor(dloc[:, z * half_c:(z + 1) * half_c],
                                               dloc[:, z * half_c:(z + 1) * half_c],
                                               bank(z)[:, 0:half_c], ALU.subtract)
            last.then_inc(setup_dloc, 1)
            dve.wait_ge(setup_tr, 1)
            full, rest = CHUNKS // P, CHUNKS % P
            for tile, at in ((dT, 2), (sT, 4)):
                nc.vector.tensor_copy(tile[:, 0:full, :], blocks_of(bank(at, 2), P, full)).then_inc(setup_ev, 1)
                nc.vector.tensor_copy(tile[0:rest, full, :], blocks_of(bank(at, 2))[0:rest, full, :]
                                      ).then_inc(setup_ev, 1)
            dve.wait_ge(setup_dloc, 2)

            def make_onehot(k, i, b):
                nc.vector.tensor_tensor(O[b], over(iota[:], HALF),
                                        along(dloc[:, ds(i * 2 * HALF + b * HALF, HALF)]),
                                        ALU.is_equal).then_inc(onehot[k][b], 1)

            def sums(k):
                per = 2 * (HALF * (2 if k == 0 else 1) + (4 if k == 2 else 0))
                for b in range(2):
                    make_onehot(k, 0, b)
                with dve.Fori(0, ITERATIONS) as i:
                    step.enter(i, per)
                    for b in range(2):
                        c = i * 2 * HALF + b * HALF
                        if k == 2:
                            for q in range(2):
                                dve.wait_ge(src_bc, i * 4 + (2 * b + q + 1))
                                nc.vector.tensor_tensor(eq[:], blocks_of(bank(4 + q), P, BATCH),
                                                        along(srcF[:, ds(c + q * BATCH, BATCH)]),
                                                        ALU.is_equal).then_inc(eq_made, 1)
                                dve.wait_ge(eq_made, i * 4 + (2 * b + q + 1))
                                step(nc.vector.tensor_tensor(eq[:], eq[:], over(lower[:], BATCH), ALU.mult))
                                step(nc.vector.tensor_reduce(repeats[:, ds(c + q * BATCH, BATCH)], eq[:],
                                                             axis=AX.X, op=ALU.add))
                        dve.wait_ge(summed[k][b], i + 1)
                        for j, n0 in enumerate(window_starts(dve, DVE, c, HALF)):
                            part = bank(2 * b, 2)[:, j * P:(j + 1) * P]
                            ins = nc.vector.tensor_tensor(acc[:, ds(n0, P)], acc[:, ds(n0, P)], part, ALU.add)
                            if k == 0:
                                step(ins)
                                part = bank(4 + 2 * b, 2)[0:1, j * P:(j + 1) * P]
                                ins = nc.vector.tensor_tensor(count_row[0:1, ds(n0, P)],
                                                              count_row[0:1, ds(n0, P)], part, ALU.add)
                            step(ins)
                        dve.sem_inc(added[k][b], 1)
                        make_onehot(k, i + 1, b)
                    step.leave(ITERATIONS)

            def norm(s, g, count_of=None):
                for j in range(GROUP):
                    last = nc.vector.bn_stats(stats[:, j, :], A[:, j, :])
                step(last)
                dve.sem_inc(gate["dve"], 1)
                for j in range(GROUP):
                    last = nc.vector.bn_aggr(mv[:, j, :], stats[:, j, :])
                step(last)
                nc.vector.tensor_scalar(var[:], mv[:, :, 1], EPS, None, ALU.add).then_inc(var_ready[s], 1)
                step(nc.vector.tensor_tensor(A[:], A[:], along(mv[:, :, 0]), ALU.subtract))
                dve.wait_ge(sd_ready[s], count_of if count_of is not None else g + 1)
                step(nc.vector.reciprocal(rstd[:], sd[:]))
                step(nc.vector.tensor_tensor(A[:], A[:], along(rstd[:]), ALU.mult))

            NORM = 5
            D = blocks_of(bank(0, 2))

            dve.wait_ge(made_iota, 5)
            sums(0)
            dve.sem_inc(counted, 1)
            dve.wait_ge(count_in, 16)
            step(nc.vector.reciprocal(cinv[:], count[:]))
            nc.vector.tensor_scalar(dinv[:], count[:], 1.0, None, ALU.add).then_inc(deg_made, 1)
            dve.wait_ge(root_made, 1)
            step(nc.vector.reciprocal(dinv[:], dinv[:]))

            def wait_t_free(s, g):
                dve.wait_ge(t_stored[s], g * 16)
                dve.wait_ge(turned[s], g)

            with dve.Fori(0, GROUPS) as g:
                step.enter(g, 2 + NORM)
                dve.wait_ge(t_ready[0], g)
                dve.wait_ge(product[0], g + 1)
                nc.vector.tensor_tensor(A[:], D, over(vec[:, VB0, :], GROUP), ALU.add).then_inc(product_read[0], 1)
                dve.wait_ge(product_read[0], g + 1)
                step(nc.vector.scalar_tensor_tensor(A[:], A[:], 0.0, x_group(g), ALU.max, ALU.add))
                norm(0, g)
                dve.sem_inc(gate["dve"], 1)
                step(nc.vector.tensor_copy(x_group(g), A[:]))
                wait_t_free(0, g)
                nc.vector.tensor_tensor(T[:], A[:], along(dinv[:, ds(g * GROUP, GROUP)]), ALU.mult
                                        ).then_inc(t_ready[0], 1)
                step.leave(GROUPS)

            dve.wait_ge(acc_set[0], GROUPS)
            sums(1)
            with dve.Fori(0, GROUPS) as g:
                step.enter(g, 1)
                dve.wait_ge(t_ready[1], g)
                dve.wait_ge(product[1], g + 1)
                nc.vector.tensor_tensor(A[:], D, along(dinv[:, ds(g * GROUP, GROUP)]), ALU.mult
                                        ).then_inc(product_read[1], 1)
                dve.wait_ge(product_read[1], g + 1)
                step(nc.vector.tensor_tensor(A[:], A[:], over(vec[:, VB1, :], GROUP), ALU.add))
                wait_t_free(1, g)
                nc.vector.scalar_tensor_tensor(T[:], A[:], 0.0, along(dinv[:, ds(g * GROUP, GROUP)]),
                                               ALU.max, ALU.mult).then_inc(t_ready[1], 1)
                step.leave(GROUPS)
            dve.wait_ge(acc_set[1], GROUPS)
            sums(2)
            step(nc.vector.tensor_scalar(repeats, repeats, 1.0, None, ALU.min))
            step(nc.vector.tensor_scalar(dstF, srcF[:], -1.0, trash[:, 0:1], ALU.mult, ALU.add))
            step(nc.vector.tensor_tensor(dstF, dstF, repeats, ALU.mult))
            nc.vector.tensor_tensor(rowI[:], dstF, srcF[:], ALU.add).then_inc(row_index, 1)

            with dve.Fori(0, GROUPS) as g:
                step.enter(g, 3 + NORM)
                dve.wait_ge(t_ready[2], g)
                dve.wait_ge(product[2], g + 1)
                nc.vector.tensor_tensor(A[:], D, along(dinv[:, ds(g * GROUP, GROUP)]), ALU.mult
                                        ).then_inc(product_read[2], 1)
                dve.wait_ge(product_read[2], g + 1)
                step(nc.vector.tensor_tensor(A[:], A[:], over(vec[:, VB2, :], GROUP), ALU.add))
                step(nc.vector.tensor_tensor(A[:], A[:], x_group(g), ALU.add))
                norm(2, g)
                dve.sem_inc(gate["dve"], 1)
                step(nc.vector.tensor_copy(x_group(g), A[:]))
                dve.wait_ge(turned[2], g)
                nc.vector.tensor_copy(T[:], A[:]).then_inc(t_ready[2], 1)
                step.leave(GROUPS)

            dve.wait_ge(acc_clear, 1)

            def spread(t, par):
                dve.wait_ge(e_turned, t + 1)
                if not (type(t) is int and t < 2):
                    dve.wait_ge(h1_product, t - 1)
                nc.vector.tensor_scalar(OT[par][:].rearrange("p a b -> p (a b)"), bank(0), iop[:, 0:1], None,
                                        ALU.is_equal).then_inc(ot_made, 1)

            def edge_onehot(i, b, t):
                if not (type(t) is int and t < 4):
                    dve.wait_ge(e_summed, t - 2)
                nc.vector.tensor_tensor(O[b], over(iota[:], HALF),
                                        along(dloc[:, ds(i * 2 * HALF + b * HALF, HALF)]),
                                        ALU.is_equal).then_inc(o_made, 1)

            def edge_add(i, s, t):
                c = i * 2 * HALF + s * BATCH
                dve.wait_ge(e_summed, t + 1)
                for j, n0 in enumerate(window_starts(dve, DVE, c, BATCH)):
                    ins = nc.vector.tensor_tensor(acc[:, ds(n0, P)], acc[:, ds(n0, P)],
                                                  bank(5 + s % 2)[:, j * P:(j + 1) * P], ALU.add)
                    if j < BATCH - 1:
                        step(ins)
                    else:
                        ins.then_inc(e_added, 1)
                dve.wait_ge(e_added, t + 1)

            def edge_iteration(i, start, end):
                for s in range(4):
                    t = i * 4 + s
                    if not (end and s == 3):
                        spread(t + 1, (s + 1) % 2)
                    if s % 2 == 0:
                        edge_onehot(i, s // 2, t)
                    if s >= 2:
                        edge_add(i, s - 2, t - 2)
                    elif not start:
                        edge_add(i - 1, s + 2, t - 2)

            spread(0, 0)
            edge_iteration(0, True, False)
            with dve.Fori(1, ITERATIONS - 1) as i:
                step.enter(i, 4 * (BATCH - 1), 1)
                edge_iteration(i, False, False)
                step.leave(ITERATIONS - 1)
            edge_iteration(ITERATIONS - 1, False, True)
            edge_add(ITERATIONS - 1, 2, STEPS - 2)
            edge_add(ITERATIONS - 1, 3, STEPS - 1)

            with dve.Fori(0, GROUPS) as g:
                step.enter(g, 8 + 3 * NORM)
                dve.wait_ge(t_ready[3], g)
                dve.wait_ge(product[3], g + 1)
                nc.vector.tensor_tensor(A[:], D, along(cinv[:, ds(g * GROUP, GROUP)]), ALU.mult
                                        ).then_inc(product_read[3], 1)
                dve.wait_ge(product_read[3], g + 1)
                step(nc.vector.tensor_tensor(A[:], A[:], over(vec[:, VB3, :], GROUP), ALU.add))
                step(nc.vector.tensor_tensor(A[:], A[:], x_group(g), ALU.add))
                norm(3, g)
                step(nc.vector.tensor_tensor(A[:], A[:], over(vec[:, VG1, :], GROUP), ALU.mult))
                nc.vector.tensor_tensor(V[:], A[:], over(vec[:, VBE1, :], GROUP), ALU.add).then_inc(t_ready[2], 1)
                dve.wait_ge(t_ready[2], g + (GROUPS + 1))
                dve.wait_ge(ffn_product, g + 1)
                nc.vector.tensor_tensor(A[:], blocks_of(bank(6, 2)), over(vec[:, VBD2, :], GROUP), ALU.add
                                        ).then_inc(ffn_read, 1)
                dve.wait_ge(ffn_read, g + 1)
                step(nc.vector.tensor_tensor(A[:], A[:], V[:], ALU.add))
                norm(4, g, g * 2 + 1)
                step(nc.vector.tensor_tensor(A[:], A[:], over(vec[:, VG2, :], GROUP), ALU.mult))
                step(nc.vector.tensor_tensor(A[:], A[:], over(vec[:, VBE2, :], GROUP), ALU.add))
                step(nc.vector.tensor_tensor(A[:], A[:], x_group(g), ALU.add))
                norm(4, g, g * 2 + 2)
                dve.sem_inc(gate["dve"], 1)
                step(nc.vector.tensor_copy(x_group(g), A[:]))
                dve.wait_ge(t_stored[3], g * 16)
                nc.vector.tensor_copy(T[:], A[:]).then_inc(t_ready[3], 1)
                step.leave(GROUPS)

            def last_spread(i, s, t, par):
                dve.wait_ge(l_bc, t + 1)
                if not (type(t) is int and t < 2):
                    dve.wait_ge(m_product, t - 1)
                nc.vector.tensor_scalar(OT[par][:].rearrange("p a b -> p (a b)"), bank(0), iop[:, 0:1], None,
                                        ALU.is_equal).then_inc(l_ot, 1)
                if not (type(t) is int and t < 2):
                    dve.wait_ge(r_product, t - 1)
                nc.vector.tensor_tensor(ET[par][:], blocks_of(bank(1), P, BATCH),
                                        along(srcF[:, ds(i * 2 * HALF + s * BATCH, BATCH)]), ALU.is_equal
                                        ).then_inc(l_eq, 1)

            for s in range(4):
                last_spread(0, s, s, s % 2)
            with dve.Fori(1, ITERATIONS) as i:
                for s in range(4):
                    last_spread(i, s, i * 4 + s, s % 2)

            with dve.Fori(0, GROUPS) as g:
                step.enter(g, 6)
                dve.wait_ge(sums_in, g * (16 * TABLES) + 16 * TABLES)
                nc.vector.tensor_reduce(S1, SG.rearrange("p t n -> p n t"), axis=AX.X, op=ALU.add
                                        ).then_inc(sums_used, 1)
                dve.wait_ge(sums_used, g + 1)
                S1v = S1.rearrange("p (a b) -> p a b", b=ROW)
                step(nc.vector.tensor_scalar(var[:], S1v[:, :, P], 1e-6, None, ALU.add))
                step(nc.vector.reciprocal(rstd[:], var[:]))
                dve.wait_ge(turned[4], g)
                dve.sem_inc(gate["dve"], 1)
                nc.vector.tensor_copy(T[:], x_group(g))
                nc.vector.tensor_tensor(TX[:], S1v[:, :, 0:P], along(rstd[:]), ALU.mult).then_inc(t_ready[2], 1)
                dve.wait_ge(t_ready[2], g + (2 * GROUPS + 1))
                dve.wait_ge(product[4], g + 1)
                dve.wait_ge(out_stored, g * 16)
                nc.vector.tensor_tensor(A[:], D, x_group(g), ALU.add).then_inc(product_read[4], 1)
                dve.wait_ge(product_read[4], g + 1)
                for j in range(GROUP):
                    last = nc.vector.bn_stats(stats[:, j, :], A[:, j, :])
                step(last)
                dve.sem_inc(gate["dve"], 1)
                for j in range(GROUP):
                    last = nc.vector.bn_aggr(mv[:, j, :], stats[:, j, :])
                step(last)
                nc.vector.tensor_scalar(var[:], mv[:, :, 1], EPS, None, ALU.add).then_inc(var_ready[5], 1)
                step(nc.vector.tensor_tensor(A[:], A[:], along(mv[:, :, 0]), ALU.subtract))
                dve.wait_ge(sd_ready[5], g + 1)
                step(nc.vector.reciprocal(rstd[:], sd[:]))
                nc.vector.tensor_tensor(A[:], A[:], along(rstd[:]), ALU.mult).then_inc(t_ready[4], 1)
                dve.wait_ge(t_ready[4], g + 1)
                step.leave(GROUPS)

        @block.tensor
        def _(pe):
            mm = nc.tensor.matmul

            pe.wait_ge(setup_dloc, 1)
            half_c = CHUNKS // 2
            for z in range(2):
                last = mm(bank(z)[:, 0:half_c], ones[0:1, :], firstF[0:1, z * half_c:(z + 1) * half_c],
                          start=True, stop=True)
            last.then_inc(setup_bc, 1)
            pe.wait_ge(setup_dloc, 2)
            for a in range(-(-CHUNKS // P)):
                n = min(P, CHUNKS - a * P)
                nc.tensor.transpose(bank(2, 2)[0:n, a * P:(a + 1) * P], dloc[:, a * P:a * P + n], ident[:])
                last = nc.tensor.transpose(bank(4, 2)[0:n, a * P:(a + 1) * P], srcF[:, a * P:a * P + n], ident[:])
            last.then_inc(setup_tr, 1)
            pe.wait_ge(setup_ev, 4)

            def sums(k):
                with pe.Fori(0, ITERATIONS) as i:
                    for b in range(2):
                        if k == 2:
                            pe.wait_ge(srow_in[b], i * 16 + 16)
                            for q in range(2):
                                if b == 1 or q == 1:
                                    pe.wait_ge(eq_made, i * 4 + (2 * b + q - 1))
                                else:
                                    pe.wait_ge(eq_made, i * 4)
                                mm(bank(4 + q), ones[0:1, :], srow[b][0:1, q * 512:(q + 1) * 512],
                                   start=True, stop=True).then_inc(src_bc, 1)
                        rows = Gw[b] if k == 0 else G[b]
                        pe.wait_ge(onehot[k][b], i + 1)
                        pe.wait_ge(added[k][b], i)
                        if k == 0:
                            for j in range(HALF):
                                mm(bank(4 + 2 * b, 2)[0:1, j * P:(j + 1) * P], ones[:, 0:1], O[b][:, j, :],
                                   start=True, stop=True)
                            pe.wait_ge(scaled[b], i + 1)
                        else:
                            pe.wait_ge(gathered[k][b], i * (16 * HALF) + 16 * HALF)
                        for j in range(HALF):
                            last = mm(bank(2 * b, 2)[:, j * P:(j + 1) * P], rows[:, j, :], O[b][:, j, :],
                                      start=True, stop=True)
                        last.then_inc(summed[k][b], 1)

            def dense(s, weight, g):
                pe.wait_ge(acc_staged[s], g + 1)
                pe.wait_ge(product_read[s], g)
                for j in range(GROUP):
                    last = mm(bank(0, 2)[:, j * P:(j + 1) * P], stage[:, j * P:(j + 1) * P], weight[:],
                              start=True, stop=True)
                last.then_inc(product[s], 1)

            def turn(s, tile, ready, n, at=2):
                for j in range(GROUP):
                    last = nc.tensor.transpose(bank(at, 2)[:, j * P:(j + 1) * P], tile[:, j, :], ident[:])
                return last

            def skewed(s, weight, tail):
                dense(s, weight, 0)
                with pe.Fori(0, GROUPS - 1) as g:
                    dense(s, weight, g + 1)
                    tail(g)
                tail(GROUPS - 1)

            def tail_t(s):
                def tail(g):
                    pe.wait_ge(t_ready[s], g + 1)
                    pe.wait_ge(acc_set[s], g)
                    turn(s, T, None, g).then_inc(turned[s], 1)
                return tail

            def tail_pq(g):
                tail_t(2)(g)
                pe.wait_ge(acc_set[2], g + 1)
                pe.wait_ge(pq_ready, g)
                for j in range(GROUP):
                    last = mm(bank(4, 4)[:, j * 256:(j + 1) * 256], XT[:, j * P:(j + 1) * P],
                              EW1[:, 1:3, :].rearrange("p a b -> p (a b)"), start=True, stop=True)
                last.then_inc(pq_product, 1)

            sums(0)
            skewed(0, W0, tail_t(0))
            sums(1)
            skewed(1, W1, tail_t(1))
            sums(2)
            skewed(2, W2, tail_pq)

            pe.wait_ge(pq_ready, GROUPS)

            def turn_edges(i, b, q, t, par):
                pe.wait_ge(e_loaded[b], i * 32 + 32)
                if not (type(t) is int and t < 1):
                    pe.wait_ge(ot_made, t)
                if not (type(t) is int and t < 2):
                    pe.wait_ge(et_ready, t - 1)
                mm(bank(0), ones_bf[0:1, :], drow[b][0:1, q * 512:(q + 1) * 512], start=True, stop=True)
                for j in range(BATCH):
                    last = nc.tensor.transpose(bank(1 if par == 0 else 7)[:, j * P:(j + 1) * P],
                                               Gw[b][:, q * BATCH + j, :], ident[:])
                last.then_inc(e_turned, 1)
                if q == 1:
                    e_used_at = e_used[b]
                    pe.wait_ge(e_turned, t + 1)
                    pe.sem_inc(e_used_at, 1)

            def first_product(i, b, q, t, par):
                pe.wait_ge(et_ready, t + 1)
                pe.wait_ge(ot_made, t + 1)
                pe.wait_ge(gathered[3][b], i * (16 * HALF) + 16 * HALF)
                pe.wait_ge(q_loaded[b], i * (16 * HALF) + 16 * HALF)
                if not (type(t) is int and t < 2):
                    pe.wait_ge(h1_ready, t - 1)
                for j in range(BATCH):
                    to = bank(2 + par)[:, j * P:(j + 1) * P]
                    mm(to, EW1[:, 0, :], ET[par][:, j, :], start=True, stop=False)
                    mm(to, G[b][:, q * BATCH + j, :], ident[:], start=False, stop=False)
                    last = mm(to, Win[b][:, q * BATCH + j, :], OT[par][:, j, :], start=False, stop=True)
                last.then_inc(h1_product, 1)
                if q == 1:
                    pe.wait_ge(h1_product, t + 1)
                    pe.sem_inc(g_used[b], 1)

            def second_product(t, par):
                pe.wait_ge(h1_ready, t + 1)
                if not (type(t) is int and t < 1):
                    pe.wait_ge(h2_ready, t)
                for j in range(BATCH):
                    to = bank(4)[:, j * P:(j + 1) * P]
                    mm(to, ones[0:1, :], eb2[:], start=True, stop=False)
                    last = mm(to, H1[par][:, j, :], EW2[:], start=False, stop=True)
                last.then_inc(h2_product, 1)

            def window_sums(i, b, q, t, par):
                pe.wait_ge(h2_ready, t + 1)
                pe.wait_ge(o_made, i * 2 + (b + 1))
                if not (type(t) is int and t < 2):
                    pe.wait_ge(e_added, t - 1)
                for j in range(BATCH):
                    last = mm(bank(5 + par)[:, j * P:(j + 1) * P], H2[par][:, j, :], O[b][:, q * BATCH + j, :],
                              start=True, stop=True)
                last.then_inc(e_summed, 1)

            def edge_iteration(i, start, end):
                for s in range(4):
                    t = i * 4 + s
                    if s < 3:
                        turn_edges(i, (s + 1) // 2, (s + 1) % 2, t + 1, (s + 1) % 2)
                    elif not end:
                        turn_edges(i + 1, 0, 0, t + 1, 0)
                    first_product(i, s // 2, s % 2, t, s % 2)
                    if not (start and s == 0):
                        second_product(t - 1, (s + 1) % 2)
                    if s >= 2:
                        window_sums(i, (s - 2) // 2, s % 2, t - 2, s % 2)
                    elif not start:
                        window_sums(i - 1, 1, s % 2, t - 2, s % 2)

            turn_edges(0, 0, 0, 0, 0)
            edge_iteration(0, True, False)
            with pe.Fori(1, ITERATIONS - 1) as i:
                edge_iteration(i, False, False)
            edge_iteration(ITERATIONS - 1, False, True)
            second_product(STEPS - 1, 1)
            window_sums(ITERATIONS - 1, 1, 0, STEPS - 2, 0)
            window_sums(ITERATIONS - 1, 1, 1, STEPS - 1, 1)

            def tail_mlp(g):
                pe.wait_ge(t_ready[2], g + (GROUPS + 1))
                turn(3, V, None, g).then_inc(turned[3], 1)
                pe.wait_ge(acc_set[3], g + 1)
                for h in range(4):
                    for z in range(2):
                        if h == 0:
                            pe.wait_ge(hid_ready, g * 8)
                        else:
                            pe.wait_ge(hid_ready, g * 8 + (2 * h + z - 1))
                        mm(bank(4 + z)[:, 0:SPAN // 2], EWd1[:, h * P:(h + 1) * P],
                           XT[:, z * (SPAN // 2):(z + 1) * (SPAN // 2)], start=True, stop=True
                           ).then_inc(hid_product, 1)
                pe.wait_ge(hid_ready, g * 8 + 8)
                pe.wait_ge(ffn_read, g)
                for j in range(GROUP):
                    for h in range(4):
                        last = mm(bank(6, 2)[:, j * P:(j + 1) * P], HD[:, h, j * P:(j + 1) * P], EWd2[:, h, :],
                                  start=(h == 0), stop=(h == 3))
                last.then_inc(ffn_product, 1)

            skewed(3, EW3, tail_mlp)

            def last_bc(i, b, q, t):
                pe.wait_ge(l_rows[b], i * 32 + 32)
                if not (type(t) is int and t < 1):
                    pe.wait_ge(l_eq, t)
                mm(bank(0), ones_bf[0:1, :], drow[b][0:1, q * 512:(q + 1) * 512], start=True, stop=True)
                mm(bank(1), ones[0:1, :], srow[b][0:1, q * 512:(q + 1) * 512], start=True, stop=True
                   ).then_inc(l_bc, 1)
                if q == 1:
                    pe.wait_ge(l_bc, t + 1)
                    pe.sem_inc(rows_used[b], 1)

            def last_rows(i, b, q, t, par):
                pe.wait_ge(l_ot, t + 1)
                pe.wait_ge(l_win[b], i * (16 * HALF) + 16 * HALF)
                if not (type(t) is int and t < 2):
                    pe.wait_ge(m_ready, t - 1)
                for j in range(BATCH):
                    last = mm(bank(2 + par)[:, j * P:(j + 1) * P], OT[par][:, j, :], Win[b][:, q * BATCH + j, :],
                              start=True, stop=True)
                last.then_inc(m_product, 1)
                if q == 1:
                    pe.wait_ge(m_product, t + 1)
                    pe.sem_inc(win_used[b], 1)

            def last_merge(t, par):
                pe.wait_ge(m_ready, t + 1)
                pe.wait_ge(l_eq, t + 1)
                if not (type(t) is int and t < 2):
                    pe.wait_ge(r_ready, t - 1)
                for j in range(BATCH):
                    last = mm(bank(4 + 2 * par, 2)[:, j * 256:j * 256 + ROW], ET[par][:, j, :], Mw[par][:, j, :],
                              start=True, stop=True)
                last.then_inc(r_product, 1)

            def last_iteration(i, start, end):
                for s in range(4):
                    t = i * 4 + s
                    if s < 3:
                        last_bc(i, (s + 1) // 2, (s + 1) % 2, t + 1)
                    elif not end:
                        last_bc(i + 1, 0, 0, t + 1)
                    last_rows(i, s // 2, s % 2, t, s % 2)
                    if not (start and s == 0):
                        last_merge(t - 1, (s + 1) % 2)

            last_bc(0, 0, 0, 0)
            last_iteration(0, True, False)
            with pe.Fori(1, ITERATIONS - 1) as i:
                last_iteration(i, False, False)
            last_iteration(ITERATIONS - 1, False, True)
            last_merge(STEPS - 1, 1)

            with pe.Fori(0, GROUPS) as g:
                pe.wait_ge(t_ready[2], g + (2 * GROUPS + 1))
                pe.wait_ge(acc_set[4], g)
                for j in range(GROUP):
                    nc.tensor.transpose(bank(2, 2)[:, j * P:(j + 1) * P], T[:, j, :], ident[:])
                    last = nc.tensor.transpose(bank(4, 2)[:, j * P:(j + 1) * P], TX[:, j, :], ident[:])
                last.then_inc(turned[4], 1)
                pe.wait_ge(acc_set[4], g + 1)
                pe.wait_ge(product_read[4], g)
                for j in range(GROUP):
                    mm(bank(0, 2)[:, j * P:(j + 1) * P], XT[:, j * P:(j + 1) * P], WL[:, 0, :], start=True, stop=False)
                    last = mm(bank(0, 2)[:, j * P:(j + 1) * P], HT[:, j * P:(j + 1) * P], WL[:, 1, :],
                              start=False, stop=True)
                last.then_inc(product[4], 1)


def kernel(**inputs):
    import numpy as np
    import concourse.bacc as bacc
    from concourse.bass_utils import run_bass_kernel_spmd

    a = {k: np.asarray(v) for k, v in inputs.items()}
    pad_e = EDGES - N_EDGES
    phantom = (N_NODES + np.arange(pad_e) * (NODES - N_NODES) // pad_e).astype(np.int32)
    dst = np.concatenate([a["dst"].astype(np.int32), phantom]).reshape(CHUNKS, P)
    src = np.concatenate([a["src"].astype(np.int32), phantom]).reshape(CHUNKS, P)
    weight = np.concatenate([a["edge_weight"], np.zeros(pad_e, np.float32)]).reshape(CHUNKS, P)
    arrays = {
        "x": np.concatenate([a["x"], np.zeros((NODES - N_NODES, P), np.float32)]),
        "edge_attr": np.concatenate([a["edge_attr_128"], np.zeros((pad_e, P), np.float32)]),
        "first_dst": np.ascontiguousarray(dst[:, 0:1].T),
        "dst_t": np.ascontiguousarray(dst.T), "src_t": np.ascontiguousarray(src.T),
        "weight_t": np.ascontiguousarray(weight.T),
        "w0_t": np.ascontiguousarray(a["L0_gnn_W"].T),
        "w1": a["L1_gnn_W1"], "w2": a["L1_gnn_W2"],
        "e_w1": a["L2_gnn_W1"], "e_w2": a["L2_gnn_W2"], "e_w3": a["L2_gnn_W3"],
        "e_wd1": a["L2_gnn_Wd1"], "e_wd2": a["L2_gnn_Wd2"], "w_last": a["L3_gnn_W"],
        "row_vectors": np.stack([a["L0_gnn_b"], a["L1_gnn_b1"], a["L1_gnn_b2"], a["L2_gnn_b3"], a["L2_gnn_bd2"],
                                 a["L2_gnn_g1"], a["L2_gnn_beta1"], a["L2_gnn_g2"], a["L2_gnn_beta2"],
                                 a["L2_gnn_b2"]]),
        "e_b1": a["L2_gnn_b1"].reshape(P, 1),
        "e_bd1": np.ascontiguousarray(a["L2_gnn_bd1"].reshape(4, P).T),
    }
    nc = bacc.Bacc("TRN2", target_bir_lowering=False, num_devices=1)
    feeds, args = {}, []
    for name, value in arrays.items():
        feeds[f"in_{name}"] = np.ascontiguousarray(value)
        args.append(nc.dram_tensor(f"in_{name}", value.shape, mybir.dt.from_np(value.dtype),
                                   kind="ExternalInput").ap())
    args.append(nc.dram_tensor("out_x", (NODES, P), mybir.dt.float32, kind="ExternalOutput").ap())
    gnn_program(nc, *args)
    r = run_bass_kernel_spmd(nc, [feeds], core_ids=[0])
    return r.results[0]["out_x"][:N_NODES]
```

```python
import concourse.bass as bass
from concourse import mybir
from contextlib import ExitStack

P = 128
N_NODES = 6250
N_EDGES = 106250
BLOCKS = -(-N_NODES // P)
NODES = BLOCKS * P
GROUP = 7
GROUPS = BLOCKS // GROUP
SPAN = GROUP * P
HALF = 8
BATCH = 4
ITERATIONS = -(-N_EDGES // (P * HALF * 2))
CHUNKS = ITERATIONS * HALF * 2
EDGES = CHUNKS * P
CHUNKS_AHEAD = CHUNKS + 2 * HALF
STEPS = CHUNKS // BATCH
WIDE = NODES + P
ROW = P + 1
EPS = 1e-5
TABLES = BATCH
ZERO_PARTS = 10
ZERO_COLS = WIDE * ROW // P // ZERO_PARTS


def gnn_program(nc, x, edge_attr, first_dst, dst_t, src_t, weight_t, w0_t, w1, w2, e_w1, e_w2, e_w3,
                e_wd1, e_wd2, w_last, row_vectors, e_b1, e_b2, e_bd1, out):
    f32, bf16, i32, u32 = mybir.dt.float32, mybir.dt.bfloat16, mybir.dt.int32, mybir.dt.uint32
    ALU = mybir.AluOpType
    ACT = mybir.ActivationFunctionType
    AX = mybir.AxisListType
    ds = bass.ds

    with ExitStack() as ctx:
        def sb(name, shape, dt=f32):
            return ctx.enter_context(nc.sbuf_tensor(name, shape, dt))

        def sem(name):
            return ctx.enter_context(nc.semaphore(name))

        def dram(name, shape, dt=f32):
            return nc.dram_tensor(name, shape, dt, kind="Internal").ap()

        table1 = dram("table1", [NODES, P])
        table2 = dram("table2", [NODES, P])
        table_p = dram("table_p", [NODES, P])
        table_q = dram("table_q", [WIDE, P])
        table_x = dram("table_x", [WIDE, P])
        edge_rows3 = dram("edge_rows3", [3, CHUNKS, P], bf16)
        count_row_d = dram("count_row_d", [NODES])
        sums_d = [dram(f"sums{t}", [WIDE, ROW]) for t in range(TABLES)]

        X = sb("X", [P, BLOCKS, P])
        acc = sb("acc", [P, WIDE])
        srcI = sb("srcI", [P, CHUNKS], i32)
        srcF = sb("srcF", [P, CHUNKS])
        dloc = sb("dloc", [P, CHUNKS_AHEAD])
        wt = sb("wt", [P, CHUNKS])
        first = sb("first", [1, CHUNKS], i32)
        rowI = sb("rowI", [P, CHUNKS], i32)
        dstI = rowI
        W0 = sb("W0", [P, P])
        W1 = sb("W1", [P, P])
        W2 = sb("W2", [P, P])
        EW1 = sb("EW1", [P, 3, P])
        EW2 = sb("EW2", [P, P])
        EW3 = sb("EW3", [P, P])
        EWd1 = sb("EWd1", [P, 4 * P])
        EWd2 = sb("EWd2", [P, 4, P])
        WL = sb("WL", [P, 2, P])
        vec = sb("vec", [P, 10, P])
        eb2 = sb("eb2", [P, 1])
        minus_b2 = sb("minus_b2", [P, P])
        eb1 = sb("eb1", [P, 1])
        ebd1 = sb("ebd1", [P, 4])
        iota = sb("iota", [P, P])
        iopI = sb("iopI", [P, 1], i32)
        iop = sb("iop", [P, 1])
        trash = sb("trash", [P, 1])
        ident = sb("ident", [P, P])
        lower = sb("lower", [P, P])
        ones = sb("ones", [P, P])
        pick_dst = sb("pick_dst", [3, P], bf16)
        pick_src = sb("pick_src", [3, P], bf16)
        zeros = sb("zeros", [P, ZERO_COLS])
        count_row = sb("count_row", [1, WIDE])
        count = sb("count", [P, BLOCKS])
        dinv = sb("dinv", [P, BLOCKS])
        cinv = sb("cinv", [P, BLOCKS])
        space = sb("space", [P, 8 * HALF * P])

        def in_space(at, *shape):
            n = shape[0] * shape[1]
            return space[:, at:at + n].rearrange("p (a b) -> p a b", b=shape[1])

        G, Gw, O, Win = ([in_space((2 * n + b) * HALF * P, HALF, P) for b in range(2)] for n in range(4))
        turned_rows = [space[:, (6 * HALF * P + n * SPAN // 2):(6 * HALF * P + (n + 1) * SPAN // 2)].bitcast(bf16)
                       .rearrange("p (a b) -> p a b", b=P) for n in range(3)]
        PQ = in_space(0, GROUP, 2 * P)
        HD = in_space(0, 4, SPAN)
        SG = in_space(0, TABLES, GROUP * ROW)
        S1 = acc[:, 0:GROUP * ROW]
        IX = [sb(f"IX{b}", [P, HALF], i32) for b in range(2)]
        rows3 = [sb(f"rows3{b}", [3, HALF * P], bf16) for b in range(2)]
        OT = [sb(f"OT{b}", [P, BATCH, P]) for b in range(2)]
        ET = [sb(f"ET{b}", [P, BATCH, P]) for b in range(2)]
        H1 = [sb(f"H1{b}", [P, BATCH, P]) for b in range(2)]
        H2 = [sb(f"H2{b}", [P, BATCH, P]) for b in range(2)]
        eq = H2[0]
        iotaI = H2[1][:, 0, :].bitcast(i32)
        Mw = [sb(f"Mw{b}", [P, BATCH, ROW]) for b in range(2)]
        R = [sb(f"R{b}", [P, BATCH, ROW]) for b in range(2)]
        RX = [sb(f"RX{b}", [P, BATCH], i32) for b in range(2)]
        stage = sb("stage", [P, SPAN])
        firstF = stage[0:1, 0:CHUNKS]
        A = sb("A", [P, GROUP, P])
        V = sb("V", [P, GROUP, P])
        T = sb("T", [P, GROUP, P])
        TX = sb("TX", [P, GROUP, P])
        XT = sb("XT", [P, SPAN])
        HT = V[:].rearrange("p a b -> p (a b)")
        repeats = HT[:, 0:CHUNKS]
        low_bits, high_bits = XT[:, 0:CHUNKS], HT[:, 0:CHUNKS]
        dstF = TX[:].rearrange("p a b -> p (a b)")[:, 0:CHUNKS]
        stats = sb("stats", [P, GROUP, 6])
        mv = sb("mv", [P, GROUP, 2])
        var = sb("var", [P, GROUP])
        degree = sb("degree", [P, GROUP])
        per_degree = sb("per_degree", [P, GROUP])
        minus_half = sb("minus_half", [P, BLOCKS])
        B = sb("B", [P, GROUP, P])
        rstd = sb("rstd", [P, GROUP])
        ps = ctx.enter_context(nc.psum_tensor("ps", [P, 8, 512], f32))

        N_LOADS = 17 + 10

        loaded = sem("loaded")
        made_iota = sem("made_iota")
        dve_step = sem("dve_step")
        setup_bc = sem("setup_bc")
        setup_dloc = sem("setup_dloc")
        setup_tr = sem("setup_tr")
        setup_ev = sem("setup_ev")
        rows_out = sem("rows_out")
        zeroed = sem("zeroed")
        gate = {n: sem(f"gate_{n}") for n in ("pool", "act", "dve", "sp")}
        staged_idx = sem("staged_idx")
        gathered = [[sem(f"gathered{k}{b}") for b in range(2)] for k in range(4)]
        onehot = [[sem(f"onehot{k}{b}") for b in range(2)] for k in range(3)]
        summed = [[sem(f"summed{k}{b}") for b in range(2)] for k in range(3)]
        added = [[sem(f"added{k}{b}") for b in range(2)] for k in range(3)]
        scaled = [sem(f"scaled{b}") for b in range(2)]
        srow_in = [sem(f"srow_in{b}") for b in range(2)]
        src_bc = sem("src_bc")
        eq_made = [sem(f"eq_made{q}") for q in range(2)]
        row_index = sem("row_index")
        acc_clear = sem("acc_clear")
        counted = sem("counted")
        count_out = sem("count_out")
        count_in = sem("count_in")
        deg_made = sem("deg_made")
        dinv_made = sem("dinv_made")
        acc_staged = [sem(f"acc_staged{s}") for s in range(4)]
        product = [sem(f"product{s}") for s in range(5)]
        product_read = [sem(f"product_read{s}") for s in range(5)]
        var_ready = [sem(f"var_ready{s}") for s in range(6)]
        rstd_ready = [sem(f"rstd_ready{s}") for s in range(6)]
        t_ready = [sem(f"t_ready{s}") for s in range(5)]
        t_stored = [sem(f"t_stored{s}") for s in range(5)]
        turned = [sem(f"turned{s}") for s in range(5)]
        acc_set = [sem(f"acc_set{s}") for s in range(5)]
        pq_product = sem("pq_product")
        pq_ready = sem("pq_ready")
        pq_stored = sem("pq_stored")
        pad_stored = sem("pad_stored")
        e_loaded = [sem(f"e_loaded{b}") for b in range(2)]
        q_loaded = [sem(f"q_loaded{b}") for b in range(2)]
        e_used = [sem(f"e_used{b}") for b in range(2)]
        g_used = [sem(f"g_used{b}") for b in range(2)]
        e_turned = sem("e_turned")
        et_ready = sem("et_ready")
        ot_made = sem("ot_made")
        o_made = sem("o_made")
        h1_product = sem("h1_product")
        h1_ready = sem("h1_ready")
        h2_product = sem("h2_product")
        h2_ready = sem("h2_ready")
        e_summed = sem("e_summed")
        e_added = sem("e_added")
        hid_product = sem("hid_product")
        hid_ready = sem("hid_ready")
        ffn_product = sem("ffn_product")
        ffn_read = sem("ffn_read")
        v_ready = sem("v_ready")
        tx_ready = sem("tx_ready")
        l_rows = [sem(f"l_rows{b}") for b in range(2)]
        l_win = [sem(f"l_win{b}") for b in range(2)]
        rows_used = [sem(f"rows_used{b}") for b in range(2)]
        win_used = [sem(f"win_used{b}") for b in range(2)]
        l_bc = sem("l_bc")
        l_ot = sem("l_ot")
        l_eq = sem("l_eq")
        m_product = sem("m_product")
        m_ready = sem("m_ready")
        r_product = sem("r_product")
        r_ready = sem("r_ready")
        scattered = [sem(f"scattered{j}") for j in range(TABLES)]
        r_free = sem("r_free")
        sums_in = sem("sums_in")
        sums_used = sem("sums_used")
        out_stored = sem("out_stored")

        block = ctx.enter_context(nc.Block())

        def bank(n, k=1):
            return ps[:, n:n + k, :].rearrange("p a b -> p (a b)")

        def blocks_of(ap, width=P, n=GROUP):
            return ap[:, 0:n * width].rearrange("p (a b) -> p a b", b=width)

        def along(ap, n=P):
            return ap.unsqueeze(2).broadcast_to([ap.shape[0], ap.shape[1], n])

        def over(ap, n):
            return ap.unsqueeze(1).broadcast_to([ap.shape[0], n, ap.shape[1]])

        def acc_group(g):
            return acc[:, ds(g * SPAN, SPAN)]

        def x_group(g):
            return X[:, ds(g * GROUP, GROUP), :]

        def window_starts(eng, kind, c, n):
            return [nc.values_load(first[0:1, ds(c + j, 1)], engines=[kind], min_val=0, max_val=NODES - 1,
                                   skip_runtime_bounds_check_because="destinations are node numbers")
                    for j in range(n)]

        class Steps:

            def __init__(self, eng):
                self.eng, self.base, self.k, self.i, self.per = eng, 0, 0, None, 0

            def __call__(self, ins):
                self.go(ins)
                self.wait(0)

            def go(self, ins):
                ins.then_inc(dve_step, 1)
                self.k += 1

            def wait(self, back):
                n = self.base + self.k - back
                self.eng.wait_ge(dve_step, n if self.i is None else self.i * self.per + n)

            def enter(self, i, per, start=0):
                self.base += self.k - start * per
                self.i, self.per, self.k = i, per, 0
                self.start = start

            def leave(self, end):
                assert self.k == self.per, (self.k, self.per)
                self.base += end * self.per
                self.i, self.k = None, 0

        @block.sync
        def _(sp):
            SP = mybir.EngineType.SP
            for tile, source in [
                (dstI[:], dst_t), (first[:], first_dst), (srcI[:], src_t), (wt[:], weight_t),
                (W0[:], w0_t), (W1[:], w1), (W2[:], w2),
                (EW1[:], e_w1.rearrange("(a p) n -> p a n", p=P)), (EW2[:], e_w2), (EW3[:], e_w3),
                (EWd1[:], e_wd1), (EWd2[:], e_wd2.rearrange("(a p) n -> p a n", p=P)),
                (WL[:], w_last.rearrange("(a p) n -> p a n", p=P)),
                (eb1[:], e_b1), (ebd1[:], e_bd1),
                (eb2[:], e_b2),
                (X[:], x.rearrange("(b p) d -> p b d", p=P)),
            ]:
                sp.dma_start(tile, source).then_inc(loaded, 16)
            for v in range(10):
                sp.dma_start(vec[:, v, :], row_vectors[v:v + 1, :].broadcast_to([P, P])).then_inc(loaded, 16)
            sp.wait_ge(setup_ev, 6)
            full = CHUNKS // P
            rest = CHUNKS - full * P
            for n in range(3):
                sp.dma_start(edge_rows3[n, 0:full * P, :].rearrange("(a p) e -> p a e", p=P),
                             turned_rows[n][:, 0:full, :]).then_inc(rows_out, 16)
                sp.dma_start(edge_rows3[n, full * P:CHUNKS, :], turned_rows[n][0:rest, full, :]
                             ).then_inc(rows_out, 16)
            sp.wait_ge(made_iota, 5)
            sp.dma_start(table_q[NODES:WIDE, :], zeros[:, 0:P]).then_inc(pad_stored, 16)
            sp.dma_start(table_x[NODES:WIDE, :], zeros[:, 0:P]).then_inc(pad_stored, 16)

            sp.wait_ge(counted, 1)
            sp.dma_start(count_row_d.rearrange("(o n) -> o n", o=1), count_row[0:1, 0:NODES]).then_inc(count_out, 16)
            sp.wait_ge(count_out, 16)
            sp.dma_start(count[:], count_row_d.rearrange("(b p) -> p b", p=P), allow_slow_non_contiguous=True).then_inc(count_in, 16)

            def store_groups(s, table, ready):
                rows = table[0:NODES, :].rearrange("(b p) d -> p b d", p=P)
                with sp.Fori(0, GROUPS) as g:
                    sp.wait_ge(ready, g + 1)
                    sp.dma_start(rows[:, ds(g * GROUP, GROUP), :], T[:]).then_inc(t_stored[s], 16)

            store_groups(0, table1, t_ready[0])
            store_groups(1, table2, t_ready[1])

            def load_rows3(b, c, done):
                sp.dma_start(rows3[b][:], edge_rows3[:, ds(c, HALF), :].rearrange("r c e -> r (c e)")
                             ).then_inc(done, 16)

            sp.wait_ge(rows_out, 96)
            for b in range(2):
                load_rows3(b, b * HALF, srow_in[b])
            with sp.Fori(1, ITERATIONS) as i:
                for b in range(2):
                    sp.wait_ge(src_bc, i * 4 + (2 * b - 2))
                    load_rows3(b, i * 2 * HALF + b * HALF, srow_in[b])

            rows_p = table_p.rearrange("(b p) d -> p b d", p=P)
            rows_q = table_q[0:NODES, :].rearrange("(b p) d -> p b d", p=P)
            with sp.Fori(0, GROUPS) as g:
                sp.wait_ge(pq_ready, g + 1)
                sp.dma_start(rows_p[:, ds(g * GROUP, GROUP), :], PQ[:, :, 0:P]).then_inc(pq_stored, 16)
                sp.dma_start(rows_q[:, ds(g * GROUP, GROUP), :], PQ[:, :, P:2 * P]).then_inc(pq_stored, 16)

            sp.wait_ge(pq_stored, 32 * GROUPS)
            sp.wait_ge(pad_stored, 32)
            edge_rows = edge_attr.rearrange("(c e) d -> e c d", e=P)
            with sp.Fori(0, ITERATIONS) as i:
                for b in range(2):
                    c = i * 2 * HALF + b * HALF
                    sp.wait_ge(e_used[b], i)
                    sp.dma_start(Gw[b], edge_rows[:, ds(c, HALF), :]).then_inc(e_loaded[b], 16)
                    load_rows3(b, c, e_loaded[b])
                    sp.wait_ge(g_used[b], i)
                    sp.sem_inc(gate["sp"], 1)
                    for j, n0 in enumerate(window_starts(sp, SP, c, HALF)):
                        sp.dma_start(Win[b][:, j, :], table_q[ds(n0, P), :]).then_inc(q_loaded[b], 16)

            store_groups(3, table_x, t_ready[3])
            sp.wait_ge(t_stored[3], 16 * GROUPS)
            with sp.Fori(0, ITERATIONS) as i:
                for b in range(2):
                    c = i * 2 * HALF + b * HALF
                    sp.wait_ge(rows_used[b], i)
                    load_rows3(b, c, l_rows[b])
                    sp.wait_ge(win_used[b], i)
                    sp.sem_inc(gate["sp"], 1)
                    for j, n0 in enumerate(window_starts(sp, SP, c, HALF)):
                        sp.dma_start(Win[b][:, j, :], table_x[ds(n0, P), :]).then_inc(l_win[b], 16)

            for j in range(TABLES):
                sp.wait_ge(scattered[j], 16 * STEPS)
            def load_sums(g):
                sp.wait_ge(sums_used, g)
                for t in range(TABLES):
                    rows = sums_d[t][0:NODES, :].rearrange("(b p) d -> p b d", p=P)
                    sp.dma_start(SG[:, t, :].rearrange("p (a b) -> p a b", b=ROW),
                                 rows[:, ds(g * GROUP, GROUP), :]).then_inc(sums_in, 16)

            def store_out(g):
                sp.wait_ge(t_ready[4], g + 1)
                sp.dma_start(out.rearrange("(b p) d -> p b d", p=P)[:, ds(g * GROUP, GROUP), :], A[:]
                             ).then_inc(out_stored, 16)

            load_sums(0)
            with sp.Fori(0, GROUPS - 1) as g:
                load_sums(g + 1)
                store_out(g)
            store_out(GROUPS - 1)
            sp.wait_ge(out_stored, 16 * GROUPS)

        @block.gpsimd
        def _(pool):
            nc.gpsimd.iota(iotaI, pattern=[[1, P]], base=0, channel_multiplier=0).then_inc(made_iota, 1)
            nc.gpsimd.iota(iopI[:], pattern=[[0, 1]], base=0, channel_multiplier=1).then_inc(made_iota, 1)
            nc.gpsimd.memset(zeros[:], 0.0).then_inc(made_iota, 1)
            nc.gpsimd.memset(acc[:], 0.0).then_inc(made_iota, 1)
            nc.gpsimd.memset(count_row[:], 0.0).then_inc(made_iota, 1)
            nc.gpsimd.memset(minus_half[:], -0.5).then_inc(made_iota, 1)
            pool.wait_ge(made_iota, 6)
            pool.wait_ge(loaded, 16 * N_LOADS)

            def gathers(k, table, used):
                with pool.Fori(0, ITERATIONS) as i:
                    for b in range(2):
                        pool.wait_ge(gathered[k][b], i * (16 * HALF))
                        pool.wait_ge(used[b], i)
                        pool.sem_inc(gate["pool"], 1)
                        nc.gpsimd.tensor_copy(IX[b][:], srcI[:, ds(i * 2 * HALF + b * HALF, HALF)]
                                              ).then_inc(staged_idx, 1)
                        pool.wait_ge(staged_idx, i * 2 + (k * 2 * ITERATIONS + b + 1))
                        pool.sem_inc(gate["pool"], 1)
                        for j in range(HALF):
                            pool.indirect_dma_start(
                                G[b][:, j, :], None, table,
                                bass.IndirectOffsetOnAxis(ap=IX[b][:, j:j + 1].bitcast(u32), axis=0),
                            ).then_inc(gathered[k][b], 16)

            def stage_group(s, g):
                pool.wait_ge(product[s], g)
                pool.sem_inc(gate["pool"], 1)
                nc.gpsimd.tensor_copy(stage[:], acc_group(g)).then_inc(acc_staged[s], 1)

            def rsqrt(s, n):
                pool.wait_ge(var_ready[s], n + 1)
                nc.gpsimd.tensor_tensor(rstd[:], var[:], minus_half[:, 0:GROUP], ALU.pow).then_inc(rstd_ready[s], 1)

            def stage_groups(s):
                stage_group(s, 0)
                with pool.Fori(0, GROUPS - 1) as g:
                    stage_group(s, g + 1)
                    if s != 1:
                        rsqrt(s, g)
                if s != 1:
                    rsqrt(s, GROUPS - 1)

            gathers(0, x, scaled)
            for b in range(2):
                pool.wait_ge(added[0][b], ITERATIONS)
            stage_group(0, 0)
            pool.wait_ge(deg_made, 1)
            nc.gpsimd.tensor_tensor(dinv[:], dinv[:], minus_half[:], ALU.pow).then_inc(dinv_made, 1)
            with pool.Fori(0, GROUPS - 1) as g:
                stage_group(0, g + 1)
                rsqrt(0, g)
            rsqrt(0, GROUPS - 1)
            pool.wait_ge(t_stored[0], 16 * GROUPS)
            gathers(1, table1, summed[1])
            for b in range(2):
                pool.wait_ge(added[1][b], ITERATIONS)
            stage_groups(1)
            pool.wait_ge(t_stored[1], 16 * GROUPS)
            gathers(2, table2, summed[2])
            for b in range(2):
                pool.wait_ge(added[2][b], ITERATIONS)
            stage_groups(2)
            pool.wait_ge(acc_staged[2], GROUPS)
            nc.gpsimd.memset(acc[:], 0.0).then_inc(acc_clear, 1)
            pool.wait_ge(pq_stored, 32 * GROUPS)
            gathers(3, table_p, g_used)
            pool.wait_ge(e_added, STEPS)
            stage_group(3, 0)
            stage_group(3, 1)
            rsqrt(3, 0)

            def mlp_part(g):
                rsqrt(3, g + 1)
                rsqrt(4, g * 2)
                rsqrt(4, g * 2 + 1)

            with pool.Fori(0, GROUPS - 2) as g:
                stage_group(3, g + 2)
                mlp_part(g)
            mlp_part(GROUPS - 2)
            rsqrt(4, 2 * GROUPS - 2)
            rsqrt(4, 2 * GROUPS - 1)

            pool.wait_ge(zeroed, 16 * TABLES * ZERO_PARTS)
            pool.wait_ge(row_index, 1)
            with pool.Fori(0, ITERATIONS * 2) as i:
                for q in range(2):
                    t = i * 2 + q
                    nc.gpsimd.tensor_copy(RX[q][:], rowI[:, ds(i * HALF + q * BATCH, BATCH)]).then_inc(staged_idx, 1)
                    pool.wait_ge(staged_idx, t + (8 * ITERATIONS + 1))
                    pool.wait_ge(r_ready, t + 1)
                    for j in range(BATCH):
                        pool.wait_ge(scattered[j], t * 16)
                        pool.sem_inc(gate["pool"], 1)
                        pool.indirect_dma_start(
                            sums_d[j],
                            bass.IndirectOffsetOnAxis(ap=RX[q][:, j:j + 1].bitcast(u32), axis=0),
                            R[q][:, j, :], None, compute_op=ALU.add,
                        ).then_inc(scattered[j], 16)
                    pool.sem_inc(r_free, 1)
            with pool.Fori(0, GROUPS) as g:
                rsqrt(5, g)

        @block.scalar
        def _(act):
            act.wait_ge(made_iota, 3)
            act.wait_ge(loaded, 16 * N_LOADS)

            with act.Fori(0, ITERATIONS) as i:
                for b in range(2):
                    act.wait_ge(gathered[0][b], i * (16 * HALF) + 16 * HALF)
                    act.wait_ge(summed[0][b], i)
                    act.sem_inc(gate["act"], 1)
                    for j in range(HALF):
                        last = nc.scalar.activation(Gw[b][:, j, :], G[b][:, j, :], ACT.Copy,
                                                    scale=wt[:, ds(i * 2 * HALF + b * HALF + j, 1)])
                    last.then_inc(scaled[b], 1)

            def set_acc(s, g):
                act.wait_ge(turned[s], g + 1)
                act.sem_inc(gate["act"], 1)
                nc.scalar.copy(acc_group(g), bank(2, 2)[:, 0:SPAN]).then_inc(acc_set[s], 1)

            with act.Fori(0, GROUPS) as g:
                set_acc(0, g)

            for t in range(TABLES):
                parts = sums_d[t].rearrange("n d -> (n d)").rearrange("(a p f) -> a p f", p=P, f=ZERO_COLS)
                for a in range(ZERO_PARTS):
                    act.dma_start(parts[a], zeros[:]).then_inc(zeroed, 16)

            with act.Fori(0, GROUPS) as g:
                set_acc(1, g)

            with act.Fori(0, GROUPS) as g:
                act.wait_ge(turned[2], g + 1)
                act.wait_ge(pq_product, g)
                nc.scalar.copy(XT[:], bank(2, 2)[:, 0:SPAN]).then_inc(acc_set[2], 1)
                act.wait_ge(pq_product, g + 1)
                act.wait_ge(pq_stored, g * 32)
                nc.scalar.copy(PQ, bank(4, 4)[:, 0:GROUP * 2 * P].rearrange("p (a b) -> p a b", b=2 * P)
                               ).then_inc(pq_ready, 1)

            def evacuate_e(t, par):
                act.wait_ge(e_turned, t + 1)
                if not (type(t) is int and t < 2):
                    act.wait_ge(h1_product, t - 1)
                nc.scalar.copy(ET[par][:].rearrange("p a b -> p (a b)"), bank(1 if par == 0 else 7)
                               ).then_inc(et_ready, 1)

            def relu_h1(t, par):
                act.wait_ge(h1_product, t + 1)
                if not (type(t) is int and t < 2):
                    act.wait_ge(h2_product, t - 1)
                nc.scalar.activation(H1[par][:].rearrange("p a b -> p (a b)"), bank(2 + par), ACT.Relu,
                                     bias=eb1[:, 0:1]).then_inc(h1_ready, 1)

            def edge_iteration(i, start, end):
                for s in range(4):
                    t = i * 4 + s
                    if not (end and s == 3):
                        evacuate_e(t + 1, (s + 1) % 2)
                    relu_h1(t, s % 2)

            evacuate_e(0, 0)
            edge_iteration(0, True, False)
            with act.Fori(1, ITERATIONS - 1) as i:
                edge_iteration(i, False, False)
            edge_iteration(ITERATIONS - 1, False, True)

            with act.Fori(0, GROUPS) as g:
                act.wait_ge(turned[3], g + 1)
                act.wait_ge(ffn_product, g)
                nc.scalar.copy(XT[:], bank(2, 2)[:, 0:SPAN]).then_inc(acc_set[3], 1)
                for h in range(4):
                    for z in range(2):
                        act.wait_ge(hid_product, g * 8 + (2 * h + z + 1))
                        nc.scalar.activation(HD[:, h, z * (SPAN // 2):(z + 1) * (SPAN // 2)],
                                             bank(4 + z)[:, 0:SPAN // 2], ACT.Relu,
                                             bias=ebd1[:, h:h + 1]).then_inc(hid_ready, 1)

            def weigh(i, q, b, t, par):
                act.wait_ge(m_product, t + 1)
                if not (type(t) is int and t < 2):
                    act.wait_ge(r_product, t - 1)
                act.sem_inc(gate["act"], 1)
                c = i * 2 * HALF + (b * HALF + q * BATCH)
                for j in range(BATCH):
                    nc.scalar.activation(Mw[par][:, j, 0:P], bank(2 + par)[:, j * P:(j + 1) * P], ACT.Copy,
                                         scale=wt[:, ds(c + j, 1)])
                nc.scalar.copy(Mw[par][:, :, P:ROW], wt[:, ds(c, BATCH)].unsqueeze(2)).then_inc(m_ready, 1)

            def evacuate_r(i, q, b, t, par):
                act.wait_ge(r_product, t + 1)
                if not (type(t) is int and t < 1):
                    act.wait_ge(r_free, t)
                nc.scalar.copy(R[par][:], bank(4, 2).rearrange("p (a b) -> p a b", b=256)[:, :, 0:ROW]
                               ).then_inc(r_ready, 1)

            def last_iteration(i, start):
                for s in range(4):
                    t = i * 4 + s
                    weigh(i, s % 2, s // 2, t, s % 2)
                    if s == 0:
                        if not start:
                            evacuate_r(i - 1, 1, 1, t - 1, 1)
                    else:
                        evacuate_r(i, (s - 1) % 2, (s - 1) // 2, t - 1, (s - 1) % 2)

            last_iteration(0, True)
            with act.Fori(1, ITERATIONS) as i:
                last_iteration(i, False)
            evacuate_r(ITERATIONS - 1, 1, 1, STEPS - 1, 1)

            with act.Fori(0, GROUPS) as g:
                act.wait_ge(turned[4], g + 1)
                act.wait_ge(product[4], g)
                nc.scalar.copy(XT[:], bank(2, 2)[:, 0:SPAN])
                nc.scalar.copy(HT[:], bank(4, 2)[:, 0:SPAN]).then_inc(acc_set[4], 1)

        @block.vector
        def _(dve):
            DVE = mybir.EngineType.DVE
            step = Steps(dve)
            VB0, VB1, VB2, VB3, VBD2, VG1, VBE1, VG2, VBE2, VB2E = range(10)

            dve.wait_ge(made_iota, 2)
            nc.vector.memset(ones[:], 1.0)
            nc.vector.memset(dloc[:, CHUNKS:CHUNKS_AHEAD], 0.0)
            nc.vector.tensor_copy(iota[:], iotaI)
            step(nc.vector.tensor_copy(iop[:], iopI[:]))
            nc.vector.tensor_scalar(pick_dst[:], iop[0:3, 0:1].broadcast_to([3, P]), 0.0, None,
                                    ALU.is_equal)
            nc.vector.tensor_scalar(pick_src[:], iop[0:3, 0:1].broadcast_to([3, P]), 0.0, None,
                                    ALU.is_gt)
            nc.vector.tensor_scalar(trash[:], iop[:], float(NODES), None, ALU.add)
            nc.vector.tensor_scalar(ident[:], iota[:], iop[:, 0:1], None, ALU.is_equal)
            nc.vector.tensor_scalar(lower[:], iota[:], iop[:, 0:1], None, ALU.is_lt)
            dve.wait_ge(loaded, 16 * N_LOADS)
            nc.vector.tensor_copy(srcF[:], srcI[:])
            step(nc.vector.tensor_scalar(low_bits.bitcast(i32), srcI[:], P - 1, None, ALU.bitwise_and))
            step(nc.vector.tensor_copy(high_bits, low_bits.bitcast(i32)))
            step(nc.vector.tensor_copy(low_bits, high_bits))
            step(nc.vector.tensor_tensor(high_bits, srcF[:], low_bits, ALU.subtract))
            nc.vector.tensor_scalar(minus_b2[:], vec[:, VB2E, :], -1.0, None, ALU.mult)
            step(nc.vector.tensor_copy(T[:, 0, :], eb2[:, 0:1].broadcast_to([P, P])))
            nc.vector.tensor_copy(dloc[:, 0:CHUNKS], dstI[:])
            nc.vector.tensor_copy(firstF, first[:]).then_inc(setup_dloc, 1)
            dve.wait_ge(setup_dloc, 1)
            dve.wait_ge(setup_bc, 1)
            half_c = CHUNKS // 2
            for z in range(2):
                last = nc.vector.tensor_tensor(dloc[:, z * half_c:(z + 1) * half_c],
                                               dloc[:, z * half_c:(z + 1) * half_c],
                                               bank(z)[:, 0:half_c], ALU.subtract)
            last.then_inc(setup_dloc, 1)
            dve.wait_ge(setup_tr, 1)
            full, rest = CHUNKS // P, CHUNKS % P
            for tile, at in zip(turned_rows, (2, 4, 6)):
                nc.vector.tensor_copy(tile[:, 0:full, :], blocks_of(bank(at, 2), P, full)).then_inc(setup_ev, 1)
                nc.vector.tensor_copy(tile[0:rest, full, :], blocks_of(bank(at, 2))[0:rest, full, :]
                                      ).then_inc(setup_ev, 1)
            dve.wait_ge(setup_dloc, 2)
            step(nc.vector.tensor_tensor(vec[:, VB3, :], vec[:, VB3, :], bank(1)[:, 0:P], ALU.add))

            def make_onehot(k, i, b):
                nc.vector.tensor_tensor(O[b], over(iota[:], HALF),
                                        along(dloc[:, ds(i * 2 * HALF + b * HALF, HALF)]),
                                        ALU.is_equal).then_inc(onehot[k][b], 1)

            def sums(k):
                per = 2 * (HALF * (2 if k == 0 else 1) + (6 if k == 2 else 0))
                for b in range(2):
                    make_onehot(k, 0, b)
                with dve.Fori(0, ITERATIONS) as i:
                    step.enter(i, per)
                    for b in range(2):
                        c = i * 2 * HALF + b * HALF
                        dve.wait_ge(summed[k][b], i + 1)
                        starts = window_starts(dve, DVE, c, HALF)

                        def add(j):
                            step.go(nc.vector.tensor_tensor(acc[:, ds(starts[j], P)], acc[:, ds(starts[j], P)],
                                                            bank(2 * b, 2)[:, j * P:(j + 1) * P], ALU.add))

                        def add_count(j):
                            step.go(nc.vector.tensor_tensor(count_row[0:1, ds(starts[j], P)],
                                                            count_row[0:1, ds(starts[j], P)],
                                                            bank(4 + 2 * b, 2)[0:1, j * P:(j + 1) * P], ALU.add))

                        for j in range(HALF):
                            if k == 2 and j < 6:
                                q = j // 3
                                if j % 3 == 0:
                                    dve.wait_ge(src_bc, i * 4 + (2 * b + q + 1))
                                    step.go(nc.vector.tensor_tensor(
                                        eq[:], blocks_of(bank(4 + q), P, BATCH),
                                        along(srcF[:, ds(c + q * BATCH, BATCH)]), ALU.is_equal))
                                elif j % 3 == 1:
                                    step.go(nc.vector.tensor_tensor(eq[:], eq[:], over(lower[:], BATCH), ALU.mult))
                                else:
                                    step.go(nc.vector.tensor_reduce(repeats[:, ds(c + q * BATCH, BATCH)], eq[:],
                                                                    axis=AX.X, op=ALU.add))
                                step.wait(1)
                            add(j)
                            if k == 0:
                                step.wait(1)
                                add_count(j)
                            step.wait(1 if k == 0 or (k == 2 and j < 5) else 0)
                            if k == 2 and j in (0, 3):
                                dve.sem_inc(eq_made[j // 3], 1)
                        if k == 0:
                            step.wait(0)
                        dve.sem_inc(added[k][b], 1)
                        make_onehot(k, i + 1, b)
                    step.leave(ITERATIONS)

            def norm(s, g, count_of=None, A=A, source=None):
                source = A[:] if source is None else source
                for j in range(GROUP):
                    last = nc.vector.bn_stats(stats[:, j, :], source[:, j, :])
                step(last)
                dve.sem_inc(gate["dve"], 1)
                for j in range(GROUP):
                    last = nc.vector.bn_aggr(mv[:, j, :], stats[:, j, :])
                step(last)
                nc.vector.tensor_scalar(var[:], mv[:, :, 1], EPS, None, ALU.add).then_inc(var_ready[s], 1)
                step(nc.vector.tensor_tensor(A[:], source, along(mv[:, :, 0]), ALU.subtract))
                dve.wait_ge(rstd_ready[s], count_of if count_of is not None else g + 1)
                step(nc.vector.tensor_tensor(A[:], A[:], along(rstd[:]), ALU.mult))

            NORM = 4
            D = blocks_of(bank(0, 2))

            dve.wait_ge(made_iota, 5)
            sums(0)
            dve.sem_inc(counted, 1)
            dve.wait_ge(count_in, 16)
            step(nc.vector.reciprocal(cinv[:], count[:]))
            nc.vector.tensor_scalar(dinv[:], count[:], 1.0, None, ALU.add).then_inc(deg_made, 1)
            dve.wait_ge(dinv_made, 1)

            def wait_t_free(s, g):
                dve.wait_ge(t_stored[s], g * 16)
                dve.wait_ge(turned[s], g)

            with dve.Fori(0, GROUPS) as g:
                step.enter(g, 1 + NORM)
                dve.wait_ge(t_ready[0], g)
                dve.wait_ge(product[0], g + 1)
                nc.vector.scalar_tensor_tensor(A[:], D, 0.0, x_group(g), ALU.max, ALU.add
                                               ).then_inc(product_read[0], 1)
                dve.wait_ge(product_read[0], g + 1)
                norm(0, g)
                dve.sem_inc(gate["dve"], 1)
                step(nc.vector.tensor_copy(x_group(g), A[:]))
                wait_t_free(0, g)
                nc.vector.tensor_tensor(T[:], A[:], along(dinv[:, ds(g * GROUP, GROUP)]), ALU.mult
                                        ).then_inc(t_ready[0], 1)
                step.leave(GROUPS)

            dve.wait_ge(acc_set[0], GROUPS)
            sums(1)
            with dve.Fori(0, GROUPS) as g:
                step.enter(g, 1)
                dve.wait_ge(t_ready[1], g)
                dve.wait_ge(product[1], g + 1)
                nc.vector.tensor_tensor(A[:], D, along(dinv[:, ds(g * GROUP, GROUP)]), ALU.mult
                                        ).then_inc(product_read[1], 1)
                dve.wait_ge(product_read[1], g + 1)
                step(nc.vector.tensor_tensor(A[:], A[:], over(vec[:, VB1, :], GROUP), ALU.add))
                wait_t_free(1, g)
                nc.vector.scalar_tensor_tensor(T[:], A[:], 0.0, along(dinv[:, ds(g * GROUP, GROUP)]),
                                               ALU.max, ALU.mult).then_inc(t_ready[1], 1)
                step.leave(GROUPS)
            dve.wait_ge(acc_set[1], GROUPS)
            sums(2)
            step(nc.vector.tensor_scalar(repeats, repeats, 1.0, None, ALU.min))
            step(nc.vector.tensor_scalar(dstF, srcF[:], -1.0, trash[:, 0:1], ALU.mult, ALU.add))
            step(nc.vector.tensor_tensor(dstF, dstF, repeats, ALU.mult))
            nc.vector.tensor_tensor(rowI[:], dstF, srcF[:], ALU.add).then_inc(row_index, 1)

            with dve.Fori(0, GROUPS) as g:
                step.enter(g, 3 + NORM)
                dve.wait_ge(t_ready[2], g)
                dve.wait_ge(product[2], g + 1)
                nc.vector.tensor_tensor(A[:], D, along(dinv[:, ds(g * GROUP, GROUP)]), ALU.mult
                                        ).then_inc(product_read[2], 1)
                dve.wait_ge(product_read[2], g + 1)
                step(nc.vector.tensor_tensor(A[:], A[:], over(vec[:, VB2, :], GROUP), ALU.add))
                step(nc.vector.tensor_tensor(A[:], A[:], x_group(g), ALU.add))
                norm(2, g)
                dve.sem_inc(gate["dve"], 1)
                step(nc.vector.tensor_copy(x_group(g), A[:]))
                dve.wait_ge(turned[2], g)
                nc.vector.tensor_copy(T[:], A[:]).then_inc(t_ready[2], 1)
                step.leave(GROUPS)

            dve.wait_ge(acc_clear, 1)

            def spread(t, par):
                dve.wait_ge(e_turned, t + 1)
                if not (type(t) is int and t < 2):
                    dve.wait_ge(h1_product, t - 1)
                nc.vector.tensor_scalar(OT[par][:].rearrange("p a b -> p (a b)"), bank(0), iop[:, 0:1], None,
                                        ALU.is_equal).then_inc(ot_made, 1)

            def edge_onehot(i, b, t):
                if not (type(t) is int and t < 4):
                    dve.wait_ge(e_summed, t - 2)
                nc.vector.tensor_tensor(O[b][:], over(iota[:], HALF),
                                        along(dloc[:, ds(i * 2 * HALF + b * HALF, HALF)]),
                                        ALU.is_equal).then_inc(o_made, 1)

            def max_h2(t, par):
                dve.wait_ge(h2_product, t + 1)
                if not (type(t) is int and t < 2):
                    dve.wait_ge(e_summed, t - 1)
                nc.vector.tensor_tensor(H2[par][:], blocks_of(bank(4), P, BATCH), over(minus_b2[:], BATCH),
                                        ALU.max).then_inc(h2_ready, 1)

            def edge_adds(i, s, t):
                dve.wait_ge(e_summed, t + 1)
                starts = window_starts(dve, DVE, i * 2 * HALF + s * BATCH, BATCH)
                for j, n0 in enumerate(starts):
                    step.wait(0)
                    step.go(nc.vector.tensor_tensor(acc[:, ds(n0, P)], acc[:, ds(n0, P)],
                                                    bank(5 + s % 2)[:, j * P:(j + 1) * P], ALU.add))
                    yield
                step.wait(0)
                dve.sem_inc(e_added, 1)

            def edge_iteration(i, start, end):
                for s in range(4):
                    t = i * 4 + s
                    if s == 3:
                        adds = edge_adds(i, 0, t - 3)
                    elif not start:
                        adds = edge_adds(i - 1, s + 1, t - 3)
                    else:
                        adds = iter(())
                    next(adds, None)
                    if not (end and s == 3):
                        spread(t + 1, (s + 1) % 2)
                    next(adds, None)
                    if s % 2 == 0:
                        edge_onehot(i, s // 2, t)
                        next(adds, None)
                    if not (start and s == 0):
                        max_h2(t - 1, (s + 1) % 2)
                    for _ in adds:
                        pass

            spread(0, 0)
            edge_iteration(0, True, False)
            with dve.Fori(1, ITERATIONS - 1) as i:
                step.enter(i, 4 * BATCH, 1)
                edge_iteration(i, False, False)
                step.leave(ITERATIONS - 1)
            edge_iteration(ITERATIONS - 1, False, True)
            max_h2(STEPS - 1, 1)
            for s in (1, 2, 3):
                for _ in edge_adds(ITERATIONS - 1, s, STEPS - 4 + s):
                    pass

            def before_mlp(g):
                dve.wait_ge(product[3], g + 1)
                nc.vector.tensor_tensor(A[:], D, along(cinv[:, ds(g * GROUP, GROUP)]), ALU.mult
                                        ).then_inc(product_read[3], 1)
                dve.wait_ge(product_read[3], g + 1)
                step(nc.vector.tensor_tensor(A[:], A[:], over(vec[:, VB3, :], GROUP), ALU.add))
                step(nc.vector.tensor_tensor(A[:], A[:], x_group(g), ALU.add))
                norm(3, g)
                step(nc.vector.tensor_tensor(A[:], A[:], over(vec[:, VG1, :], GROUP), ALU.mult))
                dve.wait_ge(turned[3], g)
                nc.vector.tensor_tensor(V[:], A[:], over(vec[:, VBE1, :], GROUP), ALU.add).then_inc(v_ready, 1)
                dve.wait_ge(v_ready, g + 1)

            def behind_mlp(g):
                dve.wait_ge(ffn_product, g + 1)
                norm(4, g, g * 2 + 1, B, blocks_of(bank(6, 2)))
                dve.sem_inc(ffn_read, 1)
                step(nc.vector.tensor_tensor(B[:], B[:], over(vec[:, VG2, :], GROUP), ALU.mult))
                step(nc.vector.tensor_tensor(B[:], B[:], over(vec[:, VBE2, :], GROUP), ALU.add))
                step(nc.vector.tensor_tensor(B[:], B[:], x_group(g), ALU.add))
                norm(4, g, g * 2 + 2, B)
                dve.sem_inc(gate["dve"], 1)
                step(nc.vector.tensor_copy(x_group(g), B[:]))
                dve.wait_ge(t_stored[3], g * 16)
                nc.vector.tensor_copy(T[:], B[:]).then_inc(t_ready[3], 1)
                dve.wait_ge(t_ready[3], g + 1)

            before_mlp(0)
            with dve.Fori(0, GROUPS - 1) as g:
                step.enter(g, 7 + 3 * NORM)
                before_mlp(g + 1)
                behind_mlp(g)
                step.leave(GROUPS - 1)
            behind_mlp(GROUPS - 1)

            def last_spread(i, s, t, par):
                dve.wait_ge(l_bc, t + 1)
                if not (type(t) is int and t < 2):
                    dve.wait_ge(m_product, t - 1)
                nc.vector.tensor_scalar(OT[par][:].rearrange("p a b -> p (a b)"), bank(6 * par), iop[:, 0:1], None,
                                        ALU.is_equal).then_inc(l_ot, 1)
                if not (type(t) is int and t < 2):
                    dve.wait_ge(r_product, t - 1)
                nc.vector.tensor_tensor(ET[par][:], blocks_of(bank(6 * par + 1), P, BATCH),
                                        along(srcF[:, ds(i * 2 * HALF + s * BATCH, BATCH)]), ALU.is_equal
                                        ).then_inc(l_eq, 1)

            for s in range(4):
                last_spread(0, s, s, s % 2)
            with dve.Fori(1, ITERATIONS) as i:
                for s in range(4):
                    last_spread(i, s, i * 4 + s, s % 2)

            def mean_rows(g):
                dve.wait_ge(sums_in, g * (16 * TABLES) + 16 * TABLES)
                nc.vector.tensor_reduce(S1, SG.rearrange("p t n -> p n t"), axis=AX.X, op=ALU.add
                                        ).then_inc(sums_used, 1)
                dve.wait_ge(sums_used, g + 1)
                S1v = S1.rearrange("p (a b) -> p a b", b=ROW)
                step(nc.vector.tensor_scalar(degree[:], S1v[:, :, P], 1e-6, None, ALU.add))
                step(nc.vector.reciprocal(per_degree[:], degree[:]))
                dve.wait_ge(turned[4], g)
                dve.sem_inc(gate["dve"], 1)
                nc.vector.tensor_copy(T[:], x_group(g))
                nc.vector.tensor_tensor(TX[:], S1v[:, :, 0:P], along(per_degree[:]), ALU.mult).then_inc(tx_ready, 1)
                dve.wait_ge(tx_ready, g + 1)

            def result(g):
                dve.wait_ge(product[4], g + 1)
                dve.wait_ge(out_stored, g * 16)
                nc.vector.tensor_tensor(A[:], D, x_group(g), ALU.add).then_inc(product_read[4], 1)
                dve.wait_ge(product_read[4], g + 1)
                norm(5, g)
                dve.sem_inc(t_ready[4], 1)

            mean_rows(0)
            with dve.Fori(0, GROUPS - 1) as g:
                step.enter(g, 2 + NORM)
                mean_rows(g + 1)
                result(g)
                step.leave(GROUPS - 1)
            result(GROUPS - 1)

        @block.tensor
        def _(pe):
            mm = nc.tensor.matmul

            pe.wait_ge(setup_dloc, 1)
            half_c = CHUNKS // 2
            for z in range(2):
                last = mm(bank(z)[:, 0:half_c], ones[0:1, :], firstF[0:1, z * half_c:(z + 1) * half_c],
                          start=True, stop=True)
            last.then_inc(setup_bc, 1)
            pe.wait_ge(setup_dloc, 2)
            mm(bank(1)[:, 0:P], T[:, 0, :], EW3[:], start=True, stop=True)
            for a in range(-(-CHUNKS // P)):
                n = min(P, CHUNKS - a * P)
                for source, at in ((dloc[:], 2), (low_bits, 4), (high_bits, 6)):
                    last = nc.tensor.transpose(bank(at, 2)[0:n, a * P:(a + 1) * P], source[:, a * P:a * P + n],
                                               ident[:])
            last.then_inc(setup_tr, 1)
            pe.wait_ge(setup_ev, 6)

            def sums(k):
                with pe.Fori(0, ITERATIONS) as i:
                    for b in range(2):
                        if k == 2:
                            pe.wait_ge(srow_in[b], i * 16 + 16)
                            for q in range(2):
                                pe.wait_ge(eq_made[q], i * 2 + b)
                                mm(bank(4 + q), pick_src[:], rows3[b][:, q * 512:(q + 1) * 512],
                                   start=True, stop=True).then_inc(src_bc, 1)
                        rows = Gw[b] if k == 0 else G[b]
                        pe.wait_ge(onehot[k][b], i + 1)
                        pe.wait_ge(added[k][b], i)
                        if k == 0:
                            for j in range(HALF):
                                mm(bank(4 + 2 * b, 2)[0:1, j * P:(j + 1) * P], ones[:, 0:1], O[b][:, j, :],
                                   start=True, stop=True)
                            pe.wait_ge(scaled[b], i + 1)
                        else:
                            pe.wait_ge(gathered[k][b], i * (16 * HALF) + 16 * HALF)
                        for j in range(HALF):
                            last = mm(bank(2 * b, 2)[:, j * P:(j + 1) * P], rows[:, j, :], O[b][:, j, :],
                                      start=True, stop=True)
                        last.then_inc(summed[k][b], 1)

            def dense(s, weight, g):
                pe.wait_ge(acc_staged[s], g + 1)
                pe.wait_ge(product_read[s], g)
                for j in range(GROUP):
                    if s == 0:
                        mm(bank(0, 2)[:, j * P:(j + 1) * P], ones[0:1, :], vec[0:1, 0, :], start=True, stop=False)
                    last = mm(bank(0, 2)[:, j * P:(j + 1) * P], stage[:, j * P:(j + 1) * P], weight[:],
                              start=(s != 0), stop=True)
                last.then_inc(product[s], 1)

            def turn(s, tile, ready, n, at=2):
                for j in range(GROUP):
                    last = nc.tensor.transpose(bank(at, 2)[:, j * P:(j + 1) * P], tile[:, j, :], ident[:])
                return last

            def skewed(s, weight, tail):
                dense(s, weight, 0)
                with pe.Fori(0, GROUPS - 1) as g:
                    dense(s, weight, g + 1)
                    tail(g)
                tail(GROUPS - 1)

            def tail_t(s):
                def tail(g):
                    pe.wait_ge(t_ready[s], g + 1)
                    pe.wait_ge(acc_set[s], g)
                    turn(s, T, None, g).then_inc(turned[s], 1)
                return tail

            def tail_pq(g):
                tail_t(2)(g)
                pe.wait_ge(acc_set[2], g + 1)
                pe.wait_ge(pq_ready, g)
                for j in range(GROUP):
                    last = mm(bank(4, 4)[:, j * 256:(j + 1) * 256], XT[:, j * P:(j + 1) * P],
                              EW1[:, 1:3, :].rearrange("p a b -> p (a b)"), start=True, stop=True)
                last.then_inc(pq_product, 1)

            sums(0)
            skewed(0, W0, tail_t(0))
            sums(1)
            skewed(1, W1, tail_t(1))
            sums(2)
            skewed(2, W2, tail_pq)

            pe.wait_ge(pq_ready, GROUPS)

            def turn_edges(i, b, q, t, par):
                pe.wait_ge(e_loaded[b], i * 32 + 32)
                if not (type(t) is int and t < 1):
                    pe.wait_ge(ot_made, t)
                if not (type(t) is int and t < 2):
                    pe.wait_ge(et_ready, t - 1)
                mm(bank(0), pick_dst[:], rows3[b][:, q * 512:(q + 1) * 512], start=True, stop=True)
                for j in range(BATCH):
                    last = nc.tensor.transpose(bank(1 if par == 0 else 7)[:, j * P:(j + 1) * P],
                                               Gw[b][:, q * BATCH + j, :], ident[:])
                last.then_inc(e_turned, 1)
                if q == 1:
                    e_used_at = e_used[b]
                    pe.wait_ge(e_turned, t + 1)
                    pe.sem_inc(e_used_at, 1)

            def first_product(i, b, q, t, par):
                pe.wait_ge(et_ready, t + 1)
                pe.wait_ge(ot_made, t + 1)
                pe.wait_ge(gathered[3][b], i * (16 * HALF) + 16 * HALF)
                pe.wait_ge(q_loaded[b], i * (16 * HALF) + 16 * HALF)
                if not (type(t) is int and t < 2):
                    pe.wait_ge(h1_ready, t - 1)
                for j in range(BATCH):
                    to = bank(2 + par)[:, j * P:(j + 1) * P]
                    mm(to, EW1[:, 0, :], ET[par][:, j, :], start=True, stop=False)
                    mm(to, G[b][:, q * BATCH + j, :], ident[:], start=False, stop=False)
                    last = mm(to, Win[b][:, q * BATCH + j, :], OT[par][:, j, :], start=False, stop=True)
                last.then_inc(h1_product, 1)
                if q == 1:
                    pe.wait_ge(h1_product, t + 1)
                    pe.sem_inc(g_used[b], 1)

            def second_product(t, par):
                pe.wait_ge(h1_ready, t + 1)
                if not (type(t) is int and t < 1):
                    pe.wait_ge(h2_ready, t)
                for j in range(BATCH):
                    to = bank(4)[:, j * P:(j + 1) * P]
                    last = mm(to, H1[par][:, j, :], EW2[:], start=True, stop=True)
                last.then_inc(h2_product, 1)

            def window_sums(i, b, q, t, par):
                pe.wait_ge(h2_ready, t + 1)
                pe.wait_ge(o_made, i * 2 + (b + 1))
                if not (type(t) is int and t < 2):
                    pe.wait_ge(e_added, t - 1)
                for j in range(BATCH):
                    last = mm(bank(5 + par)[:, j * P:(j + 1) * P], H2[par][:, j, :], O[b][:, q * BATCH + j, :],
                              start=True, stop=True)
                last.then_inc(e_summed, 1)

            def edge_iteration(i, start, end):
                for s in range(4):
                    t = i * 4 + s
                    if s < 3:
                        turn_edges(i, (s + 1) // 2, (s + 1) % 2, t + 1, (s + 1) % 2)
                    elif not end:
                        turn_edges(i + 1, 0, 0, t + 1, 0)
                    first_product(i, s // 2, s % 2, t, s % 2)
                    if not (start and s == 0):
                        second_product(t - 1, (s + 1) % 2)
                    if s >= 2:
                        window_sums(i, (s - 2) // 2, s % 2, t - 2, s % 2)
                    elif not start:
                        window_sums(i - 1, 1, s % 2, t - 2, s % 2)

            turn_edges(0, 0, 0, 0, 0)
            edge_iteration(0, True, False)
            with pe.Fori(1, ITERATIONS - 1) as i:
                edge_iteration(i, False, False)
            edge_iteration(ITERATIONS - 1, False, True)
            second_product(STEPS - 1, 1)
            window_sums(ITERATIONS - 1, 1, 0, STEPS - 2, 0)
            window_sums(ITERATIONS - 1, 1, 1, STEPS - 1, 1)

            def tail_mlp(g):
                pe.wait_ge(v_ready, g + 1)
                turn(3, V, None, g).then_inc(turned[3], 1)
                pe.wait_ge(acc_set[3], g + 1)
                for h in range(4):
                    for z in range(2):
                        if h == 0:
                            pe.wait_ge(hid_ready, g * 8)
                        else:
                            pe.wait_ge(hid_ready, g * 8 + (2 * h + z - 1))
                        mm(bank(4 + z)[:, 0:SPAN // 2], EWd1[:, h * P:(h + 1) * P],
                           XT[:, z * (SPAN // 2):(z + 1) * (SPAN // 2)], start=True, stop=True
                           ).then_inc(hid_product, 1)
                pe.wait_ge(hid_ready, g * 8 + 8)
                pe.wait_ge(ffn_read, g)
                for j in range(GROUP):
                    for h in range(4):
                        mm(bank(6, 2)[:, j * P:(j + 1) * P], HD[:, h, j * P:(j + 1) * P], EWd2[:, h, :],
                           start=(h == 0), stop=False)
                    mm(bank(6, 2)[:, j * P:(j + 1) * P], ones[0:1, :], vec[0:1, 4, :], start=False, stop=False)
                    last = mm(bank(6, 2)[:, j * P:(j + 1) * P], XT[:, j * P:(j + 1) * P], ident[:],
                              start=False, stop=True)
                last.then_inc(ffn_product, 1)

            skewed(3, EW3, tail_mlp)

            def last_bc(i, b, q, t):
                pe.wait_ge(l_rows[b], i * 16 + 16)
                if not (type(t) is int and t < 2):
                    pe.wait_ge(l_eq, t - 1)
                mm(bank(6 * q), pick_dst[:], rows3[b][:, q * 512:(q + 1) * 512], start=True, stop=True)
                mm(bank(6 * q + 1), pick_src[:], rows3[b][:, q * 512:(q + 1) * 512], start=True, stop=True
                   ).then_inc(l_bc, 1)
                if q == 1:
                    pe.wait_ge(l_bc, t + 1)
                    pe.sem_inc(rows_used[b], 1)

            def last_rows(i, b, q, t, par):
                pe.wait_ge(l_ot, t + 1)
                pe.wait_ge(l_win[b], i * (16 * HALF) + 16 * HALF)
                if not (type(t) is int and t < 2):
                    pe.wait_ge(m_ready, t - 1)
                for j in range(BATCH):
                    last = mm(bank(2 + par)[:, j * P:(j + 1) * P], OT[par][:, j, :], Win[b][:, q * BATCH + j, :],
                              start=True, stop=True)
                last.then_inc(m_product, 1)
                if q == 1:
                    pe.wait_ge(m_product, t + 1)
                    pe.sem_inc(win_used[b], 1)

            def last_merge(t, par):
                pe.wait_ge(m_ready, t + 1)
                pe.wait_ge(l_eq, t + 1)
                if not (type(t) is int and t < 1):
                    pe.wait_ge(r_ready, t)
                for j in range(BATCH):
                    last = mm(bank(4, 2)[:, j * 256:j * 256 + ROW], ET[par][:, j, :], Mw[par][:, j, :],
                              start=True, stop=True)
                last.then_inc(r_product, 1)

            def last_iteration(i, start, end):
                for s in range(4):
                    t = i * 4 + s
                    if s < 3:
                        last_bc(i, (s + 1) // 2, (s + 1) % 2, t + 1)
                    elif not end:
                        last_bc(i + 1, 0, 0, t + 1)
                    last_rows(i, s // 2, s % 2, t, s % 2)
                    if not (start and s == 0):
                        last_merge(t - 1, (s + 1) % 2)

            last_bc(0, 0, 0, 0)
            last_iteration(0, True, False)
            with pe.Fori(1, ITERATIONS - 1) as i:
                last_iteration(i, False, False)
            last_iteration(ITERATIONS - 1, False, True)
            last_merge(STEPS - 1, 1)

            def turn_last(g):
                pe.wait_ge(tx_ready, g + 1)
                pe.wait_ge(acc_set[4], g)
                for j in range(GROUP):
                    nc.tensor.transpose(bank(2, 2)[:, j * P:(j + 1) * P], T[:, j, :], ident[:])
                    last = nc.tensor.transpose(bank(4, 2)[:, j * P:(j + 1) * P], TX[:, j, :], ident[:])
                last.then_inc(turned[4], 1)

            with pe.Fori(0, GROUPS) as g:
                turn_last(g)
                pe.wait_ge(acc_set[4], g + 1)
                pe.wait_ge(product_read[4], g)
                for j in range(GROUP):
                    mm(bank(0, 2)[:, j * P:(j + 1) * P], XT[:, j * P:(j + 1) * P], WL[:, 0, :], start=True, stop=False)
                    last = mm(bank(0, 2)[:, j * P:(j + 1) * P], HT[:, j * P:(j + 1) * P], WL[:, 1, :],
                              start=False, stop=True)
                last.then_inc(product[4], 1)


def kernel(**inputs):
    import numpy as np
    import concourse.bacc as bacc
    from concourse.bass_utils import run_bass_kernel_spmd

    a = {k: np.asarray(v) for k, v in inputs.items()}
    pad_e = EDGES - N_EDGES
    phantom = (N_NODES + np.arange(pad_e) * (NODES - N_NODES) // pad_e).astype(np.int32)
    dst = np.concatenate([a["dst"].astype(np.int32), phantom]).reshape(CHUNKS, P)
    src = np.concatenate([a["src"].astype(np.int32), phantom]).reshape(CHUNKS, P)
    weight = np.concatenate([a["edge_weight"], np.zeros(pad_e, np.float32)]).reshape(CHUNKS, P)
    arrays = {
        "x": np.concatenate([a["x"], np.zeros((NODES - N_NODES, P), np.float32)]),
        "edge_attr": np.concatenate([a["edge_attr_128"], np.zeros((pad_e, P), np.float32)]),
        "first_dst": np.ascontiguousarray(dst[:, 0:1].T),
        "dst_t": np.ascontiguousarray(dst.T), "src_t": np.ascontiguousarray(src.T),
        "weight_t": np.ascontiguousarray(weight.T),
        "w0_t": np.ascontiguousarray(a["L0_gnn_W"].T),
        "w1": a["L1_gnn_W1"], "w2": a["L1_gnn_W2"],
        "e_w1": a["L2_gnn_W1"], "e_w2": a["L2_gnn_W2"], "e_w3": a["L2_gnn_W3"],
        "e_wd1": a["L2_gnn_Wd1"], "e_wd2": a["L2_gnn_Wd2"], "w_last": a["L3_gnn_W"],
        "row_vectors": np.stack([a["L0_gnn_b"], a["L1_gnn_b1"], a["L1_gnn_b2"], a["L2_gnn_b3"], a["L2_gnn_bd2"],
                                 a["L2_gnn_g1"], a["L2_gnn_beta1"], a["L2_gnn_g2"], a["L2_gnn_beta2"],
                                 a["L2_gnn_b2"]]),
        "e_b1": a["L2_gnn_b1"].reshape(P, 1),
        "e_b2": a["L2_gnn_b2"].reshape(P, 1),
        "e_bd1": np.ascontiguousarray(a["L2_gnn_bd1"].reshape(4, P).T),
    }
    nc = bacc.Bacc("TRN2", target_bir_lowering=False, num_devices=1)
    feeds, args = {}, []
    for name, value in arrays.items():
        feeds[f"in_{name}"] = np.ascontiguousarray(value)
        args.append(nc.dram_tensor(f"in_{name}", value.shape, mybir.dt.from_np(value.dtype),
                                   kind="ExternalInput").ap())
    args.append(nc.dram_tensor("out_x", (NODES, P), mybir.dt.float32, kind="ExternalOutput").ap())
    gnn_program(nc, *args)
    r = run_bass_kernel_spmd(nc, [feeds], core_ids=[0])
    return r.results[0]["out_x"][:N_NODES]
```

```python
import concourse.bass as bass
from concourse import mybir
from contextlib import ExitStack

P = 128
N_NODES = 6250
N_EDGES = 106250
BLOCKS = -(-N_NODES // P)
NODES = BLOCKS * P
GROUP = 7
GROUPS = BLOCKS // GROUP
SPAN = GROUP * P
HALF = 8
BATCH = 4
ITERATIONS = -(-N_EDGES // (P * HALF * 2))
CHUNKS = ITERATIONS * HALF * 2
EDGES = CHUNKS * P
CHUNKS_AHEAD = CHUNKS + 2 * HALF
STEPS = CHUNKS // BATCH
WIDE = NODES + P
ROW = P + 1
EPS = 1e-5
TABLES = BATCH
ZERO_PARTS = 10
ZERO_COLS = WIDE * ROW // P // ZERO_PARTS


def gnn_program(nc, x, edge_attr_t, first_dst, dst_t, src_t, weight_t, w0_t, w1, w2, e_w1, e_w2, e_w3,
                e_wd1, e_wd2, w_last, row_vectors, e_b1, e_b2, e_bd1, out):
    f32, bf16, i32, u32 = mybir.dt.float32, mybir.dt.bfloat16, mybir.dt.int32, mybir.dt.uint32
    ALU = mybir.AluOpType
    ACT = mybir.ActivationFunctionType
    AX = mybir.AxisListType
    ds = bass.ds

    with ExitStack() as ctx:
        def sb(name, shape, dt=f32):
            return ctx.enter_context(nc.sbuf_tensor(name, shape, dt))

        def sem(name):
            return ctx.enter_context(nc.semaphore(name))

        def dram(name, shape, dt=f32):
            return nc.dram_tensor(name, shape, dt, kind="Internal").ap()

        table1 = dram("table1", [NODES, P])
        table2 = dram("table2", [NODES, P])
        table_p = dram("table_p", [NODES, P])
        table_q = dram("table_q", [WIDE, P])
        table_x = dram("table_x", [WIDE, P])
        edge_rows3 = dram("edge_rows3", [3, CHUNKS, P], bf16)
        count_row_d = dram("count_row_d", [NODES])
        sums_d = [dram(f"sums{t}", [WIDE, ROW]) for t in range(TABLES)]

        X = sb("X", [P, BLOCKS, P])
        acc = sb("acc", [P, WIDE])
        srcI = sb("srcI", [P, CHUNKS_AHEAD], i32)
        srcF = sb("srcF", [P, CHUNKS])
        dloc = sb("dloc", [P, CHUNKS_AHEAD])
        wt = sb("wt", [P, CHUNKS])
        first = sb("first", [1, CHUNKS], i32)
        rowI = sb("rowI", [P, CHUNKS], i32)
        dstI = rowI
        W0 = sb("W0", [P, P])
        W1 = sb("W1", [P, P])
        W2 = sb("W2", [P, P])
        EW1 = sb("EW1", [P, 3, P])
        EW2 = sb("EW2", [P, P])
        EW3 = sb("EW3", [P, P])
        EWd1 = sb("EWd1", [P, 4 * P])
        EWd2 = sb("EWd2", [P, 4, P])
        WL = sb("WL", [P, 2, P])
        vec = sb("vec", [P, 10, P])
        eb2 = sb("eb2", [P, 1])
        minus_b2 = sb("minus_b2", [P, P])
        eb1 = sb("eb1", [P, 1])
        ebd1 = sb("ebd1", [P, 4])
        iota = sb("iota", [P, P])
        iopI = sb("iopI", [P, 1], i32)
        iop = sb("iop", [P, 1])
        trash = sb("trash", [P, 1])
        ident = sb("ident", [P, P])
        lower = sb("lower", [P, P])
        ones = sb("ones", [P, P])
        pick_dst = sb("pick_dst", [3, P], bf16)
        pick_src = sb("pick_src", [3, P], bf16)
        zeros = sb("zeros", [P, ZERO_COLS])
        count_row = sb("count_row", [1, WIDE])
        count = sb("count", [P, BLOCKS])
        dinv = sb("dinv", [P, BLOCKS])
        cinv = sb("cinv", [P, BLOCKS])
        space = sb("space", [P, 8 * HALF * P])

        def in_space(at, *shape):
            n = shape[0] * shape[1]
            return space[:, at:at + n].rearrange("p (a b) -> p a b", b=shape[1])

        G, Gw, O, Win = ([in_space((2 * n + b) * HALF * P, HALF, P) for b in range(2)] for n in range(4))
        turned_rows = [space[:, (6 * HALF * P + n * SPAN // 2):(6 * HALF * P + (n + 1) * SPAN // 2)].bitcast(bf16)
                       .rearrange("p (a b) -> p a b", b=P) for n in range(3)]
        PQ = in_space(0, GROUP, 2 * P)
        HD = in_space(0, 4, SPAN)
        SG = in_space(0, TABLES, GROUP * ROW)
        S1 = acc[:, 0:GROUP * ROW]
        IX = [sb(f"IX{b}", [P, HALF], i32) for b in range(2)]
        rows3 = [sb(f"rows3{b}", [3, HALF * P], bf16) for b in range(2)]
        OT = [sb(f"OT{b}", [P, BATCH, P]) for b in range(2)]
        ET = [sb(f"ET{b}", [P, BATCH, P]) for b in range(2)]
        H1 = [sb(f"H1{b}", [P, BATCH, P]) for b in range(2)]
        H2 = [sb(f"H2{b}", [P, BATCH, P]) for b in range(2)]
        eq = H2[0]
        iotaI = H2[1][:, 0, :].bitcast(i32)
        Mw = [sb(f"Mw{b}", [P, BATCH, ROW]) for b in range(2)]
        R = [sb(f"R{b}", [P, BATCH, ROW]) for b in range(2)]
        RX = [sb(f"RX{b}", [P, BATCH], i32) for b in range(2)]
        stage = sb("stage", [P, SPAN])
        firstF = stage[0:1, 0:CHUNKS]
        A = sb("A", [P, GROUP, P])
        V = sb("V", [P, GROUP, P])
        T = sb("T", [P, GROUP, P])
        TX = sb("TX", [P, GROUP, P])
        XT = sb("XT", [P, SPAN])
        HT = V[:].rearrange("p a b -> p (a b)")
        repeats = HT[:, 0:CHUNKS]
        low_bits, high_bits = XT[:, 0:CHUNKS], HT[:, 0:CHUNKS]
        dstF = TX[:].rearrange("p a b -> p (a b)")[:, 0:CHUNKS]
        stats = [sb(f"stats{n}", [P, GROUP, 6]) for n in range(2)]
        mv = [sb(f"mv{n}", [P, GROUP, 2]) for n in range(2)]
        var = [sb(f"var{n}", [P, GROUP]) for n in range(2)]
        rstd = [sb(f"rstd{n}", [P, GROUP]) for n in range(2)]
        minus_mean = sb("minus_mean", [P, GROUP])
        shift = sb("shift", [P, GROUP])
        degree = sb("degree", [P, GROUP])
        per_degree = sb("per_degree", [P, GROUP])
        minus_half = sb("minus_half", [P, BLOCKS])
        B = sb("B", [P, GROUP, P])
        ps = ctx.enter_context(nc.psum_tensor("ps", [P, 8, 512], f32))

        N_LOADS = 17 + 10

        loaded = sem("loaded")
        made_iota = sem("made_iota")
        dve_step = sem("dve_step")
        setup_bc = sem("setup_bc")
        setup_dloc = sem("setup_dloc")
        setup_tr = sem("setup_tr")
        setup_ev = sem("setup_ev")
        rows_out = sem("rows_out")
        zeroed = sem("zeroed")
        gate = {n: sem(f"gate_{n}") for n in ("pool", "act", "dve", "sp")}
        idx_ready = [[sem(f"idx_ready{k}{b}") for b in range(2)] for k in range(4)]
        gathered = [[sem(f"gathered{k}{b}") for b in range(2)] for k in range(4)]
        onehot = [[sem(f"onehot{k}{b}") for b in range(2)] for k in range(3)]
        summed = [[sem(f"summed{k}{b}") for b in range(2)] for k in range(3)]
        added = [[sem(f"added{k}{b}") for b in range(2)] for k in range(3)]
        scaled = [sem(f"scaled{b}") for b in range(2)]
        srow_in = [sem(f"srow_in{b}") for b in range(2)]
        src_bc = sem("src_bc")
        eq_made = [sem(f"eq_made{q}") for q in range(2)]
        row_index = sem("row_index")
        acc_clear = sem("acc_clear")
        counted = sem("counted")
        count_out = sem("count_out")
        count_in = sem("count_in")
        deg_made = sem("deg_made")
        root_made = sem("root_made")
        acc_staged = [sem(f"acc_staged{s}") for s in range(4)]
        product = [sem(f"product{s}") for s in range(5)]
        product_read = [sem(f"product_read{s}") for s in range(5)]
        var_ready = [sem(f"var_ready{s}") for s in range(6)]
        root_ready = [sem(f"root_ready{s}") for s in range(6)]
        shift_ready = {s: sem(f"shift_ready{s}") for s in (4, 5)}
        x_made = sem("x_made")
        x_kept = {s: sem(f"x_kept{s}") for s in (2, 3)}
        t_ready = [sem(f"t_ready{s}") for s in range(5)]
        t_stored = [sem(f"t_stored{s}") for s in range(5)]
        turned = [sem(f"turned{s}") for s in range(5)]
        acc_set = [sem(f"acc_set{s}") for s in range(5)]
        pq_product = sem("pq_product")
        pq_ready = sem("pq_ready")
        pq_stored = sem("pq_stored")
        pad_stored = sem("pad_stored")
        e_loaded = [sem(f"e_loaded{b}") for b in range(2)]
        q_loaded = [sem(f"q_loaded{b}") for b in range(2)]
        e_positions = sem("e_positions")
        ot_made = sem("ot_made")
        o_made = sem("o_made")
        h1_product = sem("h1_product")
        h1_ready = sem("h1_ready")
        h2_product = sem("h2_product")
        h2_ready = sem("h2_ready")
        e_summed = sem("e_summed")
        e_added = sem("e_added")
        hid_product = sem("hid_product")
        hid_ready = sem("hid_ready")
        ffn_product = sem("ffn_product")
        ffn_read = sem("ffn_read")
        v_ready = sem("v_ready")
        tx_ready = sem("tx_ready")
        l_rows = [sem(f"l_rows{b}") for b in range(2)]
        l_win = [sem(f"l_win{b}") for b in range(2)]
        l_bc = sem("l_bc")
        l_ot = sem("l_ot")
        l_eq = sem("l_eq")
        m_product = sem("m_product")
        m_ready = sem("m_ready")
        r_product = sem("r_product")
        r_ready = sem("r_ready")
        scattered = [sem(f"scattered{j}") for j in range(TABLES)]
        r_free = sem("r_free")
        sums_in = sem("sums_in")
        sums_used = sem("sums_used")
        out_stored = sem("out_stored")

        block = ctx.enter_context(nc.Block())

        def bank(n, k=1):
            return ps[:, n:n + k, :].rearrange("p a b -> p (a b)")

        def blocks_of(ap, width=P, n=GROUP):
            return ap[:, 0:n * width].rearrange("p (a b) -> p a b", b=width)

        def along(ap, n=P):
            return ap.unsqueeze(2).broadcast_to([ap.shape[0], ap.shape[1], n])

        def over(ap, n):
            return ap.unsqueeze(1).broadcast_to([ap.shape[0], n, ap.shape[1]])

        def acc_group(g):
            return acc[:, ds(g * SPAN, SPAN)]

        def x_group(g):
            return X[:, ds(g * GROUP, GROUP), :]

        def window_starts(eng, kind, c, n):
            _, starts = nc.values_load_multi_w_load_instructions(
                first[0:1, ds(c, n)], engines=[kind], min_val=0, max_val=NODES - 1,
                skip_runtime_bounds_check_because="destinations are node numbers")
            return list(starts)

        class Steps:

            def __init__(self, eng):
                self.eng, self.base, self.k, self.i, self.per = eng, 0, 0, None, 0

            def __call__(self, ins):
                self.go(ins)
                self.wait(0)

            def go(self, ins):
                ins.then_inc(dve_step, 1)
                self.k += 1

            def wait(self, back):
                n = self.base + self.k - back
                self.eng.wait_ge(dve_step, n if self.i is None else self.i * self.per + n)

            def enter(self, i, per, start=0):
                self.base += self.k - start * per
                self.i, self.per, self.k = i, per, 0
                self.start = start

            def leave(self, end):
                assert self.k == self.per, (self.k, self.per)
                self.base += end * self.per
                self.i, self.k = None, 0

        @block.sync
        def _(sp):
            SP = mybir.EngineType.SP
            for tile, source in [
                (dstI[:], dst_t), (first[:], first_dst), (srcI[:, 0:CHUNKS], src_t), (wt[:], weight_t),
                (W0[:], w0_t), (W1[:], w1), (W2[:], w2),
                (EW1[:], e_w1.rearrange("(a p) n -> p a n", p=P)), (EW2[:], e_w2), (EW3[:], e_w3),
                (EWd1[:], e_wd1), (EWd2[:], e_wd2.rearrange("(a p) n -> p a n", p=P)),
                (WL[:], w_last.rearrange("(a p) n -> p a n", p=P)),
                (eb1[:], e_b1), (ebd1[:], e_bd1),
                (eb2[:], e_b2),
                (X[:], x.rearrange("(b p) d -> p b d", p=P)),
            ]:
                sp.dma_start(tile, source).then_inc(loaded, 16)
            for v in range(10):
                sp.dma_start(vec[:, v, :], row_vectors[v:v + 1, :].broadcast_to([P, P])).then_inc(loaded, 16)
            sp.wait_ge(setup_ev, 6)
            full = CHUNKS // P
            rest = CHUNKS - full * P
            for n in range(3):
                sp.dma_start(edge_rows3[n, 0:full * P, :].rearrange("(a p) e -> p a e", p=P),
                             turned_rows[n][:, 0:full, :]).then_inc(rows_out, 16)
                sp.dma_start(edge_rows3[n, full * P:CHUNKS, :], turned_rows[n][0:rest, full, :]
                             ).then_inc(rows_out, 16)
            sp.wait_ge(made_iota, 5)
            sp.dma_start(table_q[NODES:WIDE, :], zeros[:, 0:P]).then_inc(pad_stored, 16)
            sp.dma_start(table_x[NODES:WIDE, :], zeros[:, 0:P]).then_inc(pad_stored, 16)

            sp.wait_ge(counted, 1)
            sp.dma_start(count_row_d.rearrange("(o n) -> o n", o=1), count_row[0:1, 0:NODES]).then_inc(count_out, 16)
            sp.wait_ge(count_out, 16)
            sp.dma_start(count[:], count_row_d.rearrange("(b p) -> p b", p=P), allow_slow_non_contiguous=True).then_inc(count_in, 16)

            def store_groups(s, table, ready):
                rows = table[0:NODES, :].rearrange("(b p) d -> p b d", p=P)
                with sp.Fori(0, GROUPS) as g:
                    sp.wait_ge(ready, g + 1)
                    sp.dma_start(rows[:, ds(g * GROUP, GROUP), :], T[:]).then_inc(t_stored[s], 16)

            store_groups(0, table1, t_ready[0])
            store_groups(1, table2, t_ready[1])

            def load_rows3(b, c, done):
                sp.dma_start(rows3[b][:], edge_rows3[:, ds(c, HALF), :].rearrange("r c e -> r (c e)")
                             ).then_inc(done, 16)

            sp.wait_ge(rows_out, 96)
            for b in range(2):
                load_rows3(b, b * HALF, srow_in[b])
            with sp.Fori(1, ITERATIONS) as i:
                for b in range(2):
                    sp.wait_ge(src_bc, i * 4 + (2 * b - 2))
                    load_rows3(b, i * 2 * HALF + b * HALF, srow_in[b])

            rows_p = table_p.rearrange("(b p) d -> p b d", p=P)
            rows_q = table_q[0:NODES, :].rearrange("(b p) d -> p b d", p=P)
            with sp.Fori(0, GROUPS) as g:
                sp.wait_ge(pq_ready, g + 1)
                sp.dma_start(rows_p[:, ds(g * GROUP, GROUP), :], PQ[:, :, 0:P]).then_inc(pq_stored, 16)
                sp.dma_start(rows_q[:, ds(g * GROUP, GROUP), :], PQ[:, :, P:2 * P]).then_inc(pq_stored, 16)

            sp.wait_ge(pq_stored, 32 * GROUPS)
            sp.wait_ge(pad_stored, 32)
            def load_edges(i, b):
                c = i * 2 * HALF + b * HALF
                if not (type(i) is int and i == 0):
                    sp.wait_ge(h1_product, i * 4 + (2 * b - 2))
                sp.sem_inc(gate["sp"], 1)
                sp.dma_start(Gw[b].rearrange("p a b -> p (a b)"), edge_attr_t[:, ds(c * P, HALF * P)]
                             ).then_inc(e_loaded[b], 16)
                load_rows3(b, c, e_loaded[b])
                for j, n0 in enumerate(window_starts(sp, SP, c, HALF)):
                    sp.dma_start(Win[b][:, j, :], table_q[ds(n0, P), :]).then_inc(q_loaded[b], 16)

            for b in range(2):
                load_edges(0, b)
            with sp.Fori(1, ITERATIONS) as i:
                for b in range(2):
                    load_edges(i, b)

            store_groups(3, table_x, t_ready[3])
            sp.wait_ge(t_stored[3], 16 * GROUPS)
            def load_last(i, b):
                c = i * 2 * HALF + b * HALF
                if not (type(i) is int and i == 0):
                    sp.wait_ge(l_bc, i * 4 + (2 * b - 2))
                load_rows3(b, c, l_rows[b])
                if not (type(i) is int and i == 0):
                    sp.wait_ge(m_product, i * 4 + (2 * b - 2))
                sp.sem_inc(gate["sp"], 1)
                for j, n0 in enumerate(window_starts(sp, SP, c, HALF)):
                    sp.dma_start(Win[b][:, j, :], table_x[ds(n0, P), :]).then_inc(l_win[b], 16)

            for b in range(2):
                load_last(0, b)
            with sp.Fori(1, ITERATIONS) as i:
                for b in range(2):
                    load_last(i, b)

            for j in range(TABLES):
                sp.wait_ge(scattered[j], 16 * STEPS)
            def load_sums(g):
                sp.wait_ge(sums_used, g)
                for t in range(TABLES):
                    rows = sums_d[t][0:NODES, :].rearrange("(b p) d -> p b d", p=P)
                    sp.dma_start(SG[:, t, :].rearrange("p (a b) -> p a b", b=ROW),
                                 rows[:, ds(g * GROUP, GROUP), :]).then_inc(sums_in, 16)

            load_sums(0)
            with sp.Fori(1, GROUPS) as g:
                load_sums(g)
            sp.wait_ge(out_stored, 16 * GROUPS)

        @block.gpsimd
        def _(pool):
            nc.gpsimd.iota(iotaI, pattern=[[1, P]], base=0, channel_multiplier=0).then_inc(made_iota, 1)
            nc.gpsimd.iota(iopI[:], pattern=[[0, 1]], base=0, channel_multiplier=1).then_inc(made_iota, 1)
            nc.gpsimd.memset(zeros[:], 0.0).then_inc(made_iota, 1)
            nc.gpsimd.memset(acc[:], 0.0).then_inc(made_iota, 1)
            nc.gpsimd.memset(count_row[:], 0.0).then_inc(made_iota, 1)
            nc.gpsimd.memset(minus_half[:], -0.5).then_inc(made_iota, 1)
            nc.gpsimd.memset(srcI[:, CHUNKS:CHUNKS_AHEAD], 0).then_inc(made_iota, 1)
            pool.wait_ge(made_iota, 7)
            pool.wait_ge(loaded, 16 * N_LOADS)

            def gather_half(k, table, used, i, b):
                pool.wait_ge(idx_ready[k][b], i + 1)
                if used is not None:
                    pool.wait_ge(used[b], i)
                elif not (type(i) is int and i == 0):
                    pool.wait_ge(h1_product, i * 4 + (2 * b - 2))
                pool.sem_inc(gate["pool"], 1)
                for j in range(HALF):
                    pool.indirect_dma_start(
                        G[b][:, j, :], None, table,
                        bass.IndirectOffsetOnAxis(ap=IX[b][:, j:j + 1].bitcast(u32), axis=0),
                    ).then_inc(gathered[k][b], 16)

            def gathers(k, table, used):
                for b in range(2):
                    gather_half(k, table, used, 0, b)
                with pool.Fori(1, ITERATIONS) as i:
                    for b in range(2):
                        gather_half(k, table, used, i, b)

            def rsqrt(s, n, z):
                pool.wait_ge(var_ready[s], n + 1)
                nc.gpsimd.tensor_tensor(rstd[z][:], var[z][:], minus_half[:, 0:GROUP], ALU.pow).then_inc(root_ready[s], 1)

            def rsqrts(s, first):
                with pool.Fori(first, GROUPS) as g:
                    rsqrt(s, g, 0)

            def shifts(s, n, g, z):
                pool.wait_ge(root_ready[s], n + 1)
                nc.gpsimd.tensor_tensor(shift[:], minus_mean[:], rstd[z][:], ALU.mult).then_inc(shift_ready[s], 1)

            gathers(0, x, scaled)
            rsqrt(0, 0, 0)
            pool.wait_ge(deg_made, 1)
            nc.gpsimd.tensor_tensor(dinv[:], dinv[:], minus_half[:], ALU.pow).then_inc(root_made, 1)
            rsqrts(0, 1)
            pool.wait_ge(t_stored[0], 16 * GROUPS)
            gathers(1, table1, summed[1])
            pool.wait_ge(t_stored[1], 16 * GROUPS)
            gathers(2, table2, summed[2])
            rsqrts(2, 0)
            pool.wait_ge(acc_staged[2], GROUPS)
            nc.gpsimd.memset(acc[:], 0.0).then_inc(acc_clear, 1)
            pool.wait_ge(pq_stored, 32 * GROUPS)
            gathers(3, table_p, None)
            rsqrt(3, 0, 0)

            def mlp_part(g):
                rsqrt(3, g + 1, 0)
                rsqrt(4, g * 2, 1)
                rsqrt(4, g * 2 + 1, 1)
                shifts(4, g * 2 + 1, g, 1)

            with pool.Fori(0, GROUPS - 1) as g:
                mlp_part(g)
            rsqrt(4, 2 * GROUPS - 2, 1)
            rsqrt(4, 2 * GROUPS - 1, 1)
            shifts(4, 2 * GROUPS - 1, GROUPS - 1, 1)

            pool.wait_ge(zeroed, 16 * TABLES * ZERO_PARTS)
            with pool.Fori(0, ITERATIONS * 2) as i:
                for q in range(2):
                    t = i * 2 + q
                    pool.wait_ge(r_ready, t + 1)
                    for j in range(BATCH):
                        pool.wait_ge(scattered[j], t * 16)
                        pool.sem_inc(gate["pool"], 1)
                        pool.indirect_dma_start(
                            sums_d[j],
                            bass.IndirectOffsetOnAxis(ap=RX[q][:, j:j + 1].bitcast(u32), axis=0),
                            R[q][:, j, :], None, compute_op=ALU.add,
                        ).then_inc(scattered[j], 16)
                    pool.sem_inc(r_free, 1)
            with pool.Fori(0, GROUPS) as g:
                rsqrt(5, g, 0)
                shifts(5, g, g, 0)

        @block.scalar
        def _(act):
            act.wait_ge(made_iota, 7)
            act.wait_ge(loaded, 16 * N_LOADS)

            def indices(k, b, i):
                nc.scalar.copy(IX[b][:], srcI[:, ds(i * 2 * HALF + b * HALF, HALF)]).then_inc(idx_ready[k][b], 1)

            def indices_ahead(k):
                for b in range(2):
                    indices(k, b, 0)
                with act.Fori(0, ITERATIONS) as i:
                    for b in range(2):
                        act.wait_ge(gathered[k][b], i * (16 * HALF) + 16 * HALF)
                        act.sem_inc(gate["act"], 1)
                        indices(k, b, i + 1)

            for b in range(2):
                indices(0, b, 0)
            with act.Fori(0, ITERATIONS) as i:
                for b in range(2):
                    act.wait_ge(gathered[0][b], i * (16 * HALF) + 16 * HALF)
                    act.sem_inc(gate["act"], 1)
                    indices(0, b, i + 1)
                    act.wait_ge(summed[0][b], i)
                    act.sem_inc(gate["act"], 1)
                    for j in range(HALF):
                        last = nc.scalar.activation(Gw[b][:, j, :], G[b][:, j, :], ACT.Copy,
                                                    scale=wt[:, ds(i * 2 * HALF + b * HALF + j, 1)])
                    last.then_inc(scaled[b], 1)

            def set_acc(s, g):
                act.wait_ge(turned[s], g + 1)
                act.sem_inc(gate["act"], 1)
                nc.scalar.copy(acc_group(g), bank(2, 2)[:, 0:SPAN]).then_inc(acc_set[s], 1)

            def stage_group(s, g):
                act.wait_ge(product[s], g)
                act.sem_inc(gate["act"], 1)
                nc.scalar.copy(stage[:], acc_group(g)).then_inc(acc_staged[s], 1)

            def normalise(to, source, s, g, z):
                act.wait_ge(shift_ready[s], g + 1)
                for j in range(GROUP):
                    last = nc.scalar.activation(to[:, j, :], source[:, j, :], ACT.Identity,
                                                bias=shift[:, j:j + 1], scale=rstd[z][:, j:j + 1])
                return last

            def end_of_layer(g):
                if not (type(g) is int and g < 1):
                    act.wait_ge(t_stored[3], g * 16)
                    act.wait_ge(x_kept[3], g)
                normalise(T, B, 4, g, 1).then_inc(t_ready[3], 1)
                keep_x(3, g)

            def keep_x(s, g):
                act.wait_ge(t_ready[s], g + 1)
                act.sem_inc(gate["act"], 1)
                nc.scalar.copy(x_group(g), T[:]).then_inc(x_kept[s], 1)

            def all_added(k):
                for b in range(2):
                    act.wait_ge(added[k][b], ITERATIONS)

            def scale_rows(g):
                act.wait_ge(x_made, g + 1)
                act.wait_ge(t_stored[0], g * 16)
                act.wait_ge(turned[0], g)
                act.sem_inc(gate["act"], 1)
                for j in range(GROUP):
                    last = nc.scalar.activation(T[:, j, :], X[:, ds(g * GROUP + j, 1), :].rearrange("p a b -> p (a b)"),
                                                ACT.Copy, scale=dinv[:, ds(g * GROUP + j, 1)])
                last.then_inc(t_ready[0], 1)

            all_added(0)
            stage_group(0, 0)
            stage_group(0, 1)
            act.wait_ge(root_made, 1)
            scale_rows(0)
            set_acc(0, 0)
            with act.Fori(1, GROUPS - 1) as g:
                stage_group(0, g + 1)
                scale_rows(g)
                set_acc(0, g)
            scale_rows(GROUPS - 1)
            set_acc(0, GROUPS - 1)

            for t in range(TABLES):
                parts = sums_d[t].rearrange("n d -> (n d)").rearrange("(a p f) -> a p f", p=P, f=ZERO_COLS)
                for a in range(ZERO_PARTS):
                    act.dma_start(parts[a], zeros[:]).then_inc(zeroed, 16)
            indices_ahead(1)

            all_added(1)
            stage_group(1, 0)
            with act.Fori(0, GROUPS - 1) as g:
                stage_group(1, g + 1)
                set_acc(1, g)
            set_acc(1, GROUPS - 1)
            indices_ahead(2)

            def project(g):
                act.wait_ge(turned[2], g + 1)
                act.wait_ge(pq_product, g)
                nc.scalar.copy(XT[:], bank(2, 2)[:, 0:SPAN]).then_inc(acc_set[2], 1)
                act.wait_ge(pq_product, g + 1)
                act.wait_ge(pq_stored, g * 32)
                nc.scalar.copy(PQ, bank(4, 4)[:, 0:GROUP * 2 * P].rearrange("p (a b) -> p a b", b=2 * P)
                               ).then_inc(pq_ready, 1)

            all_added(2)
            stage_group(2, 0)
            with act.Fori(0, GROUPS - 1) as g:
                stage_group(2, g + 1)
                keep_x(2, g)
                project(g)
            keep_x(2, GROUPS - 1)
            project(GROUPS - 1)

            def relu_h1(t, par):
                act.wait_ge(h1_product, t + 1)
                if not (type(t) is int and t < 2):
                    act.wait_ge(h2_product, t - 1)
                nc.scalar.activation(H1[par][:].rearrange("p a b -> p (a b)"), bank(2 + par), ACT.Relu,
                                     bias=eb1[:, 0:1]).then_inc(h1_ready, 1)

            def edge_iteration(i):
                for s in range(4):
                    t = i * 4 + s
                    relu_h1(t, s % 2)
                    if s % 2 == 0:
                        act.wait_ge(gathered[3][s // 2], i * (16 * HALF) + 16 * HALF)
                        act.sem_inc(gate["act"], 1)
                        indices(3, s // 2, i + 1)

            for b in range(2):
                indices(3, b, 0)
            edge_iteration(0)
            with act.Fori(1, ITERATIONS) as i:
                edge_iteration(i)

            def hidden(g):
                act.wait_ge(turned[3], g + 1)
                act.wait_ge(ffn_product, g)
                nc.scalar.copy(XT[:], bank(2, 2)[:, 0:SPAN]).then_inc(acc_set[3], 1)
                for h in range(4):
                    for z in range(2):
                        act.wait_ge(hid_product, g * 8 + (2 * h + z + 1))
                        nc.scalar.activation(HD[:, h, z * (SPAN // 2):(z + 1) * (SPAN // 2)],
                                             bank(4 + z)[:, 0:SPAN // 2], ACT.Relu,
                                             bias=ebd1[:, h:h + 1]).then_inc(hid_ready, 1)

            act.wait_ge(e_added, STEPS)
            stage_group(3, 0)
            stage_group(3, 1)
            hidden(0)
            stage_group(3, 2)
            with act.Fori(1, GROUPS - 2) as g:
                hidden(g)
                end_of_layer(g - 1)
                stage_group(3, g + 2)
            hidden(GROUPS - 2)
            end_of_layer(GROUPS - 3)
            hidden(GROUPS - 1)
            end_of_layer(GROUPS - 2)
            end_of_layer(GROUPS - 1)

            act.wait_ge(row_index, 1)

            def weigh(i, q, b, t, par):
                act.wait_ge(m_product, t + 1)
                if not (type(t) is int and t < 2):
                    act.wait_ge(r_product, t - 1)
                act.sem_inc(gate["act"], 1)
                c = i * 2 * HALF + (b * HALF + q * BATCH)
                for j in range(BATCH):
                    nc.scalar.activation(Mw[par][:, j, 0:P], bank(2 + par)[:, j * P:(j + 1) * P], ACT.Copy,
                                         scale=wt[:, ds(c + j, 1)])
                nc.scalar.copy(Mw[par][:, :, P:ROW], wt[:, ds(c, BATCH)].unsqueeze(2)).then_inc(m_ready, 1)

            def evacuate_r(i, q, b, t, par):
                act.wait_ge(r_product, t + 1)
                if not (type(t) is int and t < 1):
                    act.wait_ge(r_free, t)
                act.sem_inc(gate["act"], 1)
                nc.scalar.copy(RX[par][:], rowI[:, ds(i * 2 * HALF + (b * HALF + q * BATCH), BATCH)])
                nc.scalar.copy(R[par][:], bank(4, 2).rearrange("p (a b) -> p a b", b=256)[:, :, 0:ROW]
                               ).then_inc(r_ready, 1)

            def last_iteration(i, start):
                for s in range(4):
                    t = i * 4 + s
                    weigh(i, s % 2, s // 2, t, s % 2)
                    if s == 0:
                        if not start:
                            evacuate_r(i - 1, 1, 1, t - 1, 1)
                    else:
                        evacuate_r(i, (s - 1) % 2, (s - 1) // 2, t - 1, (s - 1) % 2)

            last_iteration(0, True)
            with act.Fori(1, ITERATIONS) as i:
                last_iteration(i, False)
            evacuate_r(ITERATIONS - 1, 1, 1, STEPS - 1, 1)

            def evacuate_last(g):
                act.wait_ge(turned[4], g + 1)
                act.wait_ge(product[4], g)
                nc.scalar.copy(XT[:], bank(2, 2)[:, 0:SPAN])
                nc.scalar.copy(HT[:], bank(4, 2)[:, 0:SPAN]).then_inc(acc_set[4], 1)

            def finish(g):
                normalise(A, A, 5, g, 0).then_inc(t_ready[4], 1)
                act.wait_ge(t_ready[4], g + 1)
                act.dma_start(out.rearrange("(b p) d -> p b d", p=P)[:, ds(g * GROUP, GROUP), :], A[:]
                              ).then_inc(out_stored, 16)

            evacuate_last(0)
            with act.Fori(0, GROUPS - 1) as g:
                evacuate_last(g + 1)
                finish(g)
            finish(GROUPS - 1)

        @block.vector
        def _(dve):
            DVE = mybir.EngineType.DVE
            step = Steps(dve)
            VB0, VB1, VB2, VB3, VBD2, VG1, VBE1, VG2, VBE2, VB2E = range(10)

            dve.wait_ge(made_iota, 2)
            nc.vector.memset(ones[:], 1.0)
            nc.vector.memset(dloc[:, CHUNKS:CHUNKS_AHEAD], 0.0)
            nc.vector.tensor_copy(iota[:], iotaI)
            step(nc.vector.tensor_copy(iop[:], iopI[:]))
            nc.vector.tensor_scalar(pick_dst[:], iop[0:3, 0:1].broadcast_to([3, P]), 0.0, None,
                                    ALU.is_equal)
            nc.vector.tensor_scalar(pick_src[:], iop[0:3, 0:1].broadcast_to([3, P]), 0.0, None,
                                    ALU.is_gt)
            nc.vector.tensor_scalar(trash[:], iop[:], float(NODES), None, ALU.add)
            nc.vector.tensor_scalar(ident[:], iota[:], iop[:, 0:1], None, ALU.is_equal)
            nc.vector.tensor_scalar(lower[:], iota[:], iop[:, 0:1], None, ALU.is_lt)
            dve.wait_ge(loaded, 16 * N_LOADS)
            nc.vector.tensor_copy(srcF[:], srcI[:, 0:CHUNKS])
            step(nc.vector.tensor_scalar(low_bits.bitcast(i32), srcI[:, 0:CHUNKS], P - 1, None, ALU.bitwise_and))
            step(nc.vector.tensor_copy(high_bits, low_bits.bitcast(i32)))
            step(nc.vector.tensor_copy(low_bits, high_bits))
            step(nc.vector.tensor_tensor(high_bits, srcF[:], low_bits, ALU.subtract))
            nc.vector.tensor_scalar(minus_b2[:], vec[:, VB2E, :], -1.0, None, ALU.mult)
            step(nc.vector.tensor_copy(T[:, 0, :], eb2[:, 0:1].broadcast_to([P, P])))
            nc.vector.tensor_copy(dloc[:, 0:CHUNKS], dstI[:])
            nc.vector.tensor_copy(firstF, first[:]).then_inc(setup_dloc, 1)
            dve.wait_ge(setup_dloc, 1)
            dve.wait_ge(setup_bc, 1)
            half_c = CHUNKS // 2
            for z in range(2):
                last = nc.vector.tensor_tensor(dloc[:, z * half_c:(z + 1) * half_c],
                                               dloc[:, z * half_c:(z + 1) * half_c],
                                               bank(z)[:, 0:half_c], ALU.subtract)
            last.then_inc(setup_dloc, 1)
            dve.wait_ge(setup_tr, 1)
            full, rest = CHUNKS // P, CHUNKS % P
            for tile, at in zip(turned_rows, (2, 4, 6)):
                nc.vector.tensor_copy(tile[:, 0:full, :], blocks_of(bank(at, 2), P, full)).then_inc(setup_ev, 1)
                nc.vector.tensor_copy(tile[0:rest, full, :], blocks_of(bank(at, 2))[0:rest, full, :]
                                      ).then_inc(setup_ev, 1)
            dve.wait_ge(setup_dloc, 2)
            step(nc.vector.tensor_tensor(vec[:, VB3, :], vec[:, VB3, :], bank(1)[:, 0:P], ALU.add))

            def make_onehot(k, i, b):
                nc.vector.tensor_tensor(O[b], over(iota[:], HALF),
                                        along(dloc[:, ds(i * 2 * HALF + b * HALF, HALF)]),
                                        ALU.is_equal).then_inc(onehot[k][b], 1)

            def sums(k):
                per = 2 * (HALF * (2 if k == 0 else 1) + (6 if k == 2 else 0))
                for b in range(2):
                    make_onehot(k, 0, b)
                with dve.Fori(0, ITERATIONS) as i:
                    step.enter(i, per)
                    for b in range(2):
                        c = i * 2 * HALF + b * HALF
                        dve.wait_ge(summed[k][b], i + 1)
                        starts = window_starts(dve, DVE, c, HALF)

                        def add(j):
                            step.go(nc.vector.tensor_tensor(acc[:, ds(starts[j], P)], acc[:, ds(starts[j], P)],
                                                            bank(2 * b, 2)[:, j * P:(j + 1) * P], ALU.add))

                        def add_count(j):
                            step.go(nc.vector.tensor_tensor(count_row[0:1, ds(starts[j], P)],
                                                            count_row[0:1, ds(starts[j], P)],
                                                            bank(4 + 2 * b, 2)[0:1, j * P:(j + 1) * P], ALU.add))

                        for j in range(HALF):
                            if k == 2 and j < 6:
                                q = j // 3
                                if j % 3 == 0:
                                    dve.wait_ge(src_bc, i * 4 + (2 * b + q + 1))
                                    step.go(nc.vector.tensor_tensor(
                                        eq[:], blocks_of(bank(4 + q), P, BATCH),
                                        along(srcF[:, ds(c + q * BATCH, BATCH)]), ALU.is_equal))
                                elif j % 3 == 1:
                                    step.go(nc.vector.tensor_tensor(eq[:], eq[:], over(lower[:], BATCH), ALU.mult))
                                else:
                                    step.go(nc.vector.tensor_reduce(repeats[:, ds(c + q * BATCH, BATCH)], eq[:],
                                                                    axis=AX.X, op=ALU.add))
                                step.wait(1)
                            add(j)
                            if k == 0:
                                step.wait(1)
                                add_count(j)
                            step.wait(1 if k == 0 or (k == 2 and j < 5) else 0)
                            if k == 2 and j in (0, 3):
                                dve.sem_inc(eq_made[j // 3], 1)
                        if k == 0:
                            step.wait(0)
                        dve.sem_inc(added[k][b], 1)
                        make_onehot(k, i + 1, b)
                    step.leave(ITERATIONS)

            def statistics(s, source, z=0, minus=False):
                for j in range(GROUP):
                    last = nc.vector.bn_stats(stats[z][:, j, :], source[:, j, :])
                step(last)
                dve.sem_inc(gate["dve"], 1)
                for j in range(GROUP):
                    last = nc.vector.bn_aggr(mv[z][:, j, :], stats[z][:, j, :])
                step(last)
                if minus:
                    nc.vector.tensor_scalar(minus_mean[:], mv[z][:, :, 0], -1.0, None, ALU.mult)
                nc.vector.tensor_scalar(var[z][:], mv[z][:, :, 1], EPS, None, ALU.add).then_inc(var_ready[s], 1)

            def root_of(s, g):
                dve.wait_ge(root_ready[s], g + 1)
                dve.sem_inc(gate["dve"], 1)

            def normalise(to, source, z=0):
                for j in range(GROUP):
                    last = nc.vector.tensor_scalar(to[:, j, :], source[:, j, :], mv[z][:, j, 0:1], rstd[z][:, j:j + 1],
                                                   ALU.subtract, ALU.mult)
                return last

            def scaled_by(to, source, by, g, row):
                for j in range(GROUP):
                    last = nc.vector.scalar_tensor_tensor(to[:, j, :], source[:, j, :],
                                                          by[:, ds(g * GROUP + j, 1)], vec[:, row, :],
                                                          ALU.mult, ALU.add)
                return last

            D = blocks_of(bank(0, 2))

            dve.wait_ge(made_iota, 5)
            sums(0)
            dve.sem_inc(counted, 1)

            def wait_t_free(s, g):
                dve.wait_ge(t_stored[s], g * 16)
                dve.wait_ge(turned[s], g)

            def group0(g, start):
                dve.wait_ge(x_made, g)
                dve.wait_ge(product[0], g + 1)
                nc.vector.scalar_tensor_tensor(A[:], D, 0.0, x_group(g), ALU.max, ALU.add
                                               ).then_inc(product_read[0], 1)
                dve.wait_ge(product_read[0], g + 1)
                statistics(0, A[:])
                root_of(0, g)
                normalise(x_group(g), A[:]).then_inc(x_made, 1)
                if start:
                    dve.wait_ge(count_in, 16)
                    nc.vector.tensor_scalar(dinv[:], count[:], 1.0, None, ALU.add).then_inc(deg_made, 1)
                    nc.vector.reciprocal(cinv[:], count[:])

            group0(0, True)
            with dve.Fori(1, GROUPS) as g:
                step.enter(g, 2, 1)
                group0(g, False)
                step.leave(GROUPS)

            dve.wait_ge(acc_set[0], GROUPS)
            sums(1)
            with dve.Fori(0, GROUPS) as g:
                dve.wait_ge(t_ready[1], g)
                dve.wait_ge(product[1], g + 1)
                scaled_by(A[:], D, dinv, g, VB1).then_inc(product_read[1], 1)
                dve.wait_ge(product_read[1], g + 1)
                wait_t_free(1, g)
                nc.vector.scalar_tensor_tensor(T[:], A[:], 0.0, along(dinv[:, ds(g * GROUP, GROUP)]),
                                               ALU.max, ALU.mult).then_inc(t_ready[1], 1)
            dve.wait_ge(acc_set[1], GROUPS)
            sums(2)
            step(nc.vector.tensor_scalar(repeats, repeats, 1.0, None, ALU.min))
            step(nc.vector.tensor_scalar(dstF, srcF[:], -1.0, trash[:, 0:1], ALU.mult, ALU.add))
            step(nc.vector.tensor_tensor(dstF, dstF, repeats, ALU.mult))
            nc.vector.tensor_tensor(rowI[:], dstF, srcF[:], ALU.add).then_inc(row_index, 1)

            with dve.Fori(0, GROUPS) as g:
                step.enter(g, 3)
                dve.wait_ge(t_ready[2], g)
                dve.wait_ge(product[2], g + 1)
                scaled_by(A[:], D, dinv, g, VB2).then_inc(product_read[2], 1)
                dve.wait_ge(product_read[2], g + 1)
                step(nc.vector.tensor_tensor(A[:], A[:], x_group(g), ALU.add))
                statistics(2, A[:])
                root_of(2, g)
                dve.wait_ge(turned[2], g)
                dve.wait_ge(x_kept[2], g)
                dve.sem_inc(gate["dve"], 1)
                normalise(T[:], A[:]).then_inc(t_ready[2], 1)
                step.leave(GROUPS)

            dve.wait_ge(acc_clear, 1)

            def spread(t, par):
                dve.wait_ge(e_positions, t + 1)
                if not (type(t) is int and t < 2):
                    dve.wait_ge(h1_product, t - 1)
                nc.vector.tensor_scalar(OT[par][:].rearrange("p a b -> p (a b)"), bank(par), iop[:, 0:1], None,
                                        ALU.is_equal).then_inc(ot_made, 1)

            def edge_onehot(i, b, t):
                if not (type(t) is int and t < 4):
                    dve.wait_ge(e_summed, t - 2)
                nc.vector.tensor_tensor(O[b][:], over(iota[:], HALF),
                                        along(dloc[:, ds(i * 2 * HALF + b * HALF, HALF)]),
                                        ALU.is_equal).then_inc(o_made, 1)

            def max_h2(t, par):
                dve.wait_ge(h2_product, t + 1)
                if not (type(t) is int and t < 2):
                    dve.wait_ge(e_summed, t - 1)
                nc.vector.tensor_tensor(H2[par][:], blocks_of(bank(4), P, BATCH), over(minus_b2[:], BATCH),
                                        ALU.max).then_inc(h2_ready, 1)

            def edge_adds(i, s, t):
                dve.wait_ge(e_summed, t + 1)
                starts = window_starts(dve, DVE, i * 2 * HALF + s * BATCH, BATCH)
                for j, n0 in enumerate(starts):
                    step.wait(0)
                    step.go(nc.vector.tensor_tensor(acc[:, ds(n0, P)], acc[:, ds(n0, P)],
                                                    bank(5 + s % 2)[:, j * P:(j + 1) * P], ALU.add))
                    yield
                step.wait(0)
                dve.sem_inc(e_added, 1)

            def edge_iteration(i, start, end):
                for s in range(4):
                    t = i * 4 + s
                    if s == 3:
                        adds = edge_adds(i, 0, t - 3)
                    elif not start:
                        adds = edge_adds(i - 1, s + 1, t - 3)
                    else:
                        adds = iter(())
                    next(adds, None)
                    if not (end and s == 3):
                        spread(t + 1, (s + 1) % 2)
                    next(adds, None)
                    if s % 2 == 0:
                        edge_onehot(i, s // 2, t)
                        next(adds, None)
                    if not (start and s == 0):
                        max_h2(t - 1, (s + 1) % 2)
                    for _ in adds:
                        pass

            spread(0, 0)
            edge_iteration(0, True, False)
            with dve.Fori(1, ITERATIONS - 1) as i:
                step.enter(i, 4 * BATCH, 1)
                edge_iteration(i, False, False)
                step.leave(ITERATIONS - 1)
            edge_iteration(ITERATIONS - 1, False, True)
            max_h2(STEPS - 1, 1)
            for s in (1, 2, 3):
                for _ in edge_adds(ITERATIONS - 1, s, STEPS - 4 + s):
                    pass

            MLP = blocks_of(bank(6, 2))

            def before_mlp(g):
                dve.wait_ge(product[3], g + 1)
                scaled_by(A[:], D, cinv, g, VB3).then_inc(product_read[3], 1)
                dve.wait_ge(product_read[3], g + 1)
                step(nc.vector.tensor_tensor(A[:], A[:], x_group(g), ALU.add))
                statistics(3, A[:])

            def mlp_input(g):
                dve.wait_ge(root_ready[3], g + 1)
                dve.sem_inc(gate["dve"], 1)
                step(normalise(A[:], A[:]))
                step(nc.vector.tensor_tensor(A[:], A[:], over(vec[:, VG1, :], GROUP), ALU.mult))
                dve.wait_ge(turned[3], g)
                nc.vector.tensor_tensor(V[:], A[:], over(vec[:, VBE1, :], GROUP), ALU.add).then_inc(v_ready, 1)
                dve.wait_ge(v_ready, g + 1)

            def behind_mlp(g):
                dve.wait_ge(ffn_product, g + 1)
                if not (type(g) is int and g < 1):
                    dve.wait_ge(t_ready[3], g)
                statistics(4, MLP, 1)

            def layer_end(g):
                dve.wait_ge(root_ready[4], g * 2 + 1)
                dve.sem_inc(gate["dve"], 1)
                normalise(B[:], MLP, 1).then_inc(ffn_read, 1)
                dve.wait_ge(ffn_read, g + 1)
                step(nc.vector.tensor_tensor(B[:], B[:], over(vec[:, VG2, :], GROUP), ALU.mult))
                step(nc.vector.tensor_tensor(B[:], B[:], over(vec[:, VBE2, :], GROUP), ALU.add))
                step(nc.vector.tensor_tensor(B[:], B[:], x_group(g), ALU.add))
                statistics(4, B[:], 1, True)

            before_mlp(0)
            mlp_input(0)
            with dve.Fori(0, GROUPS - 1) as g:
                step.enter(g, 3 + 2 + 2 + 5)
                before_mlp(g + 1)
                mlp_input(g + 1)
                behind_mlp(g)
                layer_end(g)
                step.leave(GROUPS - 1)
            behind_mlp(GROUPS - 1)
            layer_end(GROUPS - 1)

            def last_spread(i, s, t, par):
                dve.wait_ge(l_bc, t + 1)
                if not (type(t) is int and t < 2):
                    dve.wait_ge(m_product, t - 1)
                nc.vector.tensor_scalar(OT[par][:].rearrange("p a b -> p (a b)"), bank(6 * par), iop[:, 0:1], None,
                                        ALU.is_equal).then_inc(l_ot, 1)
                if not (type(t) is int and t < 2):
                    dve.wait_ge(r_product, t - 1)
                nc.vector.tensor_tensor(ET[par][:], blocks_of(bank(6 * par + 1), P, BATCH),
                                        along(srcF[:, ds(i * 2 * HALF + s * BATCH, BATCH)]), ALU.is_equal
                                        ).then_inc(l_eq, 1)

            for s in range(4):
                last_spread(0, s, s, s % 2)
            with dve.Fori(1, ITERATIONS) as i:
                for s in range(4):
                    last_spread(i, s, i * 4 + s, s % 2)

            def mean_rows(g):
                dve.wait_ge(sums_in, g * (16 * TABLES) + 16 * TABLES)
                nc.vector.tensor_reduce(S1, SG.rearrange("p t n -> p n t"), axis=AX.X, op=ALU.add
                                        ).then_inc(sums_used, 1)
                dve.wait_ge(sums_used, g + 1)
                S1v = S1.rearrange("p (a b) -> p a b", b=ROW)
                step(nc.vector.tensor_scalar(degree[:], S1v[:, :, P], 1e-6, None, ALU.add))
                step(nc.vector.reciprocal(per_degree[:], degree[:]))
                dve.wait_ge(turned[4], g)
                dve.sem_inc(gate["dve"], 1)
                nc.vector.tensor_copy(T[:], x_group(g))
                nc.vector.tensor_tensor(TX[:], S1v[:, :, 0:P], along(per_degree[:]), ALU.mult).then_inc(tx_ready, 1)
                dve.wait_ge(tx_ready, g + 1)

            def result(g):
                dve.wait_ge(product[4], g + 1)
                dve.wait_ge(out_stored, g * 16)
                nc.vector.tensor_tensor(A[:], D, x_group(g), ALU.add).then_inc(product_read[4], 1)
                dve.wait_ge(product_read[4], g + 1)
                statistics(5, A[:], 0, True)

            mean_rows(0)
            with dve.Fori(0, GROUPS - 1) as g:
                step.enter(g, 2 + 2)
                mean_rows(g + 1)
                result(g)
                step.leave(GROUPS - 1)
            result(GROUPS - 1)

        @block.tensor
        def _(pe):
            mm = nc.tensor.matmul

            pe.wait_ge(setup_dloc, 1)
            half_c = CHUNKS // 2
            for z in range(2):
                last = mm(bank(z)[:, 0:half_c], ones[0:1, :], firstF[0:1, z * half_c:(z + 1) * half_c],
                          start=True, stop=True)
            last.then_inc(setup_bc, 1)
            pe.wait_ge(setup_dloc, 2)
            mm(bank(1)[:, 0:P], T[:, 0, :], EW3[:], start=True, stop=True)
            for a in range(-(-CHUNKS // P)):
                n = min(P, CHUNKS - a * P)
                for source, at in ((dloc[:], 2), (low_bits, 4), (high_bits, 6)):
                    last = nc.tensor.transpose(bank(at, 2)[0:n, a * P:(a + 1) * P], source[:, a * P:a * P + n],
                                               ident[:])
            last.then_inc(setup_tr, 1)
            pe.wait_ge(setup_ev, 6)

            def sums(k):
                with pe.Fori(0, ITERATIONS) as i:
                    for b in range(2):
                        if k == 2:
                            pe.wait_ge(srow_in[b], i * 16 + 16)
                            for q in range(2):
                                pe.wait_ge(eq_made[q], i * 2 + b)
                                mm(bank(4 + q), pick_src[:], rows3[b][:, q * 512:(q + 1) * 512],
                                   start=True, stop=True).then_inc(src_bc, 1)
                        rows = Gw[b] if k == 0 else G[b]
                        pe.wait_ge(onehot[k][b], i + 1)
                        pe.wait_ge(added[k][b], i)
                        if k == 0:
                            for j in range(HALF):
                                mm(bank(4 + 2 * b, 2)[0:1, j * P:(j + 1) * P], ones[:, 0:1], O[b][:, j, :],
                                   start=True, stop=True)
                            pe.wait_ge(scaled[b], i + 1)
                        else:
                            pe.wait_ge(gathered[k][b], i * (16 * HALF) + 16 * HALF)
                        for j in range(HALF):
                            last = mm(bank(2 * b, 2)[:, j * P:(j + 1) * P], rows[:, j, :], O[b][:, j, :],
                                      start=True, stop=True)
                        last.then_inc(summed[k][b], 1)

            def dense(s, weight, g):
                pe.wait_ge(acc_staged[s], g + 1)
                pe.wait_ge(product_read[s], g)
                for j in range(GROUP):
                    if s == 0:
                        mm(bank(0, 2)[:, j * P:(j + 1) * P], ones[0:1, :], vec[0:1, 0, :], start=True, stop=False)
                    last = mm(bank(0, 2)[:, j * P:(j + 1) * P], stage[:, j * P:(j + 1) * P], weight[:],
                              start=(s != 0), stop=True)
                last.then_inc(product[s], 1)

            def turn(s, tile, ready, n, at=2):
                for j in range(GROUP):
                    last = nc.tensor.transpose(bank(at, 2)[:, j * P:(j + 1) * P], tile[:, j, :], ident[:])
                return last

            def skewed(s, weight, tail):
                dense(s, weight, 0)
                with pe.Fori(0, GROUPS - 1) as g:
                    dense(s, weight, g + 1)
                    tail(g)
                tail(GROUPS - 1)

            def tail_t(s):
                def tail(g):
                    pe.wait_ge(t_ready[s], g + 1)
                    pe.wait_ge(acc_set[s], g)
                    turn(s, T, None, g).then_inc(turned[s], 1)
                return tail

            def tail_pq(g):
                tail_t(2)(g)
                pe.wait_ge(acc_set[2], g + 1)
                pe.wait_ge(pq_ready, g)
                for j in range(GROUP):
                    last = mm(bank(4, 4)[:, j * 256:(j + 1) * 256], XT[:, j * P:(j + 1) * P],
                              EW1[:, 1:3, :].rearrange("p a b -> p (a b)"), start=True, stop=True)
                last.then_inc(pq_product, 1)

            sums(0)
            skewed(0, W0, tail_t(0))
            sums(1)
            skewed(1, W1, tail_t(1))
            sums(2)
            skewed(2, W2, tail_pq)

            pe.wait_ge(pq_ready, GROUPS)

            def spread_positions(i, b, q, t, par):
                pe.wait_ge(e_loaded[b], i * 32 + 32)
                if not (type(t) is int and t < 2):
                    pe.wait_ge(ot_made, t - 1)
                mm(bank(par), pick_dst[:], rows3[b][:, q * 512:(q + 1) * 512], start=True, stop=True
                   ).then_inc(e_positions, 1)

            def first_product(i, b, q, t, par):
                pe.wait_ge(ot_made, t + 1)
                pe.wait_ge(gathered[3][b], i * (16 * HALF) + 16 * HALF)
                pe.wait_ge(q_loaded[b], i * (16 * HALF) + 16 * HALF)
                if not (type(t) is int and t < 2):
                    pe.wait_ge(h1_ready, t - 1)
                for j in range(BATCH):
                    to = bank(2 + par)[:, j * P:(j + 1) * P]
                    mm(to, G[b][:, q * BATCH + j, :], ident[:], start=True, stop=False, is_transpose=True)
                    mm(to, EW1[:, 0, :], Gw[b][:, q * BATCH + j, :], start=False, stop=False)
                    last = mm(to, Win[b][:, q * BATCH + j, :], OT[par][:, j, :], start=False, stop=True)
                last.then_inc(h1_product, 1)

            def second_product(t, par):
                pe.wait_ge(h1_ready, t + 1)
                if not (type(t) is int and t < 1):
                    pe.wait_ge(h2_ready, t)
                for j in range(BATCH):
                    to = bank(4)[:, j * P:(j + 1) * P]
                    last = mm(to, H1[par][:, j, :], EW2[:], start=True, stop=True)
                last.then_inc(h2_product, 1)

            def window_sums(i, b, q, t, par):
                pe.wait_ge(h2_ready, t + 1)
                pe.wait_ge(o_made, i * 2 + (b + 1))
                if not (type(t) is int and t < 2):
                    pe.wait_ge(e_added, t - 1)
                for j in range(BATCH):
                    last = mm(bank(5 + par)[:, j * P:(j + 1) * P], H2[par][:, j, :], O[b][:, q * BATCH + j, :],
                              start=True, stop=True)
                last.then_inc(e_summed, 1)

            def edge_iteration(i, start, end):
                for s in range(4):
                    t = i * 4 + s
                    if s < 3:
                        spread_positions(i, (s + 1) // 2, (s + 1) % 2, t + 1, (s + 1) % 2)
                    elif not end:
                        spread_positions(i + 1, 0, 0, t + 1, 0)
                    first_product(i, s // 2, s % 2, t, s % 2)
                    if not (start and s == 0):
                        second_product(t - 1, (s + 1) % 2)
                    if s >= 2:
                        window_sums(i, (s - 2) // 2, s % 2, t - 2, s % 2)
                    elif not start:
                        window_sums(i - 1, 1, s % 2, t - 2, s % 2)

            spread_positions(0, 0, 0, 0, 0)
            edge_iteration(0, True, False)
            with pe.Fori(1, ITERATIONS - 1) as i:
                edge_iteration(i, False, False)
            edge_iteration(ITERATIONS - 1, False, True)
            second_product(STEPS - 1, 1)
            window_sums(ITERATIONS - 1, 1, 0, STEPS - 2, 0)
            window_sums(ITERATIONS - 1, 1, 1, STEPS - 1, 1)

            def tail_mlp(g):
                pe.wait_ge(v_ready, g + 1)
                turn(3, V, None, g).then_inc(turned[3], 1)
                pe.wait_ge(acc_set[3], g + 1)
                for h in range(4):
                    for z in range(2):
                        if h == 0:
                            pe.wait_ge(hid_ready, g * 8)
                        else:
                            pe.wait_ge(hid_ready, g * 8 + (2 * h + z - 1))
                        mm(bank(4 + z)[:, 0:SPAN // 2], EWd1[:, h * P:(h + 1) * P],
                           XT[:, z * (SPAN // 2):(z + 1) * (SPAN // 2)], start=True, stop=True
                           ).then_inc(hid_product, 1)
                pe.wait_ge(hid_ready, g * 8 + 8)
                pe.wait_ge(ffn_read, g)
                for j in range(GROUP):
                    to = bank(6, 2)[:, j * P:(j + 1) * P]
                    mm(to, XT[:, j * P:(j + 1) * P], ident[:], start=True, stop=False, is_transpose=True)
                    mm(to, ones[0:1, :], vec[0:1, 4, :], start=False, stop=False)
                    for h in range(4):
                        last = mm(to, HD[:, h, j * P:(j + 1) * P], EWd2[:, h, :], start=False, stop=(h == 3))
                last.then_inc(ffn_product, 1)

            skewed(3, EW3, tail_mlp)

            def last_bc(i, b, q, t):
                pe.wait_ge(l_rows[b], i * 16 + 16)
                if not (type(t) is int and t < 2):
                    pe.wait_ge(l_eq, t - 1)
                mm(bank(6 * q), pick_dst[:], rows3[b][:, q * 512:(q + 1) * 512], start=True, stop=True)
                mm(bank(6 * q + 1), pick_src[:], rows3[b][:, q * 512:(q + 1) * 512], start=True, stop=True
                   ).then_inc(l_bc, 1)

            def last_rows(i, b, q, t, par):
                pe.wait_ge(l_ot, t + 1)
                pe.wait_ge(l_win[b], i * (16 * HALF) + 16 * HALF)
                if not (type(t) is int and t < 2):
                    pe.wait_ge(m_ready, t - 1)
                for j in range(BATCH):
                    last = mm(bank(2 + par)[:, j * P:(j + 1) * P], OT[par][:, j, :], Win[b][:, q * BATCH + j, :],
                              start=True, stop=True)
                last.then_inc(m_product, 1)

            def last_merge(t, par):
                pe.wait_ge(m_ready, t + 1)
                pe.wait_ge(l_eq, t + 1)
                if not (type(t) is int and t < 1):
                    pe.wait_ge(r_ready, t)
                for j in range(BATCH):
                    last = mm(bank(4, 2)[:, j * 256:j * 256 + ROW], ET[par][:, j, :], Mw[par][:, j, :],
                              start=True, stop=True)
                last.then_inc(r_product, 1)

            def last_iteration(i, start, end):
                for s in range(4):
                    t = i * 4 + s
                    if s < 3:
                        last_bc(i, (s + 1) // 2, (s + 1) % 2, t + 1)
                    elif not end:
                        last_bc(i + 1, 0, 0, t + 1)
                    last_rows(i, s // 2, s % 2, t, s % 2)
                    if not (start and s == 0):
                        last_merge(t - 1, (s + 1) % 2)

            last_bc(0, 0, 0, 0)
            last_iteration(0, True, False)
            with pe.Fori(1, ITERATIONS - 1) as i:
                last_iteration(i, False, False)
            last_iteration(ITERATIONS - 1, False, True)
            last_merge(STEPS - 1, 1)

            def turn_last(g):
                pe.wait_ge(tx_ready, g + 1)
                pe.wait_ge(acc_set[4], g)
                for j in range(GROUP):
                    nc.tensor.transpose(bank(2, 2)[:, j * P:(j + 1) * P], T[:, j, :], ident[:])
                    last = nc.tensor.transpose(bank(4, 2)[:, j * P:(j + 1) * P], TX[:, j, :], ident[:])
                last.then_inc(turned[4], 1)

            with pe.Fori(0, GROUPS) as g:
                turn_last(g)
                pe.wait_ge(acc_set[4], g + 1)
                pe.wait_ge(product_read[4], g)
                for j in range(GROUP):
                    mm(bank(0, 2)[:, j * P:(j + 1) * P], XT[:, j * P:(j + 1) * P], WL[:, 0, :], start=True, stop=False)
                    last = mm(bank(0, 2)[:, j * P:(j + 1) * P], HT[:, j * P:(j + 1) * P], WL[:, 1, :],
                              start=False, stop=True)
                last.then_inc(product[4], 1)


def kernel(**inputs):
    import numpy as np
    import concourse.bacc as bacc
    from concourse.bass_utils import run_bass_kernel_spmd

    a = {k: np.asarray(v) for k, v in inputs.items()}
    pad_e = EDGES - N_EDGES
    phantom = (N_NODES + np.arange(pad_e) * (NODES - N_NODES) // pad_e).astype(np.int32)
    dst = np.concatenate([a["dst"].astype(np.int32), phantom]).reshape(CHUNKS, P)
    src = np.concatenate([a["src"].astype(np.int32), phantom]).reshape(CHUNKS, P)
    weight = np.concatenate([a["edge_weight"], np.zeros(pad_e, np.float32)]).reshape(CHUNKS, P)
    arrays = {
        "x": np.concatenate([a["x"], np.zeros((NODES - N_NODES, P), np.float32)]),
        "edge_attr_t": np.concatenate([a["edge_attr_128"].T, np.zeros((P, pad_e), np.float32)], axis=1),
        "first_dst": np.ascontiguousarray(dst[:, 0:1].T),
        "dst_t": np.ascontiguousarray(dst.T), "src_t": np.ascontiguousarray(src.T),
        "weight_t": np.ascontiguousarray(weight.T),
        "w0_t": np.ascontiguousarray(a["L0_gnn_W"].T),
        "w1": a["L1_gnn_W1"], "w2": a["L1_gnn_W2"],
        "e_w1": a["L2_gnn_W1"], "e_w2": a["L2_gnn_W2"], "e_w3": a["L2_gnn_W3"],
        "e_wd1": a["L2_gnn_Wd1"], "e_wd2": a["L2_gnn_Wd2"], "w_last": a["L3_gnn_W"],
        "row_vectors": np.stack([a["L0_gnn_b"], a["L1_gnn_b1"], a["L1_gnn_b2"], a["L2_gnn_b3"], a["L2_gnn_bd2"],
                                 a["L2_gnn_g1"], a["L2_gnn_beta1"], a["L2_gnn_g2"], a["L2_gnn_beta2"],
                                 a["L2_gnn_b2"]]),
        "e_b1": a["L2_gnn_b1"].reshape(P, 1),
        "e_b2": a["L2_gnn_b2"].reshape(P, 1),
        "e_bd1": np.ascontiguousarray(a["L2_gnn_bd1"].reshape(4, P).T),
    }
    nc = bacc.Bacc("TRN2", target_bir_lowering=False, num_devices=1)
    feeds, args = {}, []
    for name, value in arrays.items():
        feeds[f"in_{name}"] = np.ascontiguousarray(value)
        args.append(nc.dram_tensor(f"in_{name}", value.shape, mybir.dt.from_np(value.dtype),
                                   kind="ExternalInput").ap())
    args.append(nc.dram_tensor("out_x", (NODES, P), mybir.dt.float32, kind="ExternalOutput").ap())
    gnn_program(nc, *args)
    r = run_bass_kernel_spmd(nc, [feeds], core_ids=[0])
    return r.results[0]["out_x"][:N_NODES]
```
